# Optimizing a Trainium2 kernel written in Bass

```python
import numpy as np
import jax
import jax.numpy as jnp

def _softmax(x, axis=-1):
    return jax.nn.softmax(x, axis=axis)

def _gelu(x):
    return jax.nn.gelu(x, approximate=True)

def _silu(x):
    return jax.nn.silu(x)

def _sigmoid(x):
    return jax.nn.sigmoid(x)

def _layernorm(x, axis=-1, eps=1e-05):
    m = jnp.mean(x, axis=axis, keepdims=True)
    v = jnp.var(x, axis=axis, keepdims=True)
    return (x - m) / jnp.sqrt(v + eps)

def _scatter_add(tgt, idx, src, axis=0):
    return tgt.at[idx].add(src)

def _segment_sum(src, seg, n):
    return jax.ops.segment_sum(src, seg, n)
kernel_name = 'mk_decoder_postln_d2_seqx_r8_7603f0'

def setup_inputs(seed: int=0):
    np.random.seed(seed)
    _w = jnp.asarray

    def _rec_inputs():
        import jax
        import jax.numpy as jnp
        _rk = jax.random.key(seed)
        x = 0.0002417 + 0.9998 * jax.random.normal(jax.random.fold_in(_rk, 1), (64, 64, 128), jnp.float32)
        _lenS = 64 - jax.random.randint(jax.random.fold_in(_rk, 7), (64,), 0, max(1, 64 // 4) + 1, jnp.int32)
        _lenS2 = 64 - jax.random.randint(jax.random.fold_in(_rk, 8), (64,), 0, max(1, 64 // 4) + 1, jnp.int32)
        _ctx_1024P = jax.random.normal(jax.random.fold_in(_rk, 11), (64, 16, 128), jnp.float32)
        _ctx_1024c = jax.random.dirichlet(jax.random.fold_in(_rk, 511), 0.3 * jnp.ones((16,), jnp.float32), (64, 64))
        _ctx_1024t = jnp.einsum('bsk,bkd->bsd', _ctx_1024c, _ctx_1024P)
        _ctx_1024t = _ctx_1024t * jax.lax.rsqrt(jnp.mean(jnp.square(_ctx_1024t)) + 1e-12) * 0.953939
        ctx_1024 = 7.22013e-05 + 1.00017 * (_ctx_1024t + 0.3 * jax.random.normal(jax.random.fold_in(_rk, 611), (64, 64, 128), jnp.float32))
        _validS = jnp.arange(64)[None, :] < _lenS[:, None]
        _validS2 = jnp.arange(64)[None, :] < _lenS2[:, None]
        _causal = jnp.tril(jnp.ones((64, 64), dtype=bool))
        mask_1x1xSxS2_ik0 = jnp.where(jnp.broadcast_to(_validS2[0:1, None, None, :], (1, 1, 64, 64)), 0, 1).astype(jnp.int32)
        return (x, ctx_1024, mask_1x1xSxS2_ik0)
    x, ctx_1024, mask_1x1xSxS2_ik0 = _rec_inputs()

    def _L0_attn_setup():
        import jax, jax.numpy as jnp
        import numpy as np
        B, L, H, I, K, G = (2, 512, 128, 256, 4, 8)
        EPS = 1e-05

        def _layernorm(x, g, b):
            m = x.mean(-1, keepdims=True)
            v = jnp.var(x, axis=-1, keepdims=True)
            return (x - m) * jax.lax.rsqrt(v + EPS) * g + b
        key = jax.random.key(seed)
        ks = jax.random.split(key, 8)
        s = 0.02
        return {'hidden_states': jax.random.normal(ks[0], (B, L, H), jnp.float32), 'in_proj_w': jax.random.normal(ks[1], (2 * I, H), jnp.float32) * s, 'conv_w': jax.random.normal(ks[2], (I, I // G, K), jnp.float32) * s, 'conv_b': jax.random.normal(ks[3], (I,), jnp.float32) * s, 'ln_g': jnp.ones((I,), jnp.float32), 'ln_b': jnp.zeros((I,), jnp.float32), 'fc_w': jax.random.normal(ks[4], (H, I), jnp.float32) * s, 'fc_b': jnp.zeros((H,), jnp.float32), 'cproj_w': jax.random.normal(ks[5], (I, H), jnp.float32) * s, 'cproj_b': jnp.zeros((I,), jnp.float32), 'out_w': jax.random.normal(ks[6], (H, I), jnp.float32) * s}
    _L0_attn_all = _L0_attn_setup()
    _L0_attn_in = {k: v for k, v in _L0_attn_all.items() if k in ('in_proj_w', 'conv_w', 'conv_b', 'ln_g', 'ln_b', 'fc_w', 'fc_b', 'cproj_w', 'cproj_b', 'out_w')}
    del _L0_attn_all

    def _L0_xattn_setup():
        import jax, jax.numpy as jnp
        import numpy as np
        D_MODEL = 128
        NUM_HEADS = 16
        DEPTH = D_MODEL // NUM_HEADS

        def _split_heads(x, B):
            S = x.shape[1]
            return x.reshape(B, S, NUM_HEADS, DEPTH).transpose(0, 2, 1, 3)
        key = jax.random.key(seed)
        ks = jax.random.split(key, 11)
        B, S = (4, 256)
        scale = 1.0 / np.sqrt(D_MODEL)
        inp = {'v': jax.random.normal(ks[0], (B, S, D_MODEL), jnp.float32), 'k': jax.random.normal(ks[1], (B, S, D_MODEL), jnp.float32), 'q': jax.random.normal(ks[2], (B, S, D_MODEL), jnp.float32), 'wq': jax.random.normal(ks[3], (D_MODEL, D_MODEL), jnp.float32) * scale, 'bq': jnp.zeros((D_MODEL,), jnp.float32), 'wk': jax.random.normal(ks[4], (D_MODEL, D_MODEL), jnp.float32) * scale, 'bk': jnp.zeros((D_MODEL,), jnp.float32), 'wv': jax.random.normal(ks[5], (D_MODEL, D_MODEL), jnp.float32) * scale, 'bv': jnp.zeros((D_MODEL,), jnp.float32), 'wo': jax.random.normal(ks[6], (D_MODEL, D_MODEL), jnp.float32) * scale, 'bo': jnp.zeros((D_MODEL,), jnp.float32)}
        return inp
    _L0_xattn_all = _L0_xattn_setup()
    _L0_xattn_in = {k: v for k, v in _L0_xattn_all.items() if k in ('wq', 'bq', 'wk', 'bk', 'wv', 'bv', 'wo', 'bo')}
    del _L0_xattn_all

    def _L0_ffn_setup():
        import jax, jax.numpy as jnp
        import numpy as np
        B, T, C, H, E = (4, 256, 128, 256, 8)
        CAPACITY_FACTOR = 1.0
        key = jax.random.key(seed)
        ks = jax.random.split(key, 5)
        scale = 0.02
        return {'x': jax.random.normal(ks[0], (B, T, C), dtype=jnp.float32), 'Wg': jax.random.normal(ks[1], (E, C), dtype=jnp.float32) * scale, 'W1': jax.random.normal(ks[2], (E, H, C), dtype=jnp.float32) * scale, 'W2': jax.random.normal(ks[3], (E, C, H), dtype=jnp.float32) * scale, 'W3': jax.random.normal(ks[4], (E, H, C), dtype=jnp.float32) * scale}
    _L0_ffn_all = _L0_ffn_setup()
    _L0_ffn_in = {k: v for k, v in _L0_ffn_all.items() if k in ('Wg', 'W1', 'W2', 'W3')}
    del _L0_ffn_all

    def _L1_attn_setup():
        import jax, jax.numpy as jnp
        import numpy as np
        B, T, D = (1, 128, 128)
        H = 16
        HKV = 16
        HD = D // H
        R = 2
        K = 3
        LOWR = 32
        HR = HKV * R
        OUTW = HKV * HD * 2 * R
        SCALE = HD ** (-0.5)

        def path_attention_forward(hidden_states, q_w, k_w, v_w, w1, w2, conv_w, bt_w, bt_b, o_w, omega, phi):
            b, t, _ = hidden_states.shape
            q = hidden_states @ q_w.T
            k = hidden_states @ k_w.T
            v = hidden_states @ v_w.T
            w_raw = hidden_states @ w1.T @ w2.T
            xp = jnp.pad(w_raw, ((0, 0), (K - 1, 0), (0, 0)))
            w_raw = sum((xp[:, i:i + t, :] * conv_w[:, i] for i in range(K)))
            w_raw = jax.nn.silu(w_raw)
            w5 = w_raw.reshape(b, t, HKV, 2 * R, HD)
            Ah = w5[:, :, :, 0::2, :]
            Bh = w5[:, :, :, 1::2, :]
            pos = jnp.arange(t, dtype=jnp.float32)[None, :, None, None]
            theta = omega * pos + phi
            c = jnp.cos(theta)[..., None]
            s = jnp.sin(theta)[..., None]
            Wdir = Ah * c + Bh * s
            Wdir = Wdir * jax.lax.rsqrt(jnp.sum(Wdir * Wdir, -1, keepdims=True) + 1e-06)
            beta = jax.nn.sigmoid(hidden_states @ bt_w.T + bt_b) * 2.0
            to_h = lambda x: jnp.swapaxes(jnp.repeat(x.reshape(b, t, H, HD), R, axis=2), 1, 2)
            qh, kh, vh = (to_h(q), to_h(k), to_h(v))
            wh = jnp.swapaxes(Wdir.reshape(b, t, HR, HD), 1, 2)
            bh = jnp.swapaxes(beta, 1, 2)
            idx = jnp.arange(t)
            strict = idx[:, None] > idx[None, :]
            incl = idx[:, None] >= idx[None, :]
            Mw = jnp.where(strict, jnp.einsum('bhtd,bhsd->bhts', wh, wh) * bh[..., None], 0.0)
            rhs = jnp.where(strict, jnp.einsum('bhtd,bhjd->bhtj', wh, kh) * bh[..., None], 0.0)
            Bmat = jax.scipy.linalg.solve_triangular(Mw + jnp.eye(t, dtype=Mw.dtype), rhs, lower=True)
            qk = jnp.einsum('bhid,bhjd->bhij', qh, kh)
            qw = jnp.where(incl, jnp.einsum('bhid,bhtd->bhit', qh, wh), 0.0)
            logits = (qk - jnp.einsum('bhit,bhtj->bhij', qw, Bmat)) * SCALE
            logits = jnp.where(incl, logits, -1e+30)
            p = jax.nn.softmax(logits, axis=-1)
            o = jnp.einsum('bhij,bhjd->bhid', p, vh)
            o = jnp.swapaxes(o, 1, 2).reshape(b, t, HR * HD)
            return o @ o_w.T
        key = jax.random.key(seed)
        ks = jax.random.split(key, 10)

        def rn(k, shape, sc=1.0):
            return jax.random.normal(k, shape, dtype=jnp.float32) * sc
        return {'hidden_states': rn(ks[0], (B, T, D)), 'q_w': rn(ks[1], (D, D), D ** (-0.5)), 'k_w': rn(ks[2], (D, D), D ** (-0.5)), 'v_w': rn(ks[3], (D, D), D ** (-0.5)), 'w1': rn(ks[4], (LOWR, D), D ** (-0.5)), 'w2': rn(ks[5], (OUTW, LOWR), LOWR ** (-0.5)), 'conv_w': rn(ks[6], (OUTW, K), K ** (-0.5)), 'bt_w': rn(ks[7], (HKV * R, D), D ** (-0.5)), 'bt_b': jnp.zeros((HKV * R,), jnp.float32), 'o_w': rn(ks[8], (D, D * R), (D * R) ** (-0.5)), 'omega': 0.01 * jnp.ones((1, 1, 1, R), jnp.float32), 'phi': jnp.zeros((1, 1, 1, R), jnp.float32)}
    _L1_attn_all = _L1_attn_setup()
    _L1_attn_in = {k: v for k, v in _L1_attn_all.items() if k in ('q_w', 'k_w', 'v_w', 'w1', 'w2', 'conv_w', 'bt_w', 'bt_b', 'o_w', 'omega', 'phi')}
    del _L1_attn_all

    def _L1_xattn_setup():
        import jax, jax.numpy as jnp
        import numpy as np
        D_MODEL = 128
        NUM_HEADS = 16
        D_K = D_MODEL // NUM_HEADS
        B, S = (2, 256)

        def _split_heads(x):
            b, s, _ = x.shape
            return x.reshape(b, s, NUM_HEADS, D_K).transpose(0, 2, 1, 3)
        key = jax.random.key(seed)
        ks = jax.random.split(key, 11)
        scale = 1.0 / np.sqrt(D_MODEL)
        inp = {'Q': jax.random.normal(ks[0], (B, S, D_MODEL), jnp.float32), 'K': jax.random.normal(ks[1], (B, S, D_MODEL), jnp.float32), 'V': jax.random.normal(ks[2], (B, S, D_MODEL), jnp.float32), 'mask': jnp.tril(jnp.ones((S, S), jnp.int32))[None, None, :, :], 'Wq': jax.random.normal(ks[3], (D_MODEL, D_MODEL), jnp.float32) * scale, 'bq': jax.random.normal(ks[4], (D_MODEL,), jnp.float32) * scale, 'Wk': jax.random.normal(ks[5], (D_MODEL, D_MODEL), jnp.float32) * scale, 'bk': jax.random.normal(ks[6], (D_MODEL,), jnp.float32) * scale, 'Wv': jax.random.normal(ks[7], (D_MODEL, D_MODEL), jnp.float32) * scale, 'bv': jax.random.normal(ks[8], (D_MODEL,), jnp.float32) * scale, 'Wo': jax.random.normal(ks[9], (D_MODEL, D_MODEL), jnp.float32) * scale, 'bo': jax.random.normal(ks[10], (D_MODEL,), jnp.float32) * scale}
        return inp
    _L1_xattn_all = _L1_xattn_setup()
    _L1_xattn_in = {k: v for k, v in _L1_xattn_all.items() if k in ('Wq', 'bq', 'Wk', 'bk', 'Wv', 'bv', 'Wo', 'bo')}
    del _L1_xattn_all

    def _L1_ffn_setup():
        import jax, jax.numpy as jnp
        import numpy as np
        B, T, D, H = (4, 256, 128, 256)
        E, S, K = (8, 2, 2)

        def _swiglu_stacked(x, w1, b1, w2, b2, w3, b3):
            p1 = jnp.einsum('btd,ndh->nbth', x, w1) + b1[:, None, None, :]
            p2 = jnp.einsum('btd,ndh->nbth', x, w2) + b2[:, None, None, :]
            glu = jax.nn.silu(p1) * p2
            return jnp.einsum('nbth,nhd->nbtd', glu, w3) + b3[:, None, None, :]
        key = jax.random.key(seed)
        ks = jax.random.split(key, 10)
        s = 0.02
        return {'x': jax.random.normal(ks[0], (B, T, D), jnp.float32), 'gate_w': jax.random.normal(ks[1], (D, E), jnp.float32) * s, 'gate_b': jnp.zeros((E,), jnp.float32), 'rw1': jax.random.normal(ks[2], (E, D, H), jnp.float32) * s, 'rb1': jnp.zeros((E, H), jnp.float32), 'rw2': jax.random.normal(ks[3], (E, D, H), jnp.float32) * s, 'rb2': jnp.zeros((E, H), jnp.float32), 'rw3': jax.random.normal(ks[4], (E, H, D), jnp.float32) * s, 'rb3': jnp.zeros((E, D), jnp.float32), 'sw1': jax.random.normal(ks[5], (S, D, H), jnp.float32) * s, 'sb1': jnp.zeros((S, H), jnp.float32), 'sw2': jax.random.normal(ks[6], (S, D, H), jnp.float32) * s, 'sb2': jnp.zeros((S, H), jnp.float32), 'sw3': jax.random.normal(ks[7], (S, H, D), jnp.float32) * s, 'sb3': jnp.zeros((S, D), jnp.float32)}
    _L1_ffn_all = _L1_ffn_setup()
    _L1_ffn_in = {k: v for k, v in _L1_ffn_all.items() if k in ('gate_w', 'gate_b', 'rw1', 'rb1', 'rw2', 'rb2', 'rw3', 'rb3', 'sw1', 'sb1', 'sw2', 'sb2', 'sw3', 'sb3')}
    del _L1_ffn_all
    return {'x': x, 'ctx_1024': ctx_1024, 'mask_1x1xSxS2_ik0': mask_1x1xSxS2_ik0, 'L0_attn_in_proj_w': _L0_attn_in['in_proj_w'], 'L0_attn_conv_w': _L0_attn_in['conv_w'], 'L0_attn_conv_b': _L0_attn_in['conv_b'], 'L0_attn_ln_g': _L0_attn_in['ln_g'], 'L0_attn_ln_b': _L0_attn_in['ln_b'], 'L0_attn_fc_w': _L0_attn_in['fc_w'], 'L0_attn_fc_b': _L0_attn_in['fc_b'], 'L0_attn_cproj_w': _L0_attn_in['cproj_w'], 'L0_attn_cproj_b': _L0_attn_in['cproj_b'], 'L0_attn_out_w': _L0_attn_in['out_w'], 'L0_xattn_wq': _L0_xattn_in['wq'], 'L0_xattn_bq': _L0_xattn_in['bq'], 'L0_xattn_wk': _L0_xattn_in['wk'], 'L0_xattn_bk': _L0_xattn_in['bk'], 'L0_xattn_wv': _L0_xattn_in['wv'], 'L0_xattn_bv': _L0_xattn_in['bv'], 'L0_xattn_wo': _L0_xattn_in['wo'], 'L0_xattn_bo': _L0_xattn_in['bo'], 'L0_ffn_Wg': _L0_ffn_in['Wg'], 'L0_ffn_W1': _L0_ffn_in['W1'], 'L0_ffn_W2': _L0_ffn_in['W2'], 'L0_ffn_W3': _L0_ffn_in['W3'], 'L1_attn_q_w': _L1_attn_in['q_w'], 'L1_attn_k_w': _L1_attn_in['k_w'], 'L1_attn_v_w': _L1_attn_in['v_w'], 'L1_attn_w1': _L1_attn_in['w1'], 'L1_attn_w2': _L1_attn_in['w2'], 'L1_attn_conv_w': _L1_attn_in['conv_w'], 'L1_attn_bt_w': _L1_attn_in['bt_w'], 'L1_attn_bt_b': _L1_attn_in['bt_b'], 'L1_attn_o_w': _L1_attn_in['o_w'], 'L1_attn_omega': _L1_attn_in['omega'], 'L1_attn_phi': _L1_attn_in['phi'], 'L1_xattn_Wq': _L1_xattn_in['Wq'], 'L1_xattn_bq': _L1_xattn_in['bq'], 'L1_xattn_Wk': _L1_xattn_in['Wk'], 'L1_xattn_bk': _L1_xattn_in['bk'], 'L1_xattn_Wv': _L1_xattn_in['Wv'], 'L1_xattn_bv': _L1_xattn_in['bv'], 'L1_xattn_Wo': _L1_xattn_in['Wo'], 'L1_xattn_bo': _L1_xattn_in['bo'], 'L1_ffn_gate_w': _L1_ffn_in['gate_w'], 'L1_ffn_gate_b': _L1_ffn_in['gate_b'], 'L1_ffn_rw1': _L1_ffn_in['rw1'], 'L1_ffn_rb1': _L1_ffn_in['rb1'], 'L1_ffn_rw2': _L1_ffn_in['rw2'], 'L1_ffn_rb2': _L1_ffn_in['rb2'], 'L1_ffn_rw3': _L1_ffn_in['rw3'], 'L1_ffn_rb3': _L1_ffn_in['rb3'], 'L1_ffn_sw1': _L1_ffn_in['sw1'], 'L1_ffn_sb1': _L1_ffn_in['sb1'], 'L1_ffn_sw2': _L1_ffn_in['sw2'], 'L1_ffn_sb2': _L1_ffn_in['sb2'], 'L1_ffn_sw3': _L1_ffn_in['sw3'], 'L1_ffn_sb3': _L1_ffn_in['sb3']}

def reference(x, ctx_1024, mask_1x1xSxS2_ik0, L0_attn_in_proj_w, L0_attn_conv_w, L0_attn_conv_b, L0_attn_ln_g, L0_attn_ln_b, L0_attn_fc_w, L0_attn_fc_b, L0_attn_cproj_w, L0_attn_cproj_b, L0_attn_out_w, L0_xattn_wq, L0_xattn_bq, L0_xattn_wk, L0_xattn_bk, L0_xattn_wv, L0_xattn_bv, L0_xattn_wo, L0_xattn_bo, L0_ffn_Wg, L0_ffn_W1, L0_ffn_W2, L0_ffn_W3, L1_attn_q_w, L1_attn_k_w, L1_attn_v_w, L1_attn_w1, L1_attn_w2, L1_attn_conv_w, L1_attn_bt_w, L1_attn_bt_b, L1_attn_o_w, L1_attn_omega, L1_attn_phi, L1_xattn_Wq, L1_xattn_bq, L1_xattn_Wk, L1_xattn_bk, L1_xattn_Wv, L1_xattn_bv, L1_xattn_Wo, L1_xattn_bo, L1_ffn_gate_w, L1_ffn_gate_b, L1_ffn_rw1, L1_ffn_rb1, L1_ffn_rw2, L1_ffn_rb2, L1_ffn_rw3, L1_ffn_rb3, L1_ffn_sw1, L1_ffn_sb1, L1_ffn_sw2, L1_ffn_sb2, L1_ffn_sw3, L1_ffn_sb3):
    import jax
    import jax.numpy as jnp

    def _L0_attn_ref(hidden_states, in_proj_w, conv_w, conv_b, ln_g, ln_b, fc_w, fc_b, cproj_w, cproj_b, out_w):
        import jax, jax.numpy as jnp
        import numpy as np
        B, L, H, I, K, G = (2, 512, 128, 256, 4, 8)
        EPS = 1e-05

        def _layernorm(x, g, b):
            m = x.mean(-1, keepdims=True)
            v = jnp.var(x, axis=-1, keepdims=True)
            return (x - m) * jax.lax.rsqrt(v + EPS) * g + b
        p = hidden_states @ in_proj_w.T
        h, gate = (p[..., :I], p[..., I:])
        gate = jax.nn.silu(gate)
        hc = jnp.transpose(h, (0, 2, 1))
        conv = jax.lax.conv_general_dilated(hc, conv_w, window_strides=(1,), padding=[(K - 1, 0)], feature_group_count=G, dimension_numbers=('NCH', 'OIH', 'NCH'))
        conv = conv + conv_b[None, :, None]
        h = jnp.transpose(conv, (0, 2, 1)) * gate
        residual = h
        hn = _layernorm(h, ln_g, ln_b)
        m = jax.nn.silu(hn @ fc_w.T + fc_b) @ cproj_w.T + cproj_b
        h = m + residual
        return h @ out_w.T

    def _L0_xattn_ref(v, k, q, wq, bq, wk, bk, wv, bv, wo, bo):
        import jax, jax.numpy as jnp
        import numpy as np
        D_MODEL = 128
        NUM_HEADS = 16
        DEPTH = D_MODEL // NUM_HEADS

        def _split_heads(x, B):
            S = x.shape[1]
            return x.reshape(B, S, NUM_HEADS, DEPTH).transpose(0, 2, 1, 3)
        B, S, _ = q.shape
        qh = _split_heads(q @ wq + bq, B)
        kh = _split_heads(k @ wk + bk, B)
        vh = _split_heads(v @ wv + bv, B)
        logits = jnp.einsum('bhqd,bhkd->bhqk', qh, kh) / jnp.sqrt(jnp.float32(DEPTH))
        weights = jax.nn.softmax(logits, axis=-1)
        attn = jnp.einsum('bhqk,bhkd->bhqd', weights, vh)
        concat = attn.transpose(0, 2, 1, 3).reshape(B, S, D_MODEL)
        return concat @ wo + bo

    def _L0_ffn_ref(x, Wg, W1, W2, W3):
        import jax, jax.numpy as jnp
        import numpy as np
        B, T, C, H, E = (4, 256, 128, 256, 8)
        CAPACITY_FACTOR = 1.0
        b, t, c = x.shape
        e = Wg.shape[0]
        n = b * t
        capacity = max(1, int(CAPACITY_FACTOR * n / e))
        x_flat = x.reshape(n, c)
        scores = (x_flat @ Wg.T).T
        top_vals, token_idx = jax.lax.top_k(scores, capacity)
        token_w = jax.nn.softmax(top_vals, axis=-1)
        xg = x_flat[token_idx]
        h = jax.nn.silu(jnp.einsum('eic,ehc->eih', xg, W1)) * jnp.einsum('eic,ehc->eih', xg, W3)
        y = jnp.einsum('eih,ech->eic', h, W2) * token_w[..., None]
        out = jnp.zeros_like(x_flat).at[token_idx.reshape(-1)].add(y.reshape(-1, c))
        return out.reshape(b, t, c)

    def _L1_attn_ref(hidden_states, q_w, k_w, v_w, w1, w2, conv_w, bt_w, bt_b, o_w, omega, phi):
        import jax, jax.numpy as jnp
        import numpy as np
        B, T, D = (1, 128, 128)
        H = 16
        HKV = 16
        HD = D // H
        R = 2
        K = 3
        LOWR = 32
        HR = HKV * R
        OUTW = HKV * HD * 2 * R
        SCALE = HD ** (-0.5)

        def path_attention_forward(hidden_states, q_w, k_w, v_w, w1, w2, conv_w, bt_w, bt_b, o_w, omega, phi):
            b, t, _ = hidden_states.shape
            q = hidden_states @ q_w.T
            k = hidden_states @ k_w.T
            v = hidden_states @ v_w.T
            w_raw = hidden_states @ w1.T @ w2.T
            xp = jnp.pad(w_raw, ((0, 0), (K - 1, 0), (0, 0)))
            w_raw = sum((xp[:, i:i + t, :] * conv_w[:, i] for i in range(K)))
            w_raw = jax.nn.silu(w_raw)
            w5 = w_raw.reshape(b, t, HKV, 2 * R, HD)
            Ah = w5[:, :, :, 0::2, :]
            Bh = w5[:, :, :, 1::2, :]
            pos = jnp.arange(t, dtype=jnp.float32)[None, :, None, None]
            theta = omega * pos + phi
            c = jnp.cos(theta)[..., None]
            s = jnp.sin(theta)[..., None]
            Wdir = Ah * c + Bh * s
            Wdir = Wdir * jax.lax.rsqrt(jnp.sum(Wdir * Wdir, -1, keepdims=True) + 1e-06)
            beta = jax.nn.sigmoid(hidden_states @ bt_w.T + bt_b) * 2.0
            to_h = lambda x: jnp.swapaxes(jnp.repeat(x.reshape(b, t, H, HD), R, axis=2), 1, 2)
            qh, kh, vh = (to_h(q), to_h(k), to_h(v))
            wh = jnp.swapaxes(Wdir.reshape(b, t, HR, HD), 1, 2)
            bh = jnp.swapaxes(beta, 1, 2)
            idx = jnp.arange(t)
            strict = idx[:, None] > idx[None, :]
            incl = idx[:, None] >= idx[None, :]
            Mw = jnp.where(strict, jnp.einsum('bhtd,bhsd->bhts', wh, wh) * bh[..., None], 0.0)
            rhs = jnp.where(strict, jnp.einsum('bhtd,bhjd->bhtj', wh, kh) * bh[..., None], 0.0)
            Bmat = jax.scipy.linalg.solve_triangular(Mw + jnp.eye(t, dtype=Mw.dtype), rhs, lower=True)
            qk = jnp.einsum('bhid,bhjd->bhij', qh, kh)
            qw = jnp.where(incl, jnp.einsum('bhid,bhtd->bhit', qh, wh), 0.0)
            logits = (qk - jnp.einsum('bhit,bhtj->bhij', qw, Bmat)) * SCALE
            logits = jnp.where(incl, logits, -1e+30)
            p = jax.nn.softmax(logits, axis=-1)
            o = jnp.einsum('bhij,bhjd->bhid', p, vh)
            o = jnp.swapaxes(o, 1, 2).reshape(b, t, HR * HD)
            return o @ o_w.T
        return path_attention_forward(hidden_states, q_w, k_w, v_w, w1, w2, conv_w, bt_w, bt_b, o_w, omega, phi)

    def _L1_xattn_ref(Q, K, V, mask, Wq, bq, Wk, bk, Wv, bv, Wo, bo):
        import jax, jax.numpy as jnp
        import numpy as np
        D_MODEL = 128
        NUM_HEADS = 16
        D_K = D_MODEL // NUM_HEADS
        B, S = (2, 256)

        def _split_heads(x):
            b, s, _ = x.shape
            return x.reshape(b, s, NUM_HEADS, D_K).transpose(0, 2, 1, 3)
        q = _split_heads(Q @ Wq.T + bq)
        k = _split_heads(K @ Wk.T + bk)
        v = _split_heads(V @ Wv.T + bv)
        scores = jnp.einsum('bhqd,bhkd->bhqk', q, k) / jnp.sqrt(jnp.float32(D_K))
        scores = jnp.where(mask == 0, jnp.float32(-1000000000.0), scores)
        probs = jax.nn.softmax(scores, axis=-1)
        attn = jnp.einsum('bhqk,bhkd->bhqd', probs, v)
        attn = attn.transpose(0, 2, 1, 3).reshape(Q.shape[0], Q.shape[1], D_MODEL)
        return attn @ Wo.T + bo

    def _L1_ffn_ref(x, gate_w, gate_b, rw1, rb1, rw2, rb2, rw3, rb3, sw1, sb1, sw2, sb2, sw3, sb3):
        import jax, jax.numpy as jnp
        import numpy as np
        B, T, D, H = (4, 256, 128, 256)
        E, S, K = (8, 2, 2)

        def _swiglu_stacked(x, w1, b1, w2, b2, w3, b3):
            p1 = jnp.einsum('btd,ndh->nbth', x, w1) + b1[:, None, None, :]
            p2 = jnp.einsum('btd,ndh->nbth', x, w2) + b2[:, None, None, :]
            glu = jax.nn.silu(p1) * p2
            return jnp.einsum('nbth,nhd->nbtd', glu, w3) + b3[:, None, None, :]
        scores = jax.nn.softmax(x @ gate_w + gate_b, axis=-1)
        weights, indices = jax.lax.top_k(scores, K)
        routed_all = _swiglu_stacked(x, rw1, rb1, rw2, rb2, rw3, rb3)
        out_bted = jnp.transpose(routed_all, (1, 2, 0, 3))
        gathered = jnp.take_along_axis(out_bted, indices[..., None], axis=2)
        routed = jnp.sum(weights[..., None] * gathered, axis=2)
        shared = _swiglu_stacked(x, sw1, sb1, sw2, sb2, sw3, sb3).mean(axis=0)
        return shared + routed
    x = _layernorm(x + _L0_attn_ref(x, L0_attn_in_proj_w, L0_attn_conv_w, L0_attn_conv_b, L0_attn_ln_g, L0_attn_ln_b, L0_attn_fc_w, L0_attn_fc_b, L0_attn_cproj_w, L0_attn_cproj_b, L0_attn_out_w), axis=-1)
    x = _layernorm(x + _L0_xattn_ref(ctx_1024, ctx_1024, x, L0_xattn_wq, L0_xattn_bq, L0_xattn_wk, L0_xattn_bk, L0_xattn_wv, L0_xattn_bv, L0_xattn_wo, L0_xattn_bo), axis=-1)
    x = _layernorm(x + _L0_ffn_ref(x, L0_ffn_Wg, L0_ffn_W1, L0_ffn_W2, L0_ffn_W3), axis=-1)
    x = _layernorm(x + _L1_attn_ref(x, L1_attn_q_w, L1_attn_k_w, L1_attn_v_w, L1_attn_w1, L1_attn_w2, L1_attn_conv_w, L1_attn_bt_w, L1_attn_bt_b, L1_attn_o_w, L1_attn_omega, L1_attn_phi), axis=-1)
    x = _layernorm(x + _L1_xattn_ref(x, ctx_1024, ctx_1024, mask_1x1xSxS2_ik0, L1_xattn_Wq, L1_xattn_bq, L1_xattn_Wk, L1_xattn_bk, L1_xattn_Wv, L1_xattn_bv, L1_xattn_Wo, L1_xattn_bo), axis=-1)
    x = _layernorm(x + _L1_ffn_ref(x, L1_ffn_gate_w, L1_ffn_gate_b, L1_ffn_rw1, L1_ffn_rb1, L1_ffn_rw2, L1_ffn_rb2, L1_ffn_rw3, L1_ffn_rb3, L1_ffn_sw1, L1_ffn_sb1, L1_ffn_sw2, L1_ffn_sb2, L1_ffn_sw3, L1_ffn_sb3), axis=-1)
    return x

_drawn_inputs = setup_inputs


def setup_inputs(seed=0):
    import zlib

    import numpy as np

    out = dict(_drawn_inputs(seed))
    spreads = {'L0_attn_ln_g': (1.0, 0.6),
     'L0_attn_ln_b': (0.0, 0.8),
     'L0_attn_fc_b': (0.0, 0.8),
     'L0_attn_cproj_b': (0.0, 0.276),
     'L0_xattn_bq': (0.0, 0.31),
     'L0_xattn_bk': (0.0, 2.0),
     'L0_xattn_bv': (0.0, 0.1),
     'L0_xattn_bo': (0.0, 0.1),
     'L1_attn_bt_b': (0.0, 0.8),
     'L1_attn_omega': (0.009999999776482582, 0.6),
     'L1_attn_phi': (0.0, 0.1),
     'L1_ffn_gate_b': (0.0, 0.657),
     'L1_ffn_rb1': (0.0, 0.8),
     'L1_ffn_rb2': (0.0, 0.8),
     'L1_ffn_rb3': (0.0, 1.169),
     'L1_ffn_sb1': (0.0, 0.8),
     'L1_ffn_sb2': (0.0, 0.8),
     'L1_ffn_sb3': (0.0, 0.608)}
    factors = {'L0_attn_in_proj_w': 6.384,
     'L0_attn_conv_w': 6.75,
     'L0_attn_conv_b': 8.0,
     'L0_attn_fc_w': 6.412,
     'L0_attn_cproj_w': 5.749,
     'L0_ffn_Wg': 8.0,
     'L0_ffn_W1': 8.0,
     'L0_ffn_W2': 8.0,
     'L0_ffn_W3': 8.0,
     'L1_xattn_bk': 64.0,
     'L1_ffn_gate_w': 2.917,
     'L1_ffn_rw1': 8.0,
     'L1_ffn_rw2': 8.0,
     'L1_ffn_rw3': 8.0,
     'L1_ffn_sw1': 8.0,
     'L1_ffn_sw2': 8.0,
     'L1_ffn_sw3': 8.0}
    for name, (base, spread) in spreads.items():
        noise = np.random.default_rng([zlib.crc32(name.encode()), seed]).standard_normal(out[name].shape)
        drawn = base * np.exp(spread * noise) if base else spread * noise
        out[name] = jnp.asarray(drawn.astype(out[name].dtype))
    for name, factor in factors.items():
        out[name] = (out[name] * factor).astype(out[name].dtype)
    return out
```

```python
from contextlib import ExitStack

import concourse.bass as bass
from concourse import mybir

ALU = mybir.AluOpType
ACT = mybir.ActivationFunctionType
F32 = mybir.dt.float32
I32 = mybir.dt.int32
BF16 = mybir.dt.bfloat16
AX_X = mybir.AxisListType.X

P = 128
B = 64
S = 64
D = 128
N = B * S
W = 512
CHUNKS = N // W
BC = W // S
INNER = 256
TAPS = 4
H = 16
DH = D // H
EPS = 1e-5
LN_EXP_SET = 6


def stage_semaphore(nc, g, name):
    g["sems"].append(nc.alloc_semaphore(name))
    return g["sems"][-1]


def end_stage(nc, g):
    nc.clear_and_free_semaphores(g["sems"])
    g["sems"].clear()
    nc.all_engine_barrier()


def load_ln_exp(nc, act):
    act.add_instruction(mybir.InstLoadActFuncSet(
        name=nc.get_next_instruction_name(), engine=mybir.EngineType.Activation,
        act_func_set_id=LN_EXP_SET, ins=[], outs=[]))


class Norm:

    def __init__(self, nc, sb, sem, X, ones, eps, mean_ps, var_ps, y_ready, y_ps, per=1, buffers=None):
        self.nc, self.X, self.ones, self.eps = nc, X, ones, eps
        self.mean_ps, self.var_ps, self.y_ps, self.y_ready = mean_ps, var_ps, y_ps, y_ready
        self.per = per
        self.resid, self.rstd = buffers or (sb("resid", [P, W])[:], sb("rstd", [P, W])[:])
        self.centred = self.resid
        self.squares = self.rstd
        self.resid_ready = sem("resid_ready")
        self.mean_ready = sem("mean_ready")
        self.centred_ready = sem("centred_ready")
        self.squares_ready = sem("squares_ready")
        self.var_ready = sem("var_ready")
        self.logvar_ready = sem("logvar_ready")
        self.rstd_ready = sem("rstd_ready")
        self.x_ready = sem("x_ready")

    def chunk(self, i):
        return self.X[:, bass.ds(i * W, W)]

    def like(self, buf, x):
        return buf if len(x.shape) == 2 else buf.rearrange("p (a b) -> p a b", b=x.shape[2])

    def add(self, dve, i, bias=None, x=None, y=None):
        x = self.chunk(i) if x is None else x
        y = self.y_ps if y is None else y
        dve.wait_ge(self.y_ready, i * self.per + self.per)
        if bias is None:
            dve.tensor_tensor(self.like(self.resid, x), y, x, ALU.add).then_inc(self.resid_ready, 1)
        else:
            dve.scalar_tensor_tensor(self.like(self.resid, x), y, bias, x, ALU.add, ALU.add).then_inc(self.resid_ready, 1)

    def centre(self, dve, i):
        dve.wait_ge(self.mean_ready, i + 1)
        dve.tensor_tensor(self.centred, self.resid, self.mean_ps, ALU.subtract).then_inc(self.centred_ready, 1)

    def scale(self, dve, i, x=None):
        x = self.chunk(i) if x is None else x
        dve.wait_ge(self.rstd_ready, i + 1)
        dve.tensor_tensor(x, self.like(self.centred, x), self.like(self.rstd, x), ALU.mult).then_inc(self.x_ready, 1)

    def vector(self, dve, i, bias=None, x=None, y=None):
        self.add(dve, i, bias, x, y)
        self.centre(dve, i)
        self.scale(dve, i, x)

    def mean(self, pe, i):
        pe.wait_ge(self.resid_ready, i + 1)
        pe.matmul(self.mean_ps, self.ones[:], self.resid, start=True, stop=True).then_inc(self.mean_ready, 1)

    def variance(self, pe, i):
        pe.wait_ge(self.squares_ready, i + 1)
        pe.matmul(self.var_ps, self.ones[:], self.squares, start=True, stop=True).then_inc(self.var_ready, 1)

    def tensor(self, pe, i):
        self.mean(pe, i)
        self.variance(pe, i)

    def square(self, act, i):
        act.wait_ge(self.centred_ready, i + 1)
        act.activation(self.squares, self.centred, ACT.Square).then_inc(self.squares_ready, 1)

    def root(self, act, i):
        act.wait_ge(self.var_ready, i + 1)
        act.activation(self.rstd, self.var_ps, ACT.Ln, bias=self.eps[:, 0:1]).then_inc(self.logvar_ready, 1)
        act.wait_ge(self.logvar_ready, i + 1)
        act.activation(self.rstd, self.rstd, ACT.Exp, scale=-0.5).then_inc(self.rstd_ready, 1)

    def scalar(self, act, i, load=True):
        self.square(act, i)
        if load:
            load_ln_exp(self.nc, act)
        self.root(act, i)


def conv_mlp_stage(nc, g, tag, w):
    X, ones, eps = g["X"], g["ones"], g["eps"]
    with ExitStack() as ctx:
        def sb(name, shape):
            return ctx.enter_context(nc.sbuf_tensor(tag + name, shape, F32))

        def ps(name, shape=(P, W)):
            return ctx.enter_context(nc.psum_tensor(tag + name, list(shape), F32))

        def sem(name):
            return stage_semaphore(nc, g, tag + name)

        w_in = sb("w_in", [P, 2 * INNER])
        w_conv = sb("w_conv", [P, 2, TAPS, P])
        cols = sb("cols", [P, 9])
        w_fc = sb("w_fc", [P, 2, D])
        w_cproj = sb("w_cproj", [P, INNER])
        w_out = sb("w_out", [P, 2, D])
        ones_inner = sb("ones_inner", [P, P])
        hpad = sb("hpad", [P, 2, BC, S + TAPS - 1])
        gate = sb("gate", [P, 2, W])
        h = sb("h", [P, 2, W])
        c = sb("c", [P, 2, W])
        sq = sb("sq", [P, 2, W])
        rs = sb("rs", [P, W])
        hn = sb("hn", [P, 2, W])
        s_fc = sb("s_fc", [P, W])
        h2 = sb("h2", [P, 2, W])
        h_ps = ps("h_ps", (P, 2, W))
        g_ps = ps("g_ps", (P, 2, W))
        fc_ps = ps("fc_ps")
        out_ps = ps("out_ps")
        mean_ps = ps("mean_ps")
        var_ps = ps("var_ps")

        weights = sem("weights")
        consts = sem("consts")
        proj_h = sem("proj_h")
        proj_g = sem("proj_g")
        h_copied = sem("h_copied")
        gated = sem("gated")
        conv = sem("conv")
        h_ready = sem("h_ready")
        hmean = sem("hmean")
        c_ready = sem("c_ready")
        sq_ready = sem("sq_ready")
        hvar = sem("hvar")
        log_ready = sem("log_ready")
        rs_ready = sem("rs_ready")
        cn_ready = sem("cn_ready")
        hn_ready = sem("hn_ready")
        fc_ready = sem("fc_ready")
        fc_silu = sem("fc_silu")
        cproj = sem("cproj")
        h2_ready = sem("h2_ready")
        y_ready = sem("y_ready")
        norm = Norm(nc, sb, sem, X, ones, eps, mean_ps[:], var_ps[:], y_ready, out_ps[:])
        LOADS = 6
        block = ctx.enter_context(nc.Block())

        @block.sync
        def _(sp):
            for dst, name in ((w_in, "in"), (w_conv, "conv"), (cols, "cols"), (w_fc, "fc"),
                              (w_cproj, "cproj"), (w_out, "out")):
                sp.dma_start(dst[:], w[name]).then_inc(weights, 16)

        @block.gpsimd
        def _(pool):
            pool.memset(ones_inner[:], 1.0 / INNER).then_inc(consts, 1)
            pool.memset(hpad[:], 0.0).then_inc(consts, 1)

        @block.tensor
        def _(pe):
            pe.wait_ge(weights, 16 * LOADS)
            pe.wait_ge(consts, 2)
            with pe.Fori(0, CHUNKS) as i:
                tok = bass.ds(i * W, W)
                pe.wait_ge(h2_ready, i * 2)
                for m in range(2):
                    pe.matmul(h_ps[:, m], w_in[:, m * P:(m + 1) * P], X[:, tok], start=True, stop=True).then_inc(proj_h, 1)
                pe.wait_ge(gated, i * 2)
                for m in range(2):
                    pe.matmul(g_ps[:, m], w_in[:, INNER + m * P:INNER + (m + 1) * P], X[:, tok],
                              start=True, stop=True).then_inc(proj_g, 1)
                for m in range(2):
                    pe.wait_ge(h_copied, i * 2 + 1 + m)
                    for k in range(TAPS):
                        mm = pe.matmul(h_ps[:, m], w_conv[:, m, k], hpad[:, m, :, k:k + S],
                                       start=(k == 0), stop=(k == TAPS - 1))
                    mm.then_inc(conv, 1)
                pe.wait_ge(h_ready, i * 2 + 2)
                pe.matmul(mean_ps[:], ones_inner[:], h[:, 0], start=True, stop=False)
                pe.matmul(mean_ps[:], ones_inner[:], h[:, 1], start=False, stop=True).then_inc(hmean, 1)
                pe.wait_ge(sq_ready, i + 1)
                pe.matmul(var_ps[:], ones_inner[:], sq[:, 0], start=True, stop=False)
                pe.matmul(var_ps[:], ones_inner[:], sq[:, 1], start=False, stop=True).then_inc(hvar, 1)
                pe.wait_ge(hn_ready, i * 2 + 2)
                pe.matmul(fc_ps[:], w_fc[:, 0], hn[:, 0], start=True, stop=False)
                pe.matmul(fc_ps[:], w_fc[:, 1], hn[:, 1], start=False, stop=True).then_inc(fc_ready, 1)
                pe.wait_ge(fc_silu, i + 1)
                for m in range(2):
                    pe.matmul(h_ps[:, m], w_cproj[:, m * P:(m + 1) * P], s_fc[:], start=True, stop=True).then_inc(cproj, 1)
                pe.wait_ge(h2_ready, i * 2 + 2)
                pe.matmul(out_ps[:], w_out[:, 0], h2[:, 0], start=True, stop=False)
                pe.matmul(out_ps[:], w_out[:, 1], h2[:, 1], start=False, stop=True).then_inc(y_ready, 1)
                norm.tensor(pe, i)

        @block.scalar
        def _(act):
            act.wait_ge(weights, 16 * LOADS)
            act.wait_ge(consts, 2)
            with act.Fori(0, CHUNKS) as i:
                for m in range(2):
                    act.wait_ge(proj_h, i * 2 + 1 + m)
                    act.copy(hpad[:, m, :, TAPS - 1:], h_ps[:, m].rearrange("p (b s) -> p b s", s=S)).then_inc(h_copied, 1)
                for m in range(2):
                    act.wait_ge(proj_g, i * 2 + 1 + m)
                    act.activation(gate[:, m], g_ps[:, m], ACT.Silu).then_inc(gated, 1)
                act.wait_ge(c_ready, i + 1)
                act.activation(sq[:], c[:], ACT.Square).then_inc(sq_ready, 1)
                load_ln_exp(nc, act)
                act.wait_ge(hvar, i + 1)
                act.activation(rs[:], var_ps[:], ACT.Ln, bias=eps[:, 0:1]).then_inc(log_ready, 1)
                act.wait_ge(log_ready, i + 1)
                act.activation(rs[:], rs[:], ACT.Exp, scale=-0.5).then_inc(rs_ready, 1)
                act.wait_ge(cn_ready, i + 1)
                for m in range(2):
                    act.activation(hn[:, m], sq[:, m], ACT.Identity, scale=cols[:, 2 + m:3 + m],
                                   bias=cols[:, 4 + m:5 + m]).then_inc(hn_ready, 1)
                act.wait_ge(fc_ready, i + 1)
                act.activation(s_fc[:], fc_ps[:], ACT.Silu, bias=cols[:, 8:9]).then_inc(fc_silu, 1)
                norm.scalar(act, i)

        @block.vector
        def _(dve):
            dve.wait_ge(weights, 16 * LOADS)
            with dve.Fori(0, CHUNKS) as i:
                for m in range(2):
                    dve.wait_ge(gated, i * 2 + 1 + m)
                    dve.wait_ge(conv, i * 2 + 1 + m)
                    dve.scalar_tensor_tensor(h[:, m], h_ps[:, m], cols[:, m:m + 1], gate[:, m],
                                             ALU.add, ALU.mult).then_inc(h_ready, 1)
                dve.wait_ge(hmean, i + 1)
                dve.wait_ge(h_ready, i * 2 + 2)
                dve.tensor_tensor(c[:], h[:], mean_ps[:, None, :].to_broadcast([P, 2, W]), ALU.subtract).then_inc(c_ready, 1)
                dve.wait_ge(rs_ready, i + 1)
                dve.wait_ge(hvar, i + 1)
                dve.tensor_tensor(sq[:], c[:], rs[:, None, :].to_broadcast([P, 2, W]), ALU.mult).then_inc(cn_ready, 1)
                for m in range(2):
                    dve.wait_ge(cproj, i * 2 + 1 + m)
                    dve.scalar_tensor_tensor(h2[:, m], h_ps[:, m], cols[:, 6 + m:7 + m], h[:, m],
                                             ALU.add, ALU.add).then_inc(h2_ready, 1)
                norm.vector(dve, i)


def attention_stage(nc, g, tag, w, masked):
    X, ones, eps, ident = g["X"], g["ones"], g["eps"], g["ident"]
    with ExitStack() as ctx:
        def sb(name, shape, dt=F32):
            return ctx.enter_context(nc.sbuf_tensor(tag + name, shape, dt))

        def ps(name, shape=(P, W)):
            return ctx.enter_context(nc.psum_tensor(tag + name, list(shape), F32))

        def sem(name):
            return stage_semaphore(nc, g, tag + name)

        w_qkvo = sb("w_qkvo", [P, 4, D])
        bias = sb("bias", [P, 4])
        C = sb("C", [P, 2, W])
        K = sb("K", [P, 2, BC, S])
        Kbd = sb("Kbd", [P, 2, BC, H, S])
        Q = sb("Q", [P, W])
        Vbd = sb("Vbd", [P, 2, BC, H // 2, 2, DH])
        E = sb("E", [P, 2, H, S])
        PT = sb("PT", [P, H // 2, P])
        top = sb("top", [P, 2, H])
        total = sb("total", [P, 2, H])
        share = sb("share", [P, 2, H])
        O = sb("O", [P, 2, D])
        OT = sb("OT", [P, W])
        if masked:
            mask_i = sb("mask_i", [S, S], I32)
            drop = sb("drop", [S, 8, S], BF16)
            pick = sb("pick", [S, S], BF16)

        s_ps = ps("s_ps", (P, 2, W))
        t_ps = ps("t_ps", (P, 2, W))
        o_ps = ps("o_ps")
        ot_ps = ps("ot_ps")
        z0 = ps("z0")
        z1 = ps("z1")

        weights, zeroed = sem("weights"), sem("zeroed")
        c_loaded = [sem("c_loaded0"), sem("c_loaded1")]
        k_ready, q_ready, v_ready = sem("k_ready"), sem("q_ready"), sem("v_ready")
        k_copied, q_copied, v_copied = sem("k_copied"), sem("q_copied"), sem("v_copied")
        k_spread = [sem("k_spread0"), sem("k_spread1")]
        s_ready, top_ready, e_ready, exp_ready = sem("s_ready"), sem("top_ready"), sem("e_ready"), sem("exp_ready")
        mask_ready = sem("mask_ready")
        total_ready, share_ready = sem("total_ready"), sem("share_ready")
        pt_ready, pt_copied = sem("pt_ready"), sem("pt_copied")
        o_ready, o_scaled, ot_ready, ot_copied = sem("o_ready"), sem("o_scaled"), sem("ot_ready"), sem("ot_copied")
        y_ready = sem("y_ready")
        norm = Norm(nc, sb, sem, X, ones, eps, z1[:], z0[:], y_ready, z0[:])
        block = ctx.enter_context(nc.Block())
        LOADS = 3 if masked else 2
        PAIRS = BC // 2
        LAST = CHUNKS - 1

        def chunks(engine, body):
            body(0, 0, True, False)
            with engine.Fori(0, (CHUNKS - 2) // 2) as j:
                body(j * 2 + 1, 1, False, False)
                body(j * 2 + 2, 0, False, False)
            body(LAST, 1, False, True)

        @block.sync
        def _(sp):
            sp.dma_start(w_qkvo[:], w["qkvo"]).then_inc(weights, 16)
            sp.dma_start(bias[:], w["bias"]).then_inc(weights, 16)
            if masked:
                sp.dma_start(mask_i[:], w["mask"]).then_inc(weights, 16)
            for u in range(2):
                sp.dma_start(C[:, u], w["ctxT"][:, u * W:(u + 1) * W]).then_inc(c_loaded[u], 16)

            def spread(n, u):
                sp.wait_ge(k_copied, n + 1)
                for h in range(H):
                    sp.dma_start(Kbd[h * DH:(h + 1) * DH, u, :, h, :], K[h * DH:(h + 1) * DH, u]).then_inc(k_spread[u], 16)

            sp.wait_ge(zeroed, 3)
            spread(0, 0)
            sp.wait_ge(v_ready, 2)
            sp.dma_start(C[:, 0], w["ctxT"][:, 2 * W:3 * W]).then_inc(c_loaded[0], 16)
            with sp.Fori(0, (CHUNKS - 4) // 2) as j:
                for u in (1, 0):
                    n = j * 2 + 2 - u
                    spread(n, u)
                    sp.wait_ge(v_ready, n * 2 + 2)
                    sp.dma_start(C[:, u], w["ctxT"][:, bass.ds(n * W + 2 * W, W)]).then_inc(c_loaded[u], 16)
            spread(LAST - 2, 1)
            sp.wait_ge(v_ready, LAST * 2 - 2)
            sp.dma_start(C[:, 1], w["ctxT"][:, LAST * W:]).then_inc(c_loaded[1], 16)
            spread(LAST - 1, 0)
            spread(LAST, 1)

        @block.gpsimd
        def _(pool):
            pool.memset(Kbd[:, 1], 0.0).then_inc(zeroed, 1)
            pool.memset(Vbd[:], 0.0).then_inc(zeroed, 1)

        @block.tensor
        def _(pe):
            def project_k(n, u):
                pe.wait_ge(c_loaded[u], 16 * (n // 2) + 16 if isinstance(n, int) else loads(n, u))
                pe.matmul(z1[:], w_qkvo[:, 1], C[:, u], start=True, stop=True).then_inc(k_ready, 1)

            def loads(n, u):
                return n * 8 + (8 if u else 16)

            def project_q(n):
                pe.matmul(z0[:], w_qkvo[:, 0], X[:, bass.ds(n * W, W)], start=True, stop=True).then_inc(q_ready, 1)

            def project_v(n, u):
                for half, bank in ((0, z1), (1, z0)):
                    if half:
                        pe.wait_ge(q_copied, n + 1)
                    else:
                        pe.wait_ge(k_copied, n + 1)
                    for b in range(4):
                        at = (half * 4 + b) * S
                        for h2 in range(2):
                            mm = pe.matmul(bank[h2 * S:(h2 + 1) * S, b * P:(b + 1) * P], C[:, u, at:at + S],
                                           w_qkvo[:, 2], start=True, stop=True)
                    mm.then_inc(v_ready, 1)

            def scores(u, pr, n):
                if not isinstance(n, int) or n or pr:
                    pe.wait_ge(e_ready, n * PAIRS + pr)
                for half in range(2):
                    for b in range(2):
                        out = s_ps[b * S:(b + 1) * S, half]
                        mm = pe.matmul(out, Q[:, (2 * pr + b) * S:(2 * pr + b + 1) * S],
                                       Kbd[:, u, 2 * pr + b, half * 8:half * 8 + 8, :], start=True, stop=not masked)
                if masked:
                    for half in range(2):
                        for b in range(2):
                            mm = pe.matmul(s_ps[b * S:(b + 1) * S, half], pick[:], drop[:], start=False, stop=True)
                mm.then_inc(s_ready, 1)

            def transposes(pr, n):
                pe.wait_ge(exp_ready, n * PAIRS + pr + 1)
                for half in range(2):
                    if half == 0 and (not isinstance(n, int) or n or pr):
                        pe.wait_ge(pt_copied, (n * PAIRS + pr) * 2)
                    for c in range(4):
                        mm = pe.transpose(t_ps[:, half, c * P:(c + 1) * P],
                                          E[:, pr % 2, half * 8 + 2 * c:half * 8 + 2 * c + 2, :], ident[:])
                    mm.then_inc(pt_ready, 1)

            def weigh(pr, n, u):
                pe.wait_ge(pt_copied, (n * PAIRS + pr) * 2 + 2)
                if not isinstance(n, int) or n or pr:
                    pe.wait_ge(o_scaled, n * PAIRS + pr)
                for hp in range(H // 2):
                    for b in range(2):
                        mm = pe.matmul(o_ps[b * S:(b + 1) * S, hp * 16:hp * 16 + 16], PT[:, hp, b * S:(b + 1) * S],
                                       Vbd[:, u, 2 * pr + b, hp], start=True, stop=True)
                mm.then_inc(o_ready, 1)

            def turn(pr, n):
                pe.wait_ge(o_scaled, n * PAIRS + pr + 1)
                pe.transpose(ot_ps[:, pr * P:(pr + 1) * P], O[:, pr % 2], ident[:]).then_inc(ot_ready, 1)

            def project_o(n):
                pe.wait_ge(v_copied, n * 4 + 8 if not isinstance(n, int) or n < LAST else CHUNKS * 4)
                pe.wait_ge(ot_copied, n + 1)
                pe.matmul(z0[:], w_qkvo[:, 3], OT[:], start=True, stop=True).then_inc(y_ready, 1)

            def body(n, u, first, last):
                if not last:
                    if not first:
                        pe.wait_ge(v_copied, n * 4 + 4)
                    project_k(n + 1, 1 - u)
                pe.wait_ge(q_copied, n + 1)
                pe.wait_ge(k_spread[u], (16 * H) * (n // 2) + 16 * H if isinstance(n, int) else loads(n, u) * H)
                scores(u, 0, n)
                if not first:
                    project_o(n - 1)
                scores(u, 1, n)
                for pr in range(PAIRS):
                    transposes(pr, n)
                    if pr < PAIRS - 2:
                        scores(u, pr + 2, n)
                    if pr:
                        turn(pr - 1, n)
                    weigh(pr, n, u)
                    if not first and pr == 0:
                        if not last:
                            pe.wait_ge(k_copied, n + 2)
                        norm.mean(pe, n - 1)
                    if not first and pr == 1:
                        norm.variance(pe, n - 1)
                    if not last and pr == 2:
                        if not first:
                            pe.wait_ge(norm.logvar_ready, n)
                        project_q(n + 1)
                if not last:
                    project_v(n + 1, 1 - u)
                turn(PAIRS - 1, n)

            pe.wait_ge(weights, 16 * LOADS)
            pe.wait_ge(zeroed, 3)
            if masked:
                pe.wait_ge(mask_ready, 2)
            project_k(0, 0)
            project_q(0)
            project_v(0, 0)
            pe.wait_ge(v_copied, 4)
            chunks(pe, body)
            project_o(LAST)
            norm.mean(pe, LAST)
            norm.variance(pe, LAST)

        @block.scalar
        def _(act):
            def copy_k(n, u):
                act.wait_ge(k_ready, n + 1)
                act.activation(K[:, u], z1[:].rearrange("p (b s) -> p b s", s=S), ACT.Identity, bias=bias[:, 1:2]).then_inc(k_copied, 1)

            def copy_q(n):
                act.wait_ge(q_ready, n + 1)
                if not isinstance(n, int) or n:
                    act.wait_ge(s_ready, n * PAIRS)
                act.activation(Q[:], z0[:], ACT.Identity, bias=bias[:, 0:1]).then_inc(q_copied, 1)

            def exps(pr, n):
                act.wait_ge(e_ready, n * PAIRS + pr + 1)
                act.activation(E[:, pr % 2], E[:, pr % 2], ACT.Exp, scale=DH ** -0.5).then_inc(exp_ready, 1)

            def copy_v(n, u):
                for half, bank in ((0, z1), (1, z0)):
                    act.wait_ge(v_ready, n * 2 + half + 1)
                    for h2 in range(2):
                        rows = slice(h2 * S, (h2 + 1) * S)
                        v = bank[rows, :].rearrange("p (b c k d) -> p b c k d", b=4, k=2, d=DH)[:, :, :, h2, :]
                        act.copy(Vbd[rows, u, half * 4:half * 4 + 4, :, h2, :], v).then_inc(v_copied, 1)

            def body(n, u, first, last):
                if not last:
                    copy_k(n + 1, 1 - u)
                exps(0, n)
                exps(1, n)
                for pr in range(PAIRS):
                    pair = n * PAIRS + pr
                    if not first and pr == 1:
                        norm.square(act, n - 1)
                    for half in range(2):
                        act.wait_ge(pt_ready, pair * 2 + half + 1)
                        if half == 0 and not (first and pr == 0):
                            act.wait_ge(o_ready, pair)
                        act.copy(PT[:, half * 4:half * 4 + 4], t_ps[:, half].rearrange("p (c q) -> p c q", q=P)).then_inc(pt_copied, 1)
                    if not first and pr == 1:
                        norm.root(act, n - 1)
                    if pr < PAIRS - 2:
                        exps(pr + 2, n)
                    if not last and pr == 2:
                        copy_q(n + 1)
                if not last:
                    copy_v(n + 1, 1 - u)
                act.wait_ge(ot_ready, n * PAIRS + PAIRS)
                if not first:
                    act.wait_ge(y_ready, n)
                act.activation(OT[:], ot_ps[:], ACT.Identity, bias=bias[:, 2:3]).then_inc(ot_copied, 1)

            load_ln_exp(nc, act)
            act.wait_ge(weights, 16 * LOADS)
            act.wait_ge(zeroed, 3)
            copy_k(0, 0)
            copy_q(0)
            copy_v(0, 0)
            chunks(act, body)
            norm.square(act, LAST)
            norm.root(act, LAST)

        @block.vector
        def _(dve):
            dve.memset(Kbd[:, 0], 0.0).then_inc(zeroed, 1)
            dve.wait_ge(weights, 16 * LOADS)
            if masked:
                dve.tensor_scalar(drop[:], mask_i[:, None, :].to_broadcast([S, 8, S]), 0, -2.0 ** 60, ALU.is_equal,
                                  ALU.mult).then_inc(mask_ready, 1)
                dve.tensor_copy(pick[:], ident[0:S, 0:S]).then_inc(mask_ready, 1)

            def shift(pr, n):
                pair, e = n * PAIRS + pr, pr % 2
                s = s_ps[:].rearrange("p a (h s) -> p (a h) s", s=S)
                dve.wait_ge(s_ready, pair + 1)
                dve.tensor_reduce(top[:, e], s, AX_X, ALU.max).then_inc(top_ready, 1)
                dve.wait_ge(top_ready, pair + 1)
                dve.tensor_tensor(E[:, e], s, top[:, e, :, None].to_broadcast([P, H, S]), ALU.subtract).then_inc(e_ready, 1)

            def sums(pr, n):
                pair, e = n * PAIRS + pr, pr % 2
                dve.wait_ge(exp_ready, pair + 1)
                dve.tensor_reduce(total[:, e], E[:, e], AX_X, ALU.add).then_inc(total_ready, 1)
                dve.wait_ge(total_ready, pair + 1)
                dve.reciprocal(share[:, e], total[:, e]).then_inc(share_ready, 1)

            def scale(pr, n):
                pair, e = n * PAIRS + pr, pr % 2
                dve.wait_ge(o_ready, pair + 1)
                dve.wait_ge(share_ready, pair + 1)
                dve.tensor_tensor(O[:, e].rearrange("p (h d) -> p h d", d=DH),
                                  o_ps[:, 0:D].rearrange("p (h d) -> p h d", d=DH),
                                  share[:, e, :, None].to_broadcast([P, H, DH]), ALU.mult).then_inc(o_scaled, 1)

            def body(n, u, first, last):
                shift(0, n)
                if not first:
                    norm.add(dve, n - 1, bias[:, 3:4])
                shift(1, n)
                for pr in range(PAIRS):
                    sums(pr, n)
                    if pr < PAIRS - 2:
                        shift(pr + 2, n)
                    scale(pr, n)
                    if not first and pr == 0:
                        norm.centre(dve, n - 1)
                    if not first and pr == 1:
                        norm.scale(dve, n - 1)

            chunks(dve, body)
            norm.add(dve, LAST, bias[:, 3:4])
            norm.centre(dve, LAST)
            norm.scale(dve, LAST)


class Experts:

    def __init__(self, nc, sb, ps, sem, g, count, biased):
        self.nc, self.g, self.count, self.biased = nc, g, count, biased
        self.w_gate = sb("w_gate", [P, count, INNER])
        self.w_up = sb("w_up", [P, count, INNER])
        self.w_down = sb("w_down", [P, count, 2, D])
        self.share = sb("share", [P, W // P, count])
        self.a = sb("a", [P, 2, W])
        self.h = sb("h", [P, 2, 2, W])
        self.acc = sb("acc", [P, W // P, D])
        self.gate_ps = ps("gate_ps", (P, 2, W))
        self.up_ps = ps("up_ps", (P, 2, W))
        self.y_ps = ps("y_ps", (P, 2, W))
        self.gate_ready, self.up_ready = sem("gate_ready"), sem("up_ready")
        self.silu_ready, self.h_ready = sem("silu_ready"), sem("h_ready")
        self.down_ready, self.acc_ready = sem("down_ready"), sem("acc_ready")
        self.share_ready = sem("share_ready")
        if biased:
            self.b_gate = sb("b_gate", [P, count, 2])
            self.b_up = sb("b_up", [P, count, 2])

    def tensor(self, pe, n):
        X = self.g["X"]
        tok = bass.ds(n * W, W)

        def down(e):
            pe.wait_ge(self.h_ready, n * (2 * self.count) + 2 * e + 2)
            if e >= 1:
                pe.wait_ge(self.acc_ready, n * self.count + e - 1)
            for t in range(W // P):
                for m in range(2):
                    mm = pe.matmul(self.y_ps[:, e % 2, t * P:(t + 1) * P], self.h[:, e % 2, m, t * P:(t + 1) * P],
                                   self.w_down[:, e, m], start=(m == 0), stop=(m == 1))
            mm.then_inc(self.down_ready, 1)

        for e in range(self.count):
            pe.wait_ge(self.silu_ready, n * (2 * self.count) + 2 * e)
            for m in range(2):
                pe.matmul(self.gate_ps[:, m], self.w_gate[:, e, m * P:(m + 1) * P], X[:, tok],
                          start=True, stop=True).then_inc(self.gate_ready, 1)
            pe.wait_ge(self.h_ready, n * (2 * self.count) + 2 * e)
            for m in range(2):
                pe.matmul(self.up_ps[:, m], self.w_up[:, e, m * P:(m + 1) * P], X[:, tok],
                          start=True, stop=True).then_inc(self.up_ready, 1)
            if e:
                down(e - 1)
        down(self.count - 1)

    def scalar(self, act, n):
        for e in range(self.count):
            for m in range(2):
                k = n * (2 * self.count) + 2 * e + m
                act.wait_ge(self.gate_ready, k + 1)
                if e or m:
                    act.wait_ge(self.h_ready, k - 1)
                bias = {"bias": self.b_gate[:, e, m:m + 1]} if self.biased else {}
                act.activation(self.a[:, m], self.gate_ps[:, m], ACT.Silu, **bias).then_inc(self.silu_ready, 1)

    def vector(self, dve, n):
        def accumulate(e):
            dve.wait_ge(self.down_ready, n * self.count + e + 1)
            for t in range(W // P):
                y, acc, share = self.y_ps[:, e % 2, t * P:(t + 1) * P], self.acc[:, t], self.share[:, t, e:e + 1]
                if e == 0:
                    last = dve.tensor_scalar(acc, y, share, None, ALU.mult)
                else:
                    last = dve.scalar_tensor_tensor(acc, y, share, acc, ALU.mult, ALU.add)
            last.then_inc(self.acc_ready, 1)

        for e in range(self.count):
            for m in range(2):
                k = n * (2 * self.count) + 2 * e + m
                dve.wait_ge(self.silu_ready, k + 1)
                dve.wait_ge(self.up_ready, k + 1)
                if self.biased:
                    dve.scalar_tensor_tensor(self.h[:, e % 2, m], self.up_ps[:, m], self.b_up[:, e, m:m + 1],
                                             self.a[:, m], ALU.add, ALU.mult).then_inc(self.h_ready, 1)
                else:
                    dve.tensor_tensor(self.h[:, e % 2, m], self.up_ps[:, m], self.a[:, m], ALU.mult).then_inc(self.h_ready, 1)
            if e:
                if e > 1:
                    dve.wait_ge(self.acc_ready, n * self.count + e - 1)
                accumulate(e - 1)
        dve.wait_ge(self.acc_ready, n * self.count + self.count - 1)
        accumulate(self.count - 1)


def expert_choice_stage(nc, g, tag, w):
    X, ones, eps, ident = g["X"], g["ones"], g["eps"], g["ident"]
    NE, CAP = 8, N // 8
    SL = P // NE
    T = N // SL
    BITS = 31
    with ExitStack() as ctx:
        def sb(name, shape, dt=F32):
            return ctx.enter_context(nc.sbuf_tensor(tag + name, shape, dt))

        def ps(name, shape=(P, W)):
            return ctx.enter_context(nc.psum_tensor(tag + name, list(shape), F32))

        def sem(name):
            return stage_semaphore(nc, g, tag + name)

        ex = Experts(nc, sb, ps, sem, g, NE, False)
        yt_ps, misc_ps = ps("yt_ps"), ps("misc_ps")
        w_router = sb("w_router", [P, NE])
        same = sb("same", [P, P])
        before = sb("before", [P, P])
        spread = sb("spread", [NE, P])
        rows = sb("rows", [NE, N])
        top = sb("top", [NE, 1])
        negtop = sb("negtop", [P, 1])
        s = sb("s", [P, T])
        y = sb("y", [P, T])
        one = sb("one", [P, T])
        hits = sb("hits", [P, T])
        count = sb("count", [P, 1])
        pos = sb("pos", [P, 1])
        sign = sb("sign", [P, 1])
        want = sb("want", [P, 1])
        found = sb("found", [P, 1], I32)
        bit = sb("bit", [P, 1], I32)
        cand = sb("cand", [P, 1], I32)
        taken = sb("taken", [P, 1], I32)
        thr = sb("thr", [P, 1])
        above = sb("above", [P, T])
        equal = sb("equal", [P, T])
        rank = sb("rank", [P, T])
        room = sb("room", [P, 1])
        room2 = sb("room2", [P, 1])
        part = sb("part", [P, 1])
        inv = sb("inv", [P, 1])
        exps = sb("exps", [P, T])
        weight = sb("weight", [P, T])
        share_all = sb("share_all", [P, N // P, NE])

        early, weights, gathered, returned = sem("early"), sem("weights"), sem("gathered"), sem("returned")
        score_ready, score_copied = sem("score_ready"), sem("score_copied")
        v_step = sem("v_step")
        p_step = sem("p_step")
        exp_ready = sem("exp_ready")
        bit_counted, bit_summed = sem("bit_counted"), sem("bit_summed")
        cand_ready, taken_ready, taken_bit, found_ready, bit_moved = (
            sem("cand_ready"), sem("taken_ready"), sem("taken_bit"), sem("found_ready"), sem("bit_moved"))
        turned = sem("turned")
        share_all_ready = sem("share_all_ready")
        y_ready = sem("y_ready")
        norm = Norm(nc, sb, sem, X, ones, eps, misc_ps[:], yt_ps[:], y_ready, yt_ps[:])
        block = ctx.enter_context(nc.Block())

        @block.sync
        def _(sp):
            for dst, name in ((w_router, "router"), (same, "same"), (before, "before"), (spread, "spread")):
                sp.dma_start(dst[:], w[name]).then_inc(early, 16)
            for dst, name in ((ex.w_gate, "gate"), (ex.w_up, "up"), (ex.w_down, "down")):
                sp.dma_start(dst[:], w[name]).then_inc(weights, 16)
            sp.wait_ge(score_copied, CHUNKS)
            for e in range(NE):
                sp.dma_start(s[e * SL:(e + 1) * SL, :], rows[e:e + 1, :].rearrange("o (c t) -> o c t", t=T)).then_inc(gathered, 16)
            sp.wait_ge(v_step, 24)
            for e in range(NE):
                sp.dma_start(rows[e:e + 1, :].rearrange("o (c t) -> o c t", t=T), weight[e * SL:(e + 1) * SL, :]).then_inc(returned, 16)

        @block.tensor
        def _(pe):
            pe.wait_ge(early, 64)
            for n in range(CHUNKS):
                if n >= 2:
                    pe.wait_ge(score_copied, n - 1)
                bank = (yt_ps, misc_ps)[n % 2]
                pe.matmul(bank[0:NE, :], w_router[:], X[:, n * W:(n + 1) * W], start=True, stop=True).then_inc(score_ready, 1)
            pe.wait_ge(score_copied, CHUNKS)
            pe.wait_ge(v_step, 1)
            pe.matmul(misc_ps[:, 0:1], spread[:], top[:], start=True, stop=True).then_inc(p_step, 1)
            pe.wait_ge(v_step, 5)
            pe.matmul(misc_ps[:, 1:2], same[:], count[:], start=True, stop=True).then_inc(p_step, 1)
            with pe.Fori(0, BITS) as i:
                pe.wait_ge(bit_counted, i + 1)
                pe.matmul(yt_ps[:, 0:1], same[:], count[:], start=True, stop=True).then_inc(bit_summed, 1)
            pe.wait_ge(v_step, 14)
            pe.matmul(misc_ps[:, 2:3], same[:], count[:], start=True, stop=True).then_inc(p_step, 1)
            pe.wait_ge(v_step, 17)
            pe.matmul(misc_ps[:, 3:4], before[:], rank[:, T - 1:T], start=True, stop=True).then_inc(p_step, 1)
            pe.wait_ge(v_step, 22)
            pe.matmul(misc_ps[:, 4:5], same[:], part[:], start=True, stop=True).then_inc(p_step, 1)
            pe.wait_ge(returned, 16 * NE)
            for t in range(N // P):
                mm = pe.transpose(yt_ps[:, t * NE:(t + 1) * NE], rows[:, t * P:(t + 1) * P], ident[0:NE, 0:NE])
            mm.then_inc(turned, 1)
            pe.wait_ge(weights, 48)
            pe.wait_ge(share_all_ready, 1)
            with pe.Fori(0, CHUNKS) as n:
                ex.tensor(pe, n)
                pe.wait_ge(ex.acc_ready, n * NE + NE)
                for t in range(W // P):
                    mm = pe.transpose(yt_ps[:, t * P:(t + 1) * P], ex.acc[:, t], ident[:])
                mm.then_inc(y_ready, 1)
                norm.tensor(pe, n)

        @block.scalar
        def _(act):
            for n in range(CHUNKS):
                act.wait_ge(score_ready, n + 1)
                act.copy(rows[:, n * W:(n + 1) * W], (yt_ps, misc_ps)[n % 2][0:NE, :]).then_inc(score_copied, 1)
            act.wait_ge(v_step, 2)
            act.wait_ge(gathered, 16 * NE)
            act.activation(exps[:], s[:], ACT.Exp, bias=negtop[:, 0:1]).then_inc(exp_ready, 1)
            with act.Fori(0, CHUNKS) as n:
                ex.scalar(act, n)
                norm.scalar(act, n)

        @block.vector
        def _(dve):
            done = [0]

            def step(instruction):
                done[0] += 1
                instruction.then_inc(v_step, 1)
                dve.wait_ge(v_step, done[0])

            dve.wait_ge(score_copied, CHUNKS)
            step(dve.tensor_reduce(top[:], rows[:], AX_X, ALU.max))
            dve.wait_ge(p_step, 1)
            step(dve.tensor_scalar(negtop[:], misc_ps[:, 0:1], -1.0, None, ALU.mult))
            step(dve.memset(one[:], 1.0))
            step(dve.memset(found[:], 0))
            dve.wait_ge(gathered, 16 * NE)
            step(dve.scalar_tensor_tensor(hits[:], s[:], 0.0, one[:], ALU.is_ge, ALU.mult, accum_out=count[:]))
            dve.wait_ge(p_step, 2)
            step(dve.tensor_scalar(pos[:], misc_ps[:, 1:2], float(CAP), None, ALU.is_ge))
            step(dve.tensor_scalar(sign[:], pos[:], 2.0, -1.0, ALU.mult, ALU.add))
            step(dve.tensor_scalar(want[:], pos[:], float(2 * CAP - N - 1), float(N - CAP + 1), ALU.mult, ALU.add))
            step(dve.tensor_scalar(y[:], s[:], sign[:, 0:1], None, ALU.mult))
            step(dve.memset(bit[:], 1 << (BITS - 1)))
            with dve.Fori(0, BITS) as i:
                dve.tensor_tensor(cand[:], found[:], bit[:], ALU.bitwise_or).then_inc(cand_ready, 1)
                dve.wait_ge(cand_ready, i + 1)
                dve.scalar_tensor_tensor(hits[:], y[:], cand[:].bitcast(F32), one[:], ALU.is_ge, ALU.mult,
                                         accum_out=count[:]).then_inc(bit_counted, 1)
                dve.wait_ge(bit_summed, i + 1)
                dve.tensor_scalar(taken[:], yt_ps[:, 0:1], want[:, 0:1], -1.0, ALU.is_ge, ALU.mult).then_inc(taken_ready, 1)
                dve.wait_ge(taken_ready, i + 1)
                dve.tensor_tensor(taken[:], taken[:], bit[:], ALU.bitwise_and).then_inc(taken_bit, 1)
                dve.wait_ge(taken_bit, i + 1)
                dve.tensor_tensor(found[:], found[:], taken[:], ALU.bitwise_or).then_inc(found_ready, 1)
                dve.tensor_scalar(bit[:], bit[:], 1, None, ALU.logical_shift_right).then_inc(bit_moved, 1)
                dve.wait_ge(found_ready, i + 1)
                dve.wait_ge(bit_moved, i + 1)
            step(dve.tensor_scalar(thr[:], found[:].bitcast(F32), sign[:, 0:1], None, ALU.mult))
            step(dve.tensor_scalar(above[:], s[:], thr[:, 0:1], None, ALU.is_gt))
            step(dve.tensor_scalar(equal[:], s[:], thr[:, 0:1], None, ALU.is_equal))
            step(dve.tensor_reduce(count[:], above[:], AX_X, ALU.add))
            dve.wait_ge(p_step, 3)
            step(dve.tensor_scalar(room[:], misc_ps[:, 2:3], -1.0, float(CAP), ALU.mult, ALU.add))
            step(dve.memset(hits[:], 0.0))
            step(dve.tensor_tensor_scan(rank[:], equal[:], hits[:], 0.0, ALU.add, ALU.add))
            dve.wait_ge(p_step, 4)
            step(dve.tensor_tensor(room2[:], room[:], misc_ps[:, 3:4], ALU.subtract))
            step(dve.scalar_tensor_tensor(hits[:], rank[:], room2[:, 0:1], equal[:], ALU.is_le, ALU.mult))
            step(dve.tensor_tensor(above[:], above[:], hits[:], ALU.add))
            dve.wait_ge(exp_ready, 1)
            step(dve.tensor_tensor(exps[:], exps[:], above[:], ALU.mult))
            step(dve.tensor_reduce(part[:], exps[:], AX_X, ALU.add))
            dve.wait_ge(p_step, 5)
            step(dve.reciprocal(inv[:], misc_ps[:, 4:5]))
            step(dve.tensor_scalar(weight[:], exps[:], inv[:, 0:1], None, ALU.mult))
            dve.wait_ge(turned, 1)
            dve.tensor_copy(share_all[:], yt_ps[:, 0:N // P * NE].rearrange("p (t e) -> p t e", e=NE)).then_inc(share_all_ready, 1)
            dve.wait_ge(share_all_ready, 1)
            with dve.Fori(0, CHUNKS) as n:
                dve.tensor_scalar(ex.share[:], share_all[:, bass.ds(n * (W // P), W // P), :], 1.0, None,
                                  ALU.mult).then_inc(ex.share_ready, 1)
                dve.wait_ge(ex.share_ready, n + 1)
                ex.vector(dve, n)
                norm.vector(dve, n)


def top2_experts_stage(nc, g, tag, w):
    X, ones, eps, ident = g["X"], g["ones"], g["eps"], g["ident"]
    NR, NS = 8, 2
    NE = NR + NS
    TT = W // P
    with ExitStack() as ctx:
        def sb(name, shape, dt=F32):
            return ctx.enter_context(nc.sbuf_tensor(tag + name, shape, dt))

        def ps(name, shape=(P, W)):
            return ctx.enter_context(nc.psum_tensor(tag + name, list(shape), F32))

        def sem(name):
            return stage_semaphore(nc, g, tag + name)

        ex = Experts(nc, sb, ps, sem, g, NE, True)
        yt_ps, misc_ps = ps("yt_ps"), ps("misc_ps")
        w_router = sb("w_router", [P, NR])
        b_router = sb("b_router", [NR, 1])
        b_down = sb("b_down", [NE, D])
        lower = sb("lower", [P, NR, NR])
        gate_rows = sb("gate_rows", [P, W])
        gates = sb("gates", [P, TT, NR])
        top = sb("top", [P, TT])
        exps = sb("exps", [P, TT, NR])
        total = sb("total", [P, TT])
        inv = sb("inv", [P, TT])
        higher = sb("higher", [P, TT * NR, NR])
        ties = sb("ties", [P, TT * NR, NR])
        rank = sb("rank", [P, TT, NR])
        share_rows = sb("share_rows", [NE, W])

        weights = sem("weights")
        filled = sem("filled")
        logits_ready, logits_copied, logits_turned = sem("logits_ready"), sem("logits_copied"), sem("logits_turned")
        v_step = sem("v_step")
        exp_ready = sem("exp_ready")
        share_turned, share_copied = sem("share_turned"), sem("share_copied")
        y_ready, stored = sem("y_ready"), sem("stored")
        norm = Norm(nc, sb, sem, X, ones, eps, misc_ps[:], yt_ps[:], y_ready, yt_ps[:])
        LOADS = 9
        STEPS = 12
        block = ctx.enter_context(nc.Block())

        @block.sync
        def _(sp):
            for dst, name in ((w_router, "router"), (b_router, "b_router"), (lower, "lower"), (ex.w_gate, "gate"),
                              (ex.b_gate, "b_gate"), (ex.w_up, "up"), (ex.b_up, "b_up"), (ex.w_down, "down"), (b_down, "b_down")):
                sp.dma_start(dst[:], w[name]).then_inc(weights, 16)
            with sp.Fori(0, CHUNKS) as n:
                sp.wait_ge(norm.x_ready, n + 1)
                sp.dma_start(w["outT"][:, bass.ds(n * W, W)], X[:, bass.ds(n * W, W)]).then_inc(stored, 16)
            sp.wait_ge(stored, 16 * CHUNKS)

        @block.gpsimd
        def _(pool):
            pool.memset(ex.share[:], 1.0 / NS).then_inc(filled, 1)
            pool.memset(gate_rows[:], 0.0).then_inc(filled, 1)

        @block.tensor
        def _(pe):
            pe.wait_ge(weights, 16 * LOADS)
            with pe.Fori(0, CHUNKS) as n:
                tok = bass.ds(n * W, W)
                pe.wait_ge(norm.x_ready, n)
                pe.matmul(misc_ps[0:NR, :], w_router[:], X[:, tok], start=True, stop=True).then_inc(logits_ready, 1)
                pe.wait_ge(logits_copied, n + 1)
                for t in range(TT):
                    mm = pe.transpose(yt_ps[:, t * P:(t + 1) * P], gate_rows[:, t * P:(t + 1) * P], ident[:])
                mm.then_inc(logits_turned, 1)
                pe.wait_ge(v_step, n * STEPS + STEPS)
                for t in range(TT):
                    mm = pe.transpose(misc_ps[0:NE, t * P:(t + 1) * P], ex.share[:, t], ident[:])
                mm.then_inc(share_turned, 1)
                ex.tensor(pe, n)
                pe.wait_ge(share_copied, n + 1)
                pe.matmul(yt_ps[:], b_down[:], share_rows[:], start=True, stop=False)
                pe.wait_ge(ex.acc_ready, n * NE + NE)
                for t in range(TT):
                    mm = pe.matmul(yt_ps[:, t * P:(t + 1) * P], ex.acc[:, t], ident[:], start=False, stop=(t == TT - 1))
                mm.then_inc(y_ready, 1)
                norm.tensor(pe, n)

        @block.scalar
        def _(act):
            act.wait_ge(weights, 16 * LOADS)
            act.wait_ge(filled, 2)
            with act.Fori(0, CHUNKS) as n:
                act.wait_ge(logits_ready, n + 1)
                act.activation(gate_rows[0:NR, :], misc_ps[0:NR, :], ACT.Identity, bias=b_router[:, 0:1]).then_inc(logits_copied, 1)
                act.wait_ge(v_step, n * STEPS + 3)
                act.activation(exps[:], exps[:], ACT.Exp).then_inc(exp_ready, 1)
                act.wait_ge(share_turned, n + 1)
                act.copy(share_rows[:], misc_ps[0:NE, :]).then_inc(share_copied, 1)
                ex.scalar(act, n)
                norm.scalar(act, n)

        @block.vector
        def _(dve):
            dve.wait_ge(weights, 16 * LOADS)
            dve.wait_ge(filled, 2)
            with dve.Fori(0, CHUNKS) as n:
                done = [0]

                def step(instruction):
                    done[0] += 1
                    instruction.then_inc(v_step, 1)
                    dve.wait_ge(v_step, n * STEPS + done[0])

                dve.wait_ge(logits_turned, n + 1)
                step(dve.tensor_copy(gates[:], yt_ps[:].rearrange("p (t e) -> p t e", e=P)[:, :, 0:NR]))
                step(dve.tensor_reduce(top[:], gates[:], AX_X, ALU.max))
                step(dve.tensor_tensor(exps[:], gates[:], top[:, :, None].to_broadcast([P, TT, NR]), ALU.subtract))
                for t in range(TT):
                    mine = gates[:, t, :, None].to_broadcast([P, NR, NR])
                    other = gates[:, t, None, :].to_broadcast([P, NR, NR])
                    dve.tensor_tensor(higher[:, t * NR:(t + 1) * NR], other, mine, ALU.is_gt)
                    last = dve.tensor_tensor(ties[:, t * NR:(t + 1) * NR], other, mine, ALU.is_equal)
                step(last)
                four = lower[:, None, :, :].to_broadcast([P, TT, NR, NR])
                step(dve.tensor_tensor(ties[:].rearrange("p (t e) f -> p t e f", e=NR),
                                       ties[:].rearrange("p (t e) f -> p t e f", e=NR), four, ALU.mult))
                step(dve.tensor_tensor(higher[:], higher[:], ties[:], ALU.add))
                step(dve.tensor_reduce(rank[:].rearrange("p t e -> p (t e)"), higher[:], AX_X, ALU.add))
                step(dve.tensor_scalar(rank[:], rank[:], 1.5, None, ALU.is_lt))
                dve.wait_ge(exp_ready, n + 1)
                step(dve.tensor_reduce(total[:], exps[:], AX_X, ALU.add))
                step(dve.reciprocal(inv[:], total[:]))
                step(dve.tensor_tensor(exps[:], exps[:], inv[:, :, None].to_broadcast([P, TT, NR]), ALU.mult))
                step(dve.tensor_tensor(ex.share[:, :, 0:NR], exps[:], rank[:], ALU.mult))
                ex.vector(dve, n)
                norm.vector(dve, n)
def path_attention_stage(nc, g, tag, w):
    X, ones, eps, ident = g["X"], g["ones"], g["eps"], g["ident"]
    LOW, KT = 32, 3
    HG = H // 2
    GD = HG * DH
    STEP = 8
    QKVB = 3 * D + H
    ROW = 2 * D
    SCALE = DH ** -0.5
    PI = 3.141592653589793
    TWO_PI_HI = 6.28125
    TWO_PI_LO = 2 * PI - TWO_PI_HI
    with ExitStack() as ctx:
        def sb(name, shape, dt=F32):
            return ctx.enter_context(nc.sbuf_tensor(tag + name, shape, dt))

        def ps(name, shape=(P, W)):
            return ctx.enter_context(nc.psum_tensor(tag + name, list(shape), F32))

        def sem(name):
            return stage_semaphore(nc, g, tag + name)

        w_o = sb("w_o", [P, 2, D])
        angle = sb("angle", [P, 2])
        beta_bias = sb("beta_bias", [P, H])
        below = sb("below", [P, 2 * S])
        shut = sb("shut", [P, 2 * S])
        K = sb("K", [P, H, DH, S])
        QV = sb("QV", [P, S * ROW])
        Wd = sb("Wd", [P, S * D])
        A = sb("A", [P, 2, HG * DH * S])
        C = sb("C", [P, S * GD])
        trig = sb("trig", [P, 2, S])
        um = sb("um", [P, 2, HG * S])
        p = sb("p", [P, 2, HG * S])
        top = sb("top", [P, 2, HG])
        total = sb("total", [P, 2, HG])
        inv = sb("inv", [P, 2, HG])
        o_sum = sb("o_sum", [P, 2, GD])
        O = sb("O", [P, D])
        OT = sb("OT", [P, P])

        A_flat, used = A[:].rearrange("p a n -> p (a n)"), [0]

        def scratch(rows, *shape):
            n = 1
            for x in shape:
                n *= x
            view = A_flat[0:rows, used[0]:used[0] + n]
            used[0] += n
            return view if len(shape) == 1 else view.rearrange("p (a b) -> p a b", b=shape[1])

        w_tok = scratch(P, 2, QKVB)
        w_low = scratch(P, KT * LOW)
        w_up = scratch(KT * LOW, 2, 2 * D)
        taps = scratch(KT * LOW, 2, 2 * D)
        pos = scratch(P, S)
        turns = scratch(P, S).bitcast(I32)
        th, th2, excess = scratch(P, S), scratch(P, S), scratch(P, S)
        xs, ls = scratch(P, 2, B), scratch(KT * LOW, 2, B)
        raw = scratch(P, 2, 2 * D)
        beta = scratch(P, S, H)
        low = C[0:KT * LOW, :].rearrange("p (b s) -> p b s", s=S)
        sumsq, z = C[:, 0:S * H], C[:, S * H:2 * S * H]

        u_ps, l_ps, o_ps = ps("u_ps", (P, 2, W)), ps("l_ps", (P, 2, W)), ps("o_ps", (P, 2, W))
        ot_ps, y_ps = ps("ot_ps"), ps("y_ps")

        weights, consts = sem("weights"), sem("consts")
        v_step, s_step = sem("v_step"), sem("s_step")
        low_ready, low_copied = sem("low_ready"), sem("low_copied")
        staged, tok_ready, w_ready, silu_ready, half_ready, stored = (
            sem("staged"), sem("tok_ready"), sem("w_ready"), sem("silu_ready"), sem("half_ready"), sem("stored"))
        wk_ready, u_ready, um_ready, move_ready, k_ready, qk_ready, l_ready = (
            sem("wk_ready"), sem("u_ready"), sem("um_ready"), sem("move_ready"), sem("k_ready"), sem("qk_ready"), sem("l_ready"))
        shut_ready, top_ready, shifted, exp_ready, total_ready, inv_ready = (
            sem("shut_ready"), sem("top_ready"), sem("shifted"), sem("exp_ready"), sem("total_ready"), sem("inv_ready"))
        pv_ready, o_ready, o_summed, o_scaled, ot_ready, ot_copied, y_ready = (
            sem("pv_ready"), sem("o_ready"), sem("o_summed"), sem("o_scaled"), sem("ot_ready"), sem("ot_copied"), sem("y_ready"))
        norm = Norm(nc, sb, sem, X, ones, eps, ot_ps[:], ot_ps[:], y_ready, None, per=STEP,
                    buffers=(um[:, 1], um[:, 0]))
        block = ctx.enter_context(nc.Block())
        LOADS = 10
        Xbt = X[:].rearrange("p (b t) -> p b t", t=S)

        def heads(buf, gi, J):
            return buf[:, gi, 0:HG * DH * J].rearrange("p (h d j) -> p h d j", h=HG, d=DH)

        def keys(gi, J):
            return K[:, gi * HG:(gi + 1) * HG, :, 0:J]

        def row(buf, at, J):
            return buf[:, bass.ds(at, GD)].rearrange("p (h d) -> p h d", d=DH)[:, :, :, None].to_broadcast([P, HG, DH, J])

        @block.sync
        def _(sp):
            for dst, name in ((w_tok, "tok"), (w_low, "low"), (w_up, "up"), (taps, "taps"), (w_o, "o"), (angle, "angle"),
                              (beta_bias, "beta_bias"), (pos, "pos"), (below, "below"), (shut, "shut")):
                sp.dma_start(dst[:], w[name]).then_inc(weights, 16)

        @block.gpsimd
        def _(pool):
            pool.memset(low[0:2 * LOW, :, 0:2], 0.0).then_inc(consts, 1)

            def weigh(t, J):
                for gi in range(2):
                    k = t * 2 + gi
                    pool.wait_ge(exp_ready, k + 1)
                    pool.wait_ge(o_ready, k)
                    v = QV[:].rearrange("p (j c) -> p j c", c=ROW)[:, 0:J, D + gi * GD:D + (gi + 1) * GD]
                    pool.tensor_tensor(C[:, 0:J * GD].rearrange("p (j h d) -> p j h d", h=HG, d=DH),
                                       v.rearrange("p j (h d) -> p j h d", d=DH),
                                       p[:, gi, 0:HG * J].rearrange("p (h j) -> p j h", j=J)[:, :, :, None].to_broadcast([P, J, HG, DH]),
                                       ALU.mult).then_inc(pv_ready, 1)

            pool.wait_ge(v_step, 21)
            for c in range(S // STEP):
                with pool.Fori(0, STEP) as i:
                    weigh(i + c * STEP, (c + 1) * STEP)

        @block.tensor
        def _(pe):
            pe.wait_ge(weights, 16 * LOADS)
            with pe.Fori(0, CHUNKS // 2) as i:
                for u in range(2):
                    n = i * 2 + u
                    pe.wait_ge(low_copied, i * (2 * KT))
                    pe.matmul(o_ps[0:KT * LOW, u], w_low, X[:, bass.ds(n * W, W)], start=True, stop=True).then_inc(low_ready, 1)
            pe.wait_ge(v_step, 1)
            with pe.Fori(0, S // 2) as i:
                for u in range(2):
                    t = i * 2 + u
                    pe.wait_ge(staged, t * 2 + 2)
                    for r in range(2):
                        mm = pe.matmul(u_ps[r * B:(r + 1) * B, u, 0:QKVB], xs[:, u], w_tok[:, r], start=True, stop=True)
                    mm.then_inc(tok_ready, 1)
                    pe.wait_ge(silu_ready, i * 2)
                    for r in range(2):
                        mm = pe.matmul(l_ps[r * B:(r + 1) * B, u, 0:2 * D], ls[:, u], w_up[:, r], start=True, stop=True)
                    mm.then_inc(w_ready, 1)

            def dots(ready, bank, done, gi, k, J):
                pe.wait_ge(ready, k + 1)
                for d in range(DH):
                    mm = pe.matmul(bank[:, gi, 0:HG * J], ident[:], heads(A, gi, J)[:, :, d, :], start=(d == 0), stop=(d == DH - 1))
                mm.then_inc(done, 1)

            def outputs(t, gi, J):
                pe.wait_ge(pv_ready, t * 2 + gi + 1)
                if gi == 0:
                    pe.wait_ge(o_summed, t * 2)
                for j in range(J // 8):
                    mm = pe.matmul(o_ps[:, gi], ident[:], C[:, j * 8 * GD:(j + 1) * 8 * GD], start=(j == 0), stop=(j == J // 8 - 1))
                mm.then_inc(o_ready, 1)

            def project(t, at):
                pe.wait_ge(o_scaled, t + 1)
                pe.transpose(ot_ps[:, 0:P], O[:], ident[:]).then_inc(ot_ready, 1)
                pe.wait_ge(ot_copied, t + 1)
                for r in range(2):
                    mm = pe.matmul(y_ps[:, bass.ds(at * B, B)], w_o[:, r], OT[:, r * B:(r + 1) * B], start=(r == 0), stop=(r == 1))
                mm.then_inc(y_ready, 1)

            def body(t, J, before, at):
                for gi in range(2):
                    dots(wk_ready, u_ps, u_ready, gi, t * 2 + gi, J)
                for gi in range(2):
                    if before:
                        outputs(t - 1, gi, before)
                    dots(qk_ready, l_ps, l_ready, gi, t * 2 + gi, J)
                if before:
                    project(t - 1, at)

            for c in range(S // STEP):
                J = (c + 1) * STEP
                body(c * STEP, J, c * STEP, STEP - 1)
                if c:
                    norm.tensor(pe, c - 1)
                    pe.wait_ge(norm.logvar_ready, c)
                with pe.Fori(0, STEP - 1) as i:
                    body(i + c * STEP + 1, J, J, i)
            for gi in range(2):
                outputs(S - 1, gi, S)
            project(S - 1, STEP - 1)
            norm.tensor(pe, S // STEP - 1)

        @block.scalar
        def _(act):
            act.wait_ge(v_step, 15)
            for a in range(2):
                act.activation(trig[:, a], (th2, th)[a], ACT.Sin).then_inc(s_step, 1)
            with act.Fori(0, S // 2) as i:
                for u in range(2):
                    t = i * 2 + u
                    act.wait_ge(w_ready, t + 1)
                    act.wait_ge(stored, i * 4)
                    act.activation(raw[:, u], l_ps[:, u, 0:2 * D], ACT.Silu).then_inc(silu_ready, 1)
            act.wait_ge(stored, 2 * S)
            act.wait_ge(v_step, 16)
            act.activation(A[:].rearrange("p a n -> p (a n)"), Wd[:], ACT.Square).then_inc(s_step, 1)
            act.wait_ge(v_step, 17)
            act.activation(z, z, ACT.Exp, scale=-1.0).then_inc(s_step, 1)
            act.wait_ge(v_step, 20)
            act.activation(sumsq, sumsq, ACT.Sqrt, scale=2.0).then_inc(s_step, 1)
            load_ln_exp(nc, act)

            def body(t, J):
                for gi in range(2):
                    act.wait_ge(shifted, t * 2 + gi + 1)
                    act.activation(p[:, gi, 0:HG * J], p[:, gi, 0:HG * J], ACT.Exp, scale=SCALE).then_inc(exp_ready, 1)
                act.wait_ge(ot_ready, t + 1)
                act.copy(OT[:], ot_ps[:, 0:P]).then_inc(ot_copied, 1)

            for c in range(S // STEP):
                with act.Fori(0, STEP) as i:
                    body(i + c * STEP, (c + 1) * STEP)
                norm.scalar(act, c, load=False)

        @block.vector
        def _(dve):
            done = [0]

            def step(instruction):
                done[0] += 1
                instruction.then_inc(v_step, 1)
                dve.wait_ge(v_step, done[0])

            def wrap():
                step(dve.tensor_scalar(excess, th2, PI, -2 * PI, ALU.is_gt, ALU.mult))
                step(dve.tensor_tensor(th2, th2, excess, ALU.add))
                step(dve.tensor_scalar(excess, th2, -PI, 2 * PI, ALU.is_lt, ALU.mult))
                step(dve.tensor_tensor(th2, th2, excess, ALU.add))

            dve.wait_ge(weights, 16 * LOADS)
            step(dve.tensor_tensor(w_up, w_up, taps, ALU.mult))
            step(dve.tensor_scalar(th, pos, angle[:, 0:1], angle[:, 1:2], ALU.mult, ALU.add))
            step(dve.tensor_scalar(turns, th, 1 / (2 * PI), None, ALU.mult))
            step(dve.scalar_tensor_tensor(th, turns, -TWO_PI_HI, th, ALU.mult, ALU.add))
            step(dve.scalar_tensor_tensor(th2, turns, -TWO_PI_LO, th, ALU.mult, ALU.add))
            wrap()
            step(dve.tensor_scalar(th, th2, PI, -PI, ALU.min, ALU.max))
            step(dve.tensor_scalar(th2, th, PI / 2, None, ALU.add))
            wrap()
            dve.wait_ge(consts, 1)
            with dve.Fori(0, CHUNKS // 2) as i:
                for u in range(2):
                    dve.wait_ge(low_ready, i * 2 + u + 1)
                    for k in range(KT):
                        lag = KT - 1 - k
                        rows = slice(k * LOW, (k + 1) * LOW)
                        dve.tensor_scalar(low[rows, bass.ds((i * 2 + u) * BC, BC), lag:S],
                                          o_ps[rows, u].rearrange("p (b s) -> p b s", s=S)[:, :, 0:S - lag],
                                          1.0, None, ALU.mult).then_inc(low_copied, 1)
            dve.wait_ge(low_copied, KT * CHUNKS)
            dve.wait_ge(s_step, 2)
            with dve.Fori(0, S // 2) as i:
                for u in range(2):
                    t = i * 2 + u
                    dve.wait_ge(tok_ready, i * 2)
                    dve.wait_ge(w_ready, i * 2)
                    dve.tensor_scalar(xs[:, u, :], Xbt[:, :, bass.ds(t, 1)].rearrange("p b o -> p (b o)"), 1.0, None, ALU.mult).then_inc(staged, 1)
                    dve.tensor_scalar(ls[:, u, :], low[:, :, bass.ds(t, 1)].rearrange("p b o -> p (b o)"), 1.0, None, ALU.mult).then_inc(staged, 1)
                for u in range(2):
                    t = i * 2 + u
                    dve.wait_ge(tok_ready, t + 1)
                    dve.tensor_scalar(QV[:, bass.ds(t * ROW, ROW)], u_ps[:, u, 0:ROW], 1.0, None, ALU.mult)
                    dve.tensor_scalar(beta[:, bass.ds(t, 1), :], u_ps[:, u, None, ROW:ROW + H], 1.0, None, ALU.mult)
                    dve.tensor_scalar(K[:].rearrange("p h d j -> p (h d) j")[:, :, bass.ds(t, 1)],
                                      u_ps[:, u, ROW + H:QKVB][:, :, None], 1.0, None, ALU.mult).then_inc(stored, 1)
                    dve.wait_ge(silu_ready, t + 1)
                    dve.tensor_scalar(Wd[:, bass.ds(t * D, D)], raw[:, u, 0:D], trig[:, 0, bass.ds(t, 1)], None, ALU.mult).then_inc(half_ready, 1)
                    dve.wait_ge(half_ready, t + 1)
                    dve.scalar_tensor_tensor(Wd[:, bass.ds(t * D, D)], raw[:, u, D:2 * D], trig[:, 1, bass.ds(t, 1)],
                                             Wd[:, bass.ds(t * D, D)], ALU.mult, ALU.add).then_inc(stored, 1)
            dve.wait_ge(stored, 2 * S)
            step(dve.tensor_tensor(z.rearrange("p (t h) -> p t h", h=H), beta,
                                   beta_bias[:, None, :].to_broadcast([P, S, H]), ALU.add))
            dve.wait_ge(s_step, 3)
            step(dve.tensor_reduce(sumsq, A[:].rearrange("p a (n d) -> p (a n) d", d=DH), AX_X, ALU.add))
            dve.wait_ge(s_step, 4)
            step(dve.tensor_scalar(z, z, 1.0, None, ALU.add))
            step(dve.scalar_tensor_tensor(sumsq, sumsq, 1e-6, z, ALU.add, ALU.mult))
            step(dve.reciprocal(sumsq, sumsq))
            dve.wait_ge(s_step, 5)
            step(dve.tensor_tensor(Wd[:].rearrange("p (n d) -> p n d", d=DH), Wd[:].rearrange("p (n d) -> p n d", d=DH),
                                   sumsq[:, :, None].to_broadcast([P, S * H, DH]), ALU.mult))

            def soften(t, gi, J, to_end):
                k = t * 2 + gi
                s = p[:, gi, 0:HG * J].rearrange("p (h j) -> p h j", j=J)
                if isinstance(t, int):
                    dve.wait_ge(l_ready, k + 1)
                dve.tensor_tensor(s, l_ps[:, gi, 0:HG * J].rearrange("p (h j) -> p h j", j=J),
                                  shut[:, None, bass.ds(to_end - 1, J)].to_broadcast([P, HG, J]), ALU.add).then_inc(shut_ready, 1)
                dve.wait_ge(shut_ready, k + 1)
                dve.tensor_reduce(top[:, gi], s, AX_X, ALU.max).then_inc(top_ready, 1)
                dve.wait_ge(top_ready, k + 1)
                dve.tensor_tensor(s, s, top[:, gi, :, None].to_broadcast([P, HG, J]), ALU.subtract).then_inc(shifted, 1)

            def product(t, gi, J):
                k = t * 2 + gi
                if not isinstance(t, int) or t:
                    dve.wait_ge(l_ready, k - 1)
                dve.tensor_tensor(heads(A, gi, J), keys(gi, J), row(Wd, t * D + gi * GD, J), ALU.mult).then_inc(wk_ready, 1)

            def update(t, gi, J, to_end):
                k = t * 2 + gi
                dve.wait_ge(u_ready, k + 1)
                dve.tensor_tensor(um[:, gi, 0:HG * J].rearrange("p (h j) -> p h j", j=J),
                                  u_ps[:, gi, 0:HG * J].rearrange("p (h j) -> p h j", j=J),
                                  below[:, None, bass.ds(to_end, J)].to_broadcast([P, HG, J]), ALU.mult).then_inc(um_ready, 1)
                dve.wait_ge(um_ready, k + 1)
                dots = um[:, gi, 0:HG * J].rearrange("p (h j) -> p h j", j=J)[:, :, None, :].to_broadcast([P, HG, DH, J])
                dve.tensor_tensor(heads(A, gi, J), dots, row(Wd, t * D + gi * GD, J), ALU.mult).then_inc(move_ready, 1)
                dve.wait_ge(move_ready, k + 1)
                dve.tensor_tensor(keys(gi, J), keys(gi, J), heads(A, gi, J), ALU.subtract).then_inc(k_ready, 1)
                dve.wait_ge(k_ready, k + 1)
                dve.tensor_tensor(heads(A, gi, J), keys(gi, J), row(QV, t * ROW + gi * GD, J), ALU.mult).then_inc(qk_ready, 1)

            def finish(t, J):
                dve.wait_ge(exp_ready, t * 2 + 2)
                for gi in range(2):
                    dve.tensor_reduce(total[:, gi], p[:, gi, 0:HG * J].rearrange("p (h j) -> p h j", j=J), AX_X, ALU.add).then_inc(total_ready, 1)
                dve.wait_ge(total_ready, t * 2 + 2)
                dve.reciprocal(inv[:], total[:]).then_inc(inv_ready, 1)
                for gi in range(2):
                    dve.wait_ge(o_ready, t * 2 + gi + 1)
                    dve.tensor_reduce(o_sum[:, gi], o_ps[:, gi].rearrange("p (j n) -> p n j", j=8), AX_X, ALU.add).then_inc(o_summed, 1)
                dve.wait_ge(inv_ready, t + 1)
                dve.wait_ge(o_summed, t * 2 + 2)
                dve.wait_ge(ot_ready, t)
                dve.tensor_tensor(O[:].rearrange("p (h d) -> p h d", d=DH), o_sum[:].rearrange("p a (h d) -> p (a h) d", d=DH),
                                  inv[:].rearrange("p a h -> p (a h)")[:, :, None].to_broadcast([P, H, DH]), ALU.mult).then_inc(o_scaled, 1)

            def body(t, J, before):
                to_end = S - t if isinstance(t, int) else dve.snap(S - t)
                for gi in range(2):
                    product(t, gi, J)
                    if before:
                        soften(t - 1, gi, before, to_end + 1)
                for gi in range(2):
                    update(t, gi, J, to_end)
                if before:
                    finish(t - 1, before)

            def close(c):
                norm.vector(dve, c, x=Xbt[:, :, c * STEP:(c + 1) * STEP], y=y_ps[:].rearrange("p (t b) -> p b t", b=B))

            for c in range(S // STEP):
                J = (c + 1) * STEP
                body(c * STEP, J, c * STEP)
                if c:
                    close(c - 1)
                with dve.Fori(0, STEP - 1) as i:
                    body(i + c * STEP + 1, J, J)
            for gi in range(2):
                soften(S - 1, gi, S, 1)
            finish(S - 1, S)
            close(S // STEP - 1)


STAGES = (1, 2, 3, 4, 5, 6)


def build(nc, t):
    with ExitStack() as ctx:
        def sb(name, shape, dt=F32):
            return ctx.enter_context(nc.sbuf_tensor(name, shape, dt))

        g = {"sems": [], "X": sb("X", [P, N]), "ones": sb("ones", [P, P]), "eps": sb("eps", [P, 1]), "ident": sb("ident", [P, P])}
        loaded = ctx.enter_context(nc.semaphore("x_loaded"))
        stored = ctx.enter_context(nc.semaphore("out_stored"))
        filled = ctx.enter_context(nc.semaphore("consts_filled"))
        with nc.Block() as block:
            @block.sync
            def _(sp):
                sp.dma_start(g["X"][:], t["xT"]).then_inc(loaded, 16)
                sp.dma_start(g["ident"][:], t["ident"]).then_inc(loaded, 16)
                sp.wait_ge(loaded, 32)

            @block.gpsimd
            def _(pool):
                pool.memset(g["ones"][:], 1.0 / D).then_inc(filled, 1)
                pool.memset(g["eps"][:], EPS).then_inc(filled, 1)
                pool.wait_ge(filled, 2)
        if 1 in STAGES:
            conv_mlp_stage(nc, g, "s1_", {k[3:]: v for k, v in t.items() if k.startswith("s1_")})
            end_stage(nc, g)
        for n in (2, 3, 4, 5, 6):
            tag = f"s{n}_"
            if n in STAGES:
                w = {k[3:]: v for k, v in t.items() if k.startswith(tag)}
                w["ctxT"], w["mask"], w["outT"] = t["ctxT"], t["mask"], t["outT"]
                if n in (2, 5):
                    attention_stage(nc, g, tag, w, n == 5)
                elif n == 3:
                    expert_choice_stage(nc, g, tag, w)
                elif n == 4:
                    path_attention_stage(nc, g, tag, w)
                elif n == 6:
                    top2_experts_stage(nc, g, tag, w)
                if n != 6:
                    end_stage(nc, g)
        with nc.Block() as block:
            if 6 in STAGES:
                return
            @block.sync
            def _(sp):
                sp.dma_start(t["outT"], g["X"][:]).then_inc(stored, 16)
                sp.wait_ge(stored, 16)


def kernel(**inputs):
    import numpy as np
    import concourse.bacc as bacc
    from concourse.bass_utils import run_bass_kernel_spmd

    a = {k: np.asarray(v) for k, v in inputs.items()}
    f32 = np.float32

    def columns(v):
        return v.reshape(-1, P).T

    def halves(m):
        return m.reshape(2, P, -1).transpose(1, 0, 2)

    def down(m):
        return m.reshape(-1, 2, P, D).transpose(2, 0, 1, 3)

    def direction(m):
        return m.reshape(-1, H, 2, 2, DH).transpose(0, 2, 3, 1, 4).reshape(-1, 2, 2 * D)

    def per_r(m):
        return np.repeat(m, B, 0)

    conv = a["L0_attn_conv_w"]
    conv_bd = np.zeros((P, 2, TAPS, P), f32)
    for o in range(INNER):
        m, r = divmod(o, P)
        conv_bd[r // 32 * 32:r // 32 * 32 + 32, m, :, r] = conv[o]
    lay = {
        "xT": a["x"].reshape(N, D).T,
        "ident": np.eye(P, dtype=f32),
        "s1_in": a["L0_attn_in_proj_w"].T,
        "s1_conv": conv_bd,
        "s1_cols": np.concatenate([columns(a["L0_attn_" + k]) for k in ("conv_b", "ln_g", "ln_b", "cproj_b", "fc_b")], 1),
        "s1_fc": halves(a["L0_attn_fc_w"].T),
        "s1_cproj": a["L0_attn_cproj_w"].T,
        "s1_out": halves(a["L0_attn_out_w"].T),
        "ctxT": a["ctx_1024"].reshape(N, D).T,
        "mask": a["mask_1x1xSxS2_ik0"].reshape(S, S),
        "s3_router": a["L0_ffn_Wg"].T,
        "s3_same": np.kron(np.eye(8), np.ones((16, 16))).astype(f32),
        "s3_before": np.kron(np.eye(8), np.triu(np.ones((16, 16)), 1)).astype(f32),
        "s3_spread": np.kron(np.eye(8), np.ones((1, 16))).astype(f32),
        "s3_gate": a["L0_ffn_W1"].transpose(2, 0, 1),
        "s3_up": a["L0_ffn_W3"].transpose(2, 0, 1),
        "s3_down": down(a["L0_ffn_W2"].transpose(0, 2, 1)),
        "s4_tok": np.stack([np.concatenate([a["L1_attn_q_w"].T, a["L1_attn_v_w"].T, a["L1_attn_bt_w"][r::2].T,
                                            a["L1_attn_k_w"].T], 1) for r in range(2)], 1),
        "s4_low": np.tile(a["L1_attn_w1"].T, (1, 3)),
        "s4_up": np.tile(direction(a["L1_attn_w2"].T), (3, 1, 1)),
        "s4_taps": np.repeat(direction(a["L1_attn_conv_w"].T), 32, 0),
        "s4_o": a["L1_attn_o_w"].T.reshape(H, 2, DH, D).transpose(0, 2, 1, 3).reshape(P, 2, D),
        "s4_angle": per_r(np.stack([a["L1_attn_omega"].reshape(2), a["L1_attn_phi"].reshape(2)], 1)),
        "s4_beta_bias": per_r(a["L1_attn_bt_b"].reshape(H, 2).T),
        "s4_pos": np.broadcast_to(np.arange(S, dtype=f32), (P, S)),
        "s4_below": np.broadcast_to((np.arange(2 * S) < S).astype(f32), (P, 2 * S)),
        "s4_shut": np.broadcast_to(np.where(np.arange(2 * S) < S, 0, -1e30).astype(f32), (P, 2 * S)),
        "s6_router": a["L1_ffn_gate_w"],
        "s6_b_router": a["L1_ffn_gate_b"][:, None],
        "s6_lower": np.broadcast_to(np.tril(np.ones((8, 8), f32), -1), (P, 8, 8)),
        "s6_gate": np.concatenate([a["L1_ffn_rw1"], a["L1_ffn_sw1"]]).transpose(1, 0, 2),
        "s6_up": np.concatenate([a["L1_ffn_rw2"], a["L1_ffn_sw2"]]).transpose(1, 0, 2),
        "s6_down": down(np.concatenate([a["L1_ffn_rw3"], a["L1_ffn_sw3"]])),
        "s6_b_gate": np.concatenate([a["L1_ffn_rb1"], a["L1_ffn_sb1"]]).reshape(-1, 2, P).transpose(2, 0, 1),
        "s6_b_up": np.concatenate([a["L1_ffn_rb2"], a["L1_ffn_sb2"]]).reshape(-1, 2, P).transpose(2, 0, 1),
        "s6_b_down": np.concatenate([a["L1_ffn_rb3"], a["L1_ffn_sb3"]]),
        "s2_qkvo": np.stack([a["L0_xattn_w" + c] for c in "qkvo"], 1),
        "s2_bias": np.stack([a["L0_xattn_b" + c] for c in "qkvo"], 1),
        "s5_qkvo": np.stack([a["L1_xattn_W" + c].T for c in "qkvo"], 1),
        "s5_bias": np.stack([a["L1_xattn_b" + c] for c in "qkvo"], 1),
    }
    nc = bacc.Bacc("TRN2", target_bir_lowering=False, num_devices=1)
    arrays = {k: np.ascontiguousarray(v) for k, v in lay.items()}
    t = {k: nc.dram_tensor("in_" + k, v.shape, mybir.dt.from_np(v.dtype), kind="ExternalInput").ap() for k, v in arrays.items()}
    t["outT"] = nc.dram_tensor("outT", (D, N), F32, kind="ExternalOutput").ap()
    build(nc, t)
    r = run_bass_kernel_spmd(nc, [{"in_" + k: v for k, v in arrays.items()}], core_ids=[0])
    return np.ascontiguousarray(r.results[0]["outT"].T).reshape(B, S, D)
```

```python
from contextlib import ExitStack

import concourse.bass as bass
from concourse import mybir

ALU = mybir.AluOpType
ACT = mybir.ActivationFunctionType
F32 = mybir.dt.float32
I32 = mybir.dt.int32
BF16 = mybir.dt.bfloat16
AX_X = mybir.AxisListType.X

P = 128
B = 64
S = 64
D = 128
N = B * S
W = 512
CHUNKS = N // W
BC = W // S
INNER = 256
TAPS = 4
H = 16
DH = D // H
EPS = 1e-5
LN_EXP_SET = 6


def stage_semaphore(nc, g, name):
    g["sems"].append(nc.alloc_semaphore(name))
    return g["sems"][-1]


def end_stage(nc, g):
    nc.clear_and_free_semaphores(g["sems"])
    g["sems"].clear()
    nc.all_engine_barrier()


def load_ln_exp(nc, act):
    act.add_instruction(mybir.InstLoadActFuncSet(
        name=nc.get_next_instruction_name(), engine=mybir.EngineType.Activation,
        act_func_set_id=LN_EXP_SET, ins=[], outs=[]))


class Norm:

    def __init__(self, nc, sb, sem, X, ones, eps, mean_ps, var_ps, y_ready, y_ps, per=1, buffers=None):
        self.nc, self.X, self.ones, self.eps = nc, X, ones, eps
        self.mean_ps, self.var_ps, self.y_ps, self.y_ready = mean_ps, var_ps, y_ps, y_ready
        self.per = per
        self.resid, self.rstd = buffers or (sb("resid", [P, W])[:], sb("rstd", [P, W])[:])
        self.centred = self.resid
        self.squares = self.rstd
        self.resid_ready = sem("resid_ready")
        self.mean_ready = sem("mean_ready")
        self.centred_ready = sem("centred_ready")
        self.squares_ready = sem("squares_ready")
        self.var_ready = sem("var_ready")
        self.logvar_ready = sem("logvar_ready")
        self.rstd_ready = sem("rstd_ready")
        self.x_ready = sem("x_ready")

    def chunk(self, i):
        return self.X[:, bass.ds(i * W, W)]

    def like(self, buf, x):
        return buf if len(x.shape) == 2 else buf.rearrange("p (a b) -> p a b", b=x.shape[2])

    def add(self, dve, i, bias=None, x=None, y=None):
        x = self.chunk(i) if x is None else x
        y = self.y_ps if y is None else y
        dve.wait_ge(self.y_ready, i * self.per + self.per)
        if bias is None:
            dve.tensor_tensor(self.like(self.resid, x), y, x, ALU.add).then_inc(self.resid_ready, 1)
        else:
            dve.scalar_tensor_tensor(self.like(self.resid, x), y, bias, x, ALU.add, ALU.add).then_inc(self.resid_ready, 1)

    def centre(self, dve, i):
        dve.wait_ge(self.mean_ready, i + 1)
        dve.tensor_tensor(self.centred, self.resid, self.mean_ps, ALU.subtract).then_inc(self.centred_ready, 1)

    def scale(self, dve, i, x=None):
        x = self.chunk(i) if x is None else x
        dve.wait_ge(self.rstd_ready, i + 1)
        dve.tensor_tensor(x, self.like(self.centred, x), self.like(self.rstd, x), ALU.mult).then_inc(self.x_ready, 1)

    def vector(self, dve, i, bias=None, x=None, y=None):
        self.add(dve, i, bias, x, y)
        self.centre(dve, i)
        self.scale(dve, i, x)

    def mean(self, pe, i):
        pe.wait_ge(self.resid_ready, i + 1)
        pe.matmul(self.mean_ps, self.ones[:], self.resid, start=True, stop=True).then_inc(self.mean_ready, 1)

    def variance(self, pe, i):
        pe.wait_ge(self.squares_ready, i + 1)
        pe.matmul(self.var_ps, self.ones[:], self.squares, start=True, stop=True).then_inc(self.var_ready, 1)

    def tensor(self, pe, i):
        self.mean(pe, i)
        self.variance(pe, i)

    def square(self, act, i):
        act.wait_ge(self.centred_ready, i + 1)
        act.activation(self.squares, self.centred, ACT.Square).then_inc(self.squares_ready, 1)

    def root(self, act, i):
        act.wait_ge(self.var_ready, i + 1)
        act.activation(self.rstd, self.var_ps, ACT.Ln, bias=self.eps[:, 0:1]).then_inc(self.logvar_ready, 1)
        act.wait_ge(self.logvar_ready, i + 1)
        act.activation(self.rstd, self.rstd, ACT.Exp, scale=-0.5).then_inc(self.rstd_ready, 1)

    def scalar(self, act, i, load=True):
        self.square(act, i)
        if load:
            load_ln_exp(self.nc, act)
        self.root(act, i)


def conv_mlp_stage(nc, g, tag, w):
    X, ones, eps = g["X"], g["ones"], g["eps"]
    with ExitStack() as ctx:
        def sb(name, shape):
            return ctx.enter_context(nc.sbuf_tensor(tag + name, shape, F32))

        def ps(name, shape=(P, W)):
            return ctx.enter_context(nc.psum_tensor(tag + name, list(shape), F32))

        def sem(name):
            return stage_semaphore(nc, g, tag + name)

        w_in = sb("w_in", [P, 2 * INNER])
        w_conv = sb("w_conv", [P, 2, TAPS, P])
        cols = sb("cols", [P, 9])
        w_fc = sb("w_fc", [P, 2, D])
        w_cproj = sb("w_cproj", [P, INNER])
        w_out = sb("w_out", [P, 2, D])
        ones_inner = sb("ones_inner", [P, P])
        hpad = sb("hpad", [P, 2, BC, S + TAPS - 1])
        gate = sb("gate", [P, 2, W])
        h = sb("h", [P, 2, W])
        c = sb("c", [P, 2, W])
        sq = sb("sq", [P, 2, W])
        rs = sb("rs", [P, W])
        hn = sb("hn", [P, 2, W])
        s_fc = sb("s_fc", [P, W])
        h2 = sb("h2", [P, 2, W])
        h_ps = ps("h_ps", (P, 2, W))
        g_ps = ps("g_ps", (P, 2, W))
        fc_ps = ps("fc_ps")
        var_ps = ps("var_ps")
        cproj_ps = ps("cproj_ps", (P, 2, W))
        mean_ps, norm_var_ps, out_ps = fc_ps, cproj_ps[:, 0], cproj_ps[:, 1]

        weights = sem("weights")
        consts = sem("consts")
        proj_h = sem("proj_h")
        proj_g = sem("proj_g")
        h_copied = sem("h_copied")
        gated = sem("gated")
        conv = sem("conv")
        h_ready = sem("h_ready")
        hmean = sem("hmean")
        c_ready = sem("c_ready")
        sq_ready = sem("sq_ready")
        hvar = sem("hvar")
        log_ready = sem("log_ready")
        rs_ready = sem("rs_ready")
        cn_ready = sem("cn_ready")
        hn_ready = sem("hn_ready")
        fc_ready = sem("fc_ready")
        fc_silu = sem("fc_silu")
        cproj = sem("cproj")
        h2_ready = sem("h2_ready")
        y_ready = sem("y_ready")
        norm = Norm(nc, sb, sem, X, ones, eps, var_ps[:], norm_var_ps, y_ready, out_ps)
        LOADS = 6
        block = ctx.enter_context(nc.Block())

        LAST = CHUNKS - 1

        def chunks(engine, body):
            body(0, False, True)
            with engine.Fori(0, CHUNKS - 2) as i:
                body(i + 1, True, True)
            body(LAST, True, False)

        @block.sync
        def _(sp):
            for dst, name in ((w_in, "in"), (w_conv, "conv"), (cols, "cols"), (w_fc, "fc"),
                              (w_cproj, "cproj"), (w_out, "out")):
                sp.dma_start(dst[:], w[name]).then_inc(weights, 16)

        @block.gpsimd
        def _(pool):
            pool.memset(ones_inner[:], 1.0 / INNER).then_inc(consts, 1)
            pool.memset(hpad[:], 0.0).then_inc(consts, 1)

        @block.tensor
        def _(pe):
            pe.wait_ge(weights, 16 * LOADS)
            pe.wait_ge(consts, 2)

            def project_h(n):
                for m in range(2):
                    pe.matmul(h_ps[:, m], w_in[:, m * P:(m + 1) * P], X[:, bass.ds(n * W, W)], start=True, stop=True).then_inc(proj_h, 1)

            def project_gate(n):
                for m in range(2):
                    pe.matmul(g_ps[:, m], w_in[:, INNER + m * P:INNER + (m + 1) * P], X[:, bass.ds(n * W, W)],
                              start=True, stop=True).then_inc(proj_g, 1)

            def convolve(n, m):
                pe.wait_ge(h_copied, n * 2 + 2)
                for k in range(TAPS):
                    mm = pe.matmul(h_ps[:, m], w_conv[:, m, k], hpad[:, m, :, k:k + S],
                                   start=(k == 0), stop=(k == TAPS - 1))
                mm.then_inc(conv, 1)

            def both(bank, lhs, rhs, done):
                pe.matmul(bank, lhs[0], rhs[:, 0], start=True, stop=False)
                pe.matmul(bank, lhs[1], rhs[:, 1], start=False, stop=True).then_inc(done, 1)

            def body(n, earlier, later):
                pe.wait_ge(h_ready, n * 2 + 2)
                both(mean_ps[:], (ones_inner[:], ones_inner[:]), h, hmean)
                if earlier:
                    norm.mean(pe, n - 1)
                if later:
                    project_h(n + 1)
                if earlier:
                    norm.variance(pe, n - 1)
                pe.wait_ge(sq_ready, n + 1)
                both(var_ps[:], (ones_inner[:], ones_inner[:]), sq, hvar)
                if later:
                    project_gate(n + 1)
                    convolve(n + 1, 0)
                pe.wait_ge(hn_ready, n * 2 + 2)
                both(fc_ps[:], (w_fc[:, 0], w_fc[:, 1]), hn, fc_ready)
                if later:
                    convolve(n + 1, 1)
                pe.wait_ge(fc_silu, n + 1)
                if earlier:
                    pe.wait_ge(norm.logvar_ready, n)
                for m in range(2):
                    pe.matmul(cproj_ps[:, m], w_cproj[:, m * P:(m + 1) * P], s_fc[:], start=True, stop=True).then_inc(cproj, 1)
                pe.wait_ge(h2_ready, n * 2 + 2)
                both(out_ps, (w_out[:, 0], w_out[:, 1]), h2, y_ready)

            project_h(0)
            project_gate(0)
            convolve(0, 0)
            convolve(0, 1)
            chunks(pe, body)
            norm.tensor(pe, LAST)

        @block.scalar
        def _(act):
            act.wait_ge(weights, 16 * LOADS)
            act.wait_ge(consts, 2)

            def pad(n):
                for m in range(2):
                    act.wait_ge(proj_h, n * 2 + 1 + m)
                    act.copy(hpad[:, m, :, TAPS - 1:], h_ps[:, m].rearrange("p (b s) -> p b s", s=S)).then_inc(h_copied, 1)

            def gates(n):
                for m in range(2):
                    act.wait_ge(proj_g, n * 2 + 1 + m)
                    act.activation(gate[:, m], g_ps[:, m], ACT.Silu).then_inc(gated, 1)

            def body(n, earlier, later):
                act.wait_ge(c_ready, n + 1)
                act.activation(sq[:], c[:], ACT.Square).then_inc(sq_ready, 1)
                if earlier:
                    norm.square(act, n - 1)
                if later:
                    pad(n + 1)
                load_ln_exp(nc, act)
                if earlier:
                    norm.root(act, n - 1)
                act.wait_ge(hvar, n + 1)
                act.activation(rs[:], var_ps[:], ACT.Ln, bias=eps[:, 0:1]).then_inc(log_ready, 1)
                act.wait_ge(log_ready, n + 1)
                act.activation(rs[:], rs[:], ACT.Exp, scale=-0.5).then_inc(rs_ready, 1)
                act.wait_ge(cn_ready, n + 1)
                for m in range(2):
                    act.activation(hn[:, m], sq[:, m], ACT.Identity, scale=cols[:, 2 + m:3 + m],
                                   bias=cols[:, 4 + m:5 + m]).then_inc(hn_ready, 1)
                if later:
                    gates(n + 1)
                act.wait_ge(fc_ready, n + 1)
                act.activation(s_fc[:], fc_ps[:], ACT.Silu, bias=cols[:, 8:9]).then_inc(fc_silu, 1)

            pad(0)
            gates(0)
            chunks(act, body)
            norm.scalar(act, LAST)

        @block.vector
        def _(dve):
            dve.wait_ge(weights, 16 * LOADS)

            def gated_channels(n):
                for m in range(2):
                    dve.wait_ge(gated, n * 2 + 1 + m)
                    dve.wait_ge(conv, n * 2 + 1 + m)
                    dve.scalar_tensor_tensor(h[:, m], h_ps[:, m], cols[:, m:m + 1], gate[:, m],
                                             ALU.add, ALU.mult).then_inc(h_ready, 1)

            def body(n, earlier, later):
                dve.wait_ge(hmean, n + 1)
                dve.wait_ge(h_ready, n * 2 + 2)
                dve.tensor_tensor(c[:], h[:], mean_ps[:, None, :].to_broadcast([P, 2, W]), ALU.subtract).then_inc(c_ready, 1)
                if earlier:
                    norm.centre(dve, n - 1)
                    norm.scale(dve, n - 1)
                dve.wait_ge(rs_ready, n + 1)
                dve.wait_ge(hvar, n + 1)
                dve.tensor_tensor(sq[:], c[:], rs[:, None, :].to_broadcast([P, 2, W]), ALU.mult).then_inc(cn_ready, 1)
                for m in range(2):
                    dve.wait_ge(cproj, n * 2 + 1 + m)
                    dve.scalar_tensor_tensor(h2[:, m], cproj_ps[:, m], cols[:, 6 + m:7 + m], h[:, m],
                                             ALU.add, ALU.add).then_inc(h2_ready, 1)
                if later:
                    dve.wait_ge(h2_ready, n * 2 + 2)
                    gated_channels(n + 1)
                norm.add(dve, n)

            gated_channels(0)
            chunks(dve, body)
            norm.centre(dve, LAST)
            norm.scale(dve, LAST)


def attention_stage(nc, g, tag, w, masked):
    X, ones, eps, ident = g["X"], g["ones"], g["eps"], g["ident"]
    with ExitStack() as ctx:
        def sb(name, shape, dt=F32):
            return ctx.enter_context(nc.sbuf_tensor(tag + name, shape, dt))

        def ps(name, shape=(P, W)):
            return ctx.enter_context(nc.psum_tensor(tag + name, list(shape), F32))

        def sem(name):
            return stage_semaphore(nc, g, tag + name)

        w_qkvo = sb("w_qkvo", [P, 4, D])
        bias = sb("bias", [P, 4])
        C = sb("C", [P, 2, W])
        K = sb("K", [P, 2, BC, S])
        Kbd = sb("Kbd", [P, 2, BC, H, S])
        Q = sb("Q", [P, 2, W])
        Vbd = sb("Vbd", [P, 2, BC, H // 2, 2, DH])
        E = sb("E", [P, 2, H, S])
        PT = sb("PT", [P, H // 2, P])
        top = sb("top", [P, 2, H])
        total = sb("total", [P, 2, H])
        share = sb("share", [P, 2, H])
        O = sb("O", [P, 2, D])
        OT = sb("OT", [P, W])
        if masked:
            mask_i = sb("mask_i", [S, S], I32)
            drop = sb("drop", [S, 8, S], BF16)
            pick = sb("pick", [S, S], BF16)

        s_ps = ps("s_ps", (P, 2, W))
        t_ps = ps("t_ps", (P, 2, W))
        o_ps = ps("o_ps")
        ot_ps = ps("ot_ps")
        z0 = ps("z0")
        z1 = ps("z1")

        weights, zeroed = sem("weights"), sem("zeroed")
        c_loaded = [sem("c_loaded0"), sem("c_loaded1")]
        k_ready, q_ready = sem("k_ready"), sem("q_ready")
        k_copied, q_copied = sem("k_copied"), sem("q_copied")
        v_ready = [sem("v0_ready"), sem("v1_ready")]
        v_copied = [sem("v0_copied"), sem("v1_copied")]
        k_spread = [sem("k_spread0"), sem("k_spread1")]
        s_ready, top_ready, e_ready, exp_ready = sem("s_ready"), sem("top_ready"), sem("e_ready"), sem("exp_ready")
        mask_ready = sem("mask_ready")
        total_ready, share_ready = sem("total_ready"), sem("share_ready")
        pt_ready, pt_copied = sem("pt_ready"), sem("pt_copied")
        o_ready, o_scaled, ot_ready, ot_copied = sem("o_ready"), sem("o_scaled"), sem("ot_ready"), sem("ot_copied")
        y_ready = sem("y_ready")
        norm = Norm(nc, sb, sem, X, ones, eps, z1[:], z0[:], y_ready, z0[:])
        block = ctx.enter_context(nc.Block())
        LOADS = 3 if masked else 2
        PAIRS = BC // 2
        LAST = CHUNKS - 1

        def chunks(engine, body):
            body(0, 0)
            body(1, 1)
            with engine.Fori(0, (CHUNKS - 4) // 2) as j:
                body(j * 2 + 2, 0)
                body(j * 2 + 3, 1)
            body(LAST - 1, 0)
            body(LAST, 1)

        def inside(n, ahead):
            return not isinstance(n, int) or 0 <= n + ahead < CHUNKS

        def loads(n, u):
            return n * 8 + (8 if u else 16)

        @block.sync
        def _(sp):
            sp.dma_start(w_qkvo[:], w["qkvo"]).then_inc(weights, 16)
            sp.dma_start(bias[:], w["bias"]).then_inc(weights, 16)
            if masked:
                sp.dma_start(mask_i[:], w["mask"]).then_inc(weights, 16)
            for u in range(2):
                sp.dma_start(C[:, u], w["ctxT"][:, u * W:(u + 1) * W]).then_inc(c_loaded[u], 16)

            def spread(n, u):
                sp.wait_ge(k_copied, n + 1)
                for h in range(H):
                    sp.dma_start(Kbd[h * DH:(h + 1) * DH, u, :, h, :], K[h * DH:(h + 1) * DH, u]).then_inc(k_spread[u], 16)

            sp.wait_ge(zeroed, 3)
            spread(0, 0)
            spread(1, 1)

            def reload(n, u):
                sp.wait_ge(v_ready[1], n + 1)
                sp.dma_start(C[:, u], w["ctxT"][:, bass.ds(n * W + 2 * W, W)]).then_inc(c_loaded[u], 16)
                spread(n + 2, u)

            with sp.Fori(0, (CHUNKS - 2) // 2) as j:
                for u in range(2):
                    reload(j * 2 + u, u)

        @block.gpsimd
        def _(pool):
            pool.memset(Kbd[:, 1], 0.0).then_inc(zeroed, 1)
            pool.memset(Vbd[:], 0.0).then_inc(zeroed, 1)

        @block.tensor
        def _(pe):
            def project_k(n, u):
                pe.wait_ge(c_loaded[u], loads(n, u))
                pe.matmul(z1[:], w_qkvo[:, 1], C[:, u], start=True, stop=True).then_inc(k_ready, 1)

            def project_q(n):
                pe.matmul(z1[:], w_qkvo[:, 0], X[:, bass.ds(n * W, W)], start=True, stop=True).then_inc(q_ready, 1)

            def project_v(half, bank, u):
                for b in range(4):
                    at = (half * 4 + b) * S
                    for h2 in range(2):
                        mm = pe.matmul(bank[h2 * S:(h2 + 1) * S, b * P:(b + 1) * P], C[:, u, at:at + S],
                                       w_qkvo[:, 2], start=True, stop=True)
                mm.then_inc(v_ready[half], 1)

            def scores(u, pr, n):
                if pr == 0:
                    pe.wait_ge(q_copied, n + 1)
                    pe.wait_ge(k_spread[u], loads(n, u) * H)
                if inside(n, -1) or pr:
                    pe.wait_ge(e_ready, n * PAIRS + pr)
                for half in range(2):
                    for b in range(2):
                        out = s_ps[b * S:(b + 1) * S, half]
                        mm = pe.matmul(out, Q[:, u, (2 * pr + b) * S:(2 * pr + b + 1) * S],
                                       Kbd[:, u, 2 * pr + b, half * 8:half * 8 + 8, :], start=True, stop=not masked)
                if masked:
                    for half in range(2):
                        for b in range(2):
                            mm = pe.matmul(s_ps[b * S:(b + 1) * S, half], pick[:], drop[:], start=False, stop=True)
                mm.then_inc(s_ready, 1)

            def transposes(pr, n):
                pe.wait_ge(exp_ready, n * PAIRS + pr + 1)
                if inside(n, -1) or pr:
                    pe.wait_ge(pt_copied, (n * PAIRS + pr) * 2)
                for half in range(2):
                    for c in range(4):
                        mm = pe.transpose(t_ps[:, half, c * P:(c + 1) * P],
                                          E[:, pr % 2, half * 8 + 2 * c:half * 8 + 2 * c + 2, :], ident[:])
                    mm.then_inc(pt_ready, 1)

            def weigh(pr, n, u):
                pe.wait_ge(pt_copied, (n * PAIRS + pr) * 2 + 2)
                if inside(n, -1) or pr:
                    pe.wait_ge(o_scaled, n * PAIRS + pr)
                for hp in range(H // 2):
                    for b in range(2):
                        mm = pe.matmul(o_ps[b * S:(b + 1) * S, hp * 16:hp * 16 + 16], PT[:, hp, b * S:(b + 1) * S],
                                       Vbd[:, u, 2 * pr + b, hp], start=True, stop=True)
                mm.then_inc(o_ready, 1)

            def turn(pr, n):
                pe.wait_ge(o_scaled, n * PAIRS + pr + 1)
                pe.transpose(ot_ps[:, pr * P:(pr + 1) * P], O[:, pr % 2], ident[:]).then_inc(ot_ready, 1)

            def project_o(n):
                pe.wait_ge(ot_copied, n + 1)
                pe.matmul(z0[:], w_qkvo[:, 3], OT[:], start=True, stop=True).then_inc(y_ready, 1)

            def beside(pr, n, u):
                if pr == 0:
                    if inside(n, -2):
                        pe.wait_ge(norm.logvar_ready, n - 1)
                    project_v(1, z0, u)
                    if inside(n, 1):
                        pe.wait_ge(k_copied, n + 2)
                        project_q(n + 1)
                if pr == 1:
                    if inside(n, -1):
                        pe.wait_ge(v_copied[1], n * 2 + 2)
                        project_o(n - 1)
                    if inside(n, 1):
                        pe.wait_ge(q_copied, n + 2)
                        project_v(0, z1, 1 - u)
                if pr == 2 and inside(n, -1):
                    if inside(n, 1):
                        pe.wait_ge(v_copied[0], n * 2 + 4)
                    norm.mean(pe, n - 1)
                if pr == 3:
                    if inside(n, -1):
                        norm.variance(pe, n - 1)
                    elif inside(n, 2):
                        pe.wait_ge(v_copied[0], n * 2 + 4)
                    if inside(n, 2):
                        project_k(n + 2, u)

            def body(n, u):
                for pr in range(PAIRS):
                    transposes(pr, n)
                    if pr < PAIRS - 2:
                        scores(u, pr + 2, n)
                    elif inside(n, 1):
                        scores(1 - u, pr + 2 - PAIRS, n + 1)
                    beside(pr, n, u)
                    if pr:
                        turn(pr - 1, n)
                    elif inside(n, -1):
                        turn(PAIRS - 1, n - 1)
                    weigh(pr, n, u)

            pe.wait_ge(weights, 16 * LOADS)
            if masked:
                pe.wait_ge(mask_ready, 2)
            project_k(0, 0)
            pe.wait_ge(k_copied, 1)
            project_q(0)
            pe.wait_ge(q_copied, 1)
            project_k(1, 1)
            pe.wait_ge(k_copied, 2)
            project_v(0, z1, 0)
            pe.wait_ge(v_copied[0], 2)
            scores(0, 0, 0)
            scores(0, 1, 0)
            chunks(pe, body)
            turn(PAIRS - 1, LAST)
            project_o(LAST)
            norm.mean(pe, LAST)
            norm.variance(pe, LAST)

        @block.scalar
        def _(act):
            def copy_k(n, u):
                act.wait_ge(k_ready, n + 1)
                act.activation(K[:, u], z1[:].rearrange("p (b s) -> p b s", s=S), ACT.Identity, bias=bias[:, 1:2]).then_inc(k_copied, 1)

            def copy_q(n, u):
                act.wait_ge(q_ready, n + 1)
                act.activation(Q[:, u], z1[:], ACT.Identity, bias=bias[:, 0:1]).then_inc(q_copied, 1)

            def copy_v(half, bank, n, u):
                act.wait_ge(v_ready[half], n + 1)
                for h2 in range(2):
                    rows = slice(h2 * S, (h2 + 1) * S)
                    v = bank[rows, :].rearrange("p (b c k d) -> p b c k d", b=4, k=2, d=DH)[:, :, :, h2, :]
                    act.copy(Vbd[rows, u, half * 4:half * 4 + 4, :, h2, :], v).then_inc(v_copied[half], 1)

            def copy_o(n):
                act.wait_ge(ot_ready, n * PAIRS + PAIRS)
                if inside(n, -1):
                    act.wait_ge(y_ready, n)
                act.activation(OT[:], ot_ps[:], ACT.Identity, bias=bias[:, 2:3]).then_inc(ot_copied, 1)

            def exponentials(pr, n):
                act.wait_ge(e_ready, n * PAIRS + pr + 1)
                act.activation(E[:, pr % 2], E[:, pr % 2], ACT.Exp, scale=DH ** -0.5).then_inc(exp_ready, 1)

            def beside(pr, n, u):
                if pr == 0:
                    copy_v(1, z0, n, u)
                    if inside(n, 1):
                        copy_q(n + 1, 1 - u)
                    if inside(n, -1):
                        copy_o(n - 1)
                if pr == 1 and inside(n, 1):
                    copy_v(0, z1, n + 1, 1 - u)
                if pr == 2 and inside(n, -1):
                    norm.square(act, n - 1)
                if pr == 3:
                    if inside(n, -1):
                        norm.root(act, n - 1)
                    if inside(n, 2):
                        copy_k(n + 2, u)

            def body(n, u):
                for pr in range(PAIRS):
                    pair = n * PAIRS + pr
                    for half in range(2):
                        act.wait_ge(pt_ready, pair * 2 + half + 1)
                        if half == 0 and (inside(n, -1) or pr):
                            act.wait_ge(o_ready, pair)
                        act.copy(PT[:, half * 4:half * 4 + 4], t_ps[:, half].rearrange("p (c q) -> p c q", q=P)).then_inc(pt_copied, 1)
                    if pr < PAIRS - 2:
                        exponentials(pr + 2, n)
                    elif inside(n, 1):
                        exponentials(pr + 2 - PAIRS, n + 1)
                    beside(pr, n, u)

            load_ln_exp(nc, act)
            act.wait_ge(weights, 16 * LOADS)
            copy_k(0, 0)
            copy_q(0, 0)
            copy_k(1, 1)
            act.wait_ge(zeroed, 3)
            copy_v(0, z1, 0, 0)
            exponentials(0, 0)
            exponentials(1, 0)
            chunks(act, body)
            copy_o(LAST)
            norm.square(act, LAST)
            norm.root(act, LAST)

        @block.vector
        def _(dve):
            dve.memset(Kbd[:, 0], 0.0).then_inc(zeroed, 1)
            dve.wait_ge(weights, 16 * LOADS)
            if masked:
                dve.tensor_scalar(drop[:], mask_i[:, None, :].to_broadcast([S, 8, S]), 0, -2.0 ** 60, ALU.is_equal,
                                  ALU.mult).then_inc(mask_ready, 1)
                dve.tensor_copy(pick[:], ident[0:S, 0:S]).then_inc(mask_ready, 1)

            def shift(pr, n):
                pair, e = n * PAIRS + pr, pr % 2
                s = s_ps[:].rearrange("p a (h s) -> p (a h) s", s=S)
                dve.wait_ge(s_ready, pair + 1)
                dve.tensor_reduce(top[:, e], s, AX_X, ALU.max).then_inc(top_ready, 1)
                dve.wait_ge(top_ready, pair + 1)
                dve.tensor_tensor(E[:, e], s, top[:, e, :, None].to_broadcast([P, H, S]), ALU.subtract).then_inc(e_ready, 1)

            def sums(pr, n):
                pair, e = n * PAIRS + pr, pr % 2
                dve.wait_ge(exp_ready, pair + 1)
                dve.tensor_reduce(total[:, e], E[:, e], AX_X, ALU.add).then_inc(total_ready, 1)
                dve.wait_ge(total_ready, pair + 1)
                dve.reciprocal(share[:, e], total[:, e]).then_inc(share_ready, 1)

            def scale(pr, n):
                pair, e = n * PAIRS + pr, pr % 2
                dve.wait_ge(o_ready, pair + 1)
                dve.wait_ge(share_ready, pair + 1)
                dve.tensor_tensor(O[:, e].rearrange("p (h d) -> p h d", d=DH),
                                  o_ps[:, 0:D].rearrange("p (h d) -> p h d", d=DH),
                                  share[:, e, :, None].to_broadcast([P, H, DH]), ALU.mult).then_inc(o_scaled, 1)

            def body(n, u):
                for pr in range(PAIRS):
                    sums(pr, n)
                    if pr < PAIRS - 2:
                        shift(pr + 2, n)
                    elif inside(n, 1):
                        shift(pr + 2 - PAIRS, n + 1)
                    scale(pr, n)
                    if pr == 0 and inside(n, -2):
                        norm.scale(dve, n - 2)
                    if pr == 1 and inside(n, -1):
                        norm.add(dve, n - 1, bias[:, 3:4])
                    if pr == 2 and inside(n, -1):
                        norm.centre(dve, n - 1)

            shift(0, 0)
            shift(1, 0)
            chunks(dve, body)
            norm.scale(dve, LAST - 1)
            dve.wait_ge(norm.x_ready, LAST)
            norm.add(dve, LAST, bias[:, 3:4])
            norm.centre(dve, LAST)
            norm.scale(dve, LAST)


class Experts:

    def __init__(self, nc, sb, ps, sem, g, count, biased):
        self.nc, self.g, self.count, self.biased = nc, g, count, biased
        self.w_gate = sb("w_gate", [P, count, INNER])
        self.w_up = sb("w_up", [P, count, INNER])
        self.w_down = sb("w_down", [P, count, 2, D])
        self.share = sb("share", [P, W // P, count])
        self.share_all = sb("share_all", [P, N // P, count])
        self.a = sb("a", [P, 2, W])
        self.h = sb("h", [P, 2, 2, W])
        self.acc = sb("acc", [P, W // P, D])
        self.gate_ps = ps("gate_ps", (P, 2, W))
        self.up_ps = ps("up_ps", (P, 2, W))
        self.y_ps = ps("y_ps", (P, 2, W))
        self.gate_ready, self.up_ready = sem("gate_ready"), sem("up_ready")
        self.silu_ready, self.h_ready = sem("silu_ready"), sem("h_ready")
        self.down_ready, self.acc_ready = sem("down_ready"), sem("acc_ready")
        self.share_ready, self.share_all_ready = sem("share_ready"), sem("share_all_ready")
        if biased:
            self.b_gate = sb("b_gate", [P, count, 2])
            self.b_up = sb("b_up", [P, count, 2])

    def number(self, n, e):
        return n * self.count + e

    def wait(self, engine, semaphore, value):
        if not isinstance(value, int) or value > 0:
            engine.wait_ge(semaphore, value)

    def down(self, pe, k, e):
        pe.wait_ge(self.h_ready, k * 2 + 2)
        self.wait(pe, self.acc_ready, k - 1)
        for t in range(W // P):
            for m in range(2):
                mm = pe.matmul(self.y_ps[:, e % 2, t * P:(t + 1) * P], self.h[:, e % 2, m, t * P:(t + 1) * P],
                               self.w_down[:, e, m], start=(m == 0), stop=(m == 1))
        mm.then_inc(self.down_ready, 1)

    def tensor(self, pe, n, beside):
        tok = bass.ds(n * W, W)
        for e in range(self.count):
            k = self.number(n, e)
            self.wait(pe, self.silu_ready, k * 2)
            for m in range(2):
                pe.matmul(self.gate_ps[:, m], self.w_gate[:, e, m * P:(m + 1) * P], self.g["X"][:, tok],
                          start=True, stop=True).then_inc(self.gate_ready, 1)
            self.wait(pe, self.h_ready, k * 2)
            for m in range(2):
                pe.matmul(self.up_ps[:, m], self.w_up[:, e, m * P:(m + 1) * P], self.g["X"][:, tok],
                          start=True, stop=True).then_inc(self.up_ready, 1)
            beside(e)
            if e or not isinstance(n, int) or n:
                self.down(pe, k - 1, (e - 1) % self.count)

    def scalar(self, act, n, beside):
        for e in range(self.count):
            for m in range(2):
                k = self.number(n, e) * 2 + m
                act.wait_ge(self.gate_ready, k + 1)
                self.wait(act, self.h_ready, k - 1)
                bias = {"bias": self.b_gate[:, e, m:m + 1]} if self.biased else {}
                act.activation(self.a[:, m], self.gate_ps[:, m], ACT.Silu, **bias).then_inc(self.silu_ready, 1)
            beside(e)

    def accumulate(self, dve, k, e):
        dve.wait_ge(self.down_ready, k + 1)
        self.wait(dve, self.acc_ready, k)
        for t in range(W // P):
            y, acc, share = self.y_ps[:, e % 2, t * P:(t + 1) * P], self.acc[:, t], self.share[:, t, e:e + 1]
            if e == 0:
                last = dve.tensor_scalar(acc, y, share, None, ALU.mult)
            else:
                last = dve.scalar_tensor_tensor(acc, y, share, acc, ALU.mult, ALU.add)
        last.then_inc(self.acc_ready, 1)

    def vector(self, dve, n, beside):
        for e in range(self.count):
            k = self.number(n, e)
            for m in range(2):
                dve.wait_ge(self.silu_ready, k * 2 + m + 1)
                dve.wait_ge(self.up_ready, k * 2 + m + 1)
                if self.biased:
                    dve.scalar_tensor_tensor(self.h[:, e % 2, m], self.up_ps[:, m], self.b_up[:, e, m:m + 1],
                                             self.a[:, m], ALU.add, ALU.mult).then_inc(self.h_ready, 1)
                else:
                    dve.tensor_tensor(self.h[:, e % 2, m], self.up_ps[:, m], self.a[:, m], ALU.mult).then_inc(self.h_ready, 1)
            beside(e)
            if e or not isinstance(n, int) or n:
                self.accumulate(dve, k - 1, (e - 1) % self.count)
            if e == 0:
                dve.wait_ge(self.share_all_ready, 1)
                self.wait(dve, self.acc_ready, k)
                dve.tensor_scalar(self.share[:], self.share_all[:, bass.ds(n * (W // P), W // P), :], 1.0, None,
                                  ALU.mult).then_inc(self.share_ready, 1)
                dve.wait_ge(self.share_ready, n + 1)

    def run(self, block, norm, collect, before):
        last = self.count - 1

        def chunks(engine, body):
            body(0)
            with engine.Fori(0, CHUNKS - 1) as i:
                body(i + 1)

        def gather(pe, n):
            pe.wait_ge(self.acc_ready, self.number(n, last) + 1)
            collect(pe, n)

        def beside(n, *work):
            def run(e):
                if (not isinstance(n, int) or n) and 1 <= e <= len(work) and work[e - 1] is not None:
                    work[e - 1](n - 1)
            return run

        @block.tensor
        def _(pe):
            before["tensor"](pe)
            chunks(pe, lambda n: self.tensor(pe, n, beside(
                n, lambda m: gather(pe, m), lambda m: norm.mean(pe, m), lambda m: norm.variance(pe, m))))
            self.down(pe, self.number(CHUNKS - 1, last), last)
            gather(pe, CHUNKS - 1)
            norm.tensor(pe, CHUNKS - 1)

        @block.scalar
        def _(act):
            before["scalar"](act)
            chunks(act, lambda n: self.scalar(act, n, beside(
                n, None, lambda m: norm.square(act, m), lambda m: (load_ln_exp(self.nc, act), norm.root(act, m)))))
            norm.scalar(act, CHUNKS - 1)

        @block.vector
        def _(dve):
            before["vector"](dve)
            chunks(dve, lambda n: self.vector(dve, n, beside(
                n, lambda m: norm.add(dve, m), lambda m: norm.centre(dve, m), None, lambda m: norm.scale(dve, m))))
            self.accumulate(dve, self.number(CHUNKS - 1, last), last)
            norm.vector(dve, CHUNKS - 1)


def expert_choice_stage(nc, g, tag, w):
    X, ones, eps, ident = g["X"], g["ones"], g["eps"], g["ident"]
    NE, CAP = 8, N // 8
    SL = P // NE
    T = N // SL
    BITS = 31
    with ExitStack() as ctx:
        def sb(name, shape, dt=F32):
            return ctx.enter_context(nc.sbuf_tensor(tag + name, shape, dt))

        def ps(name, shape=(P, W)):
            return ctx.enter_context(nc.psum_tensor(tag + name, list(shape), F32))

        def sem(name):
            return stage_semaphore(nc, g, tag + name)

        ex = Experts(nc, sb, ps, sem, g, NE, False)
        yt_ps, misc_ps = ps("yt_ps"), ps("misc_ps")
        w_router = sb("w_router", [P, NE])
        same = sb("same", [P, P])
        before = sb("before", [P, P])
        spread = sb("spread", [NE, P])
        rows = sb("rows", [NE, N])
        top = sb("top", [NE, 1])
        negtop = sb("negtop", [P, 1])
        s = sb("s", [P, T])
        y = sb("y", [P, T])
        one = sb("one", [P, T])
        hits = sb("hits", [P, T])
        count = sb("count", [P, 1])
        pos = sb("pos", [P, 1])
        sign = sb("sign", [P, 1])
        want = sb("want", [P, 1])
        found = sb("found", [P, 1], I32)
        bit = sb("bit", [P, 1], I32)
        cand = sb("cand", [P, 1], I32)
        taken = sb("taken", [P, 1], I32)
        thr = sb("thr", [P, 1])
        above = sb("above", [P, T])
        equal = sb("equal", [P, T])
        rank = sb("rank", [P, T])
        room = sb("room", [P, 1])
        room2 = sb("room2", [P, 1])
        part = sb("part", [P, 1])
        inv = sb("inv", [P, 1])
        exps = sb("exps", [P, T])
        weight = sb("weight", [P, T])

        early, weights, gathered, returned = sem("early"), sem("weights"), sem("gathered"), sem("returned")
        score_ready, score_copied = sem("score_ready"), sem("score_copied")
        v_step = sem("v_step")
        p_step = sem("p_step")
        exp_ready = sem("exp_ready")
        bit_counted, bit_summed = sem("bit_counted"), sem("bit_summed")
        cand_ready, taken_ready, taken_bit, found_ready, bit_moved = (
            sem("cand_ready"), sem("taken_ready"), sem("taken_bit"), sem("found_ready"), sem("bit_moved"))
        turned = sem("turned")
        y_ready = sem("y_ready")
        norm = Norm(nc, sb, sem, X, ones, eps, misc_ps[:], yt_ps[:], y_ready, yt_ps[:])
        block = ctx.enter_context(nc.Block())

        @block.sync
        def _(sp):
            for dst, name in ((w_router, "router"), (same, "same"), (before, "before"), (spread, "spread")):
                sp.dma_start(dst[:], w[name]).then_inc(early, 16)
            for dst, name in ((ex.w_gate, "gate"), (ex.w_up, "up"), (ex.w_down, "down")):
                sp.dma_start(dst[:], w[name]).then_inc(weights, 16)
            sp.wait_ge(score_copied, CHUNKS)
            for e in range(NE):
                sp.dma_start(s[e * SL:(e + 1) * SL, :], rows[e:e + 1, :].rearrange("o (c t) -> o c t", t=T)).then_inc(gathered, 16)
            sp.wait_ge(v_step, 24)
            for e in range(NE):
                sp.dma_start(rows[e:e + 1, :].rearrange("o (c t) -> o c t", t=T), weight[e * SL:(e + 1) * SL, :]).then_inc(returned, 16)

        def route_tensor(pe):
            pe.wait_ge(early, 64)
            for n in range(CHUNKS):
                if n >= 2:
                    pe.wait_ge(score_copied, n - 1)
                bank = (yt_ps, misc_ps)[n % 2]
                pe.matmul(bank[0:NE, :], w_router[:], X[:, n * W:(n + 1) * W], start=True, stop=True).then_inc(score_ready, 1)
            pe.wait_ge(score_copied, CHUNKS)
            pe.wait_ge(v_step, 1)
            pe.matmul(misc_ps[:, 0:1], spread[:], top[:], start=True, stop=True).then_inc(p_step, 1)
            pe.wait_ge(v_step, 5)
            pe.matmul(misc_ps[:, 1:2], same[:], count[:], start=True, stop=True).then_inc(p_step, 1)
            with pe.Fori(0, BITS) as i:
                pe.wait_ge(bit_counted, i + 1)
                pe.matmul(yt_ps[:, 0:1], same[:], count[:], start=True, stop=True).then_inc(bit_summed, 1)
            pe.wait_ge(v_step, 14)
            pe.matmul(misc_ps[:, 2:3], same[:], count[:], start=True, stop=True).then_inc(p_step, 1)
            pe.wait_ge(v_step, 17)
            pe.matmul(misc_ps[:, 3:4], before[:], rank[:, T - 1:T], start=True, stop=True).then_inc(p_step, 1)
            pe.wait_ge(v_step, 22)
            pe.matmul(misc_ps[:, 4:5], same[:], part[:], start=True, stop=True).then_inc(p_step, 1)
            pe.wait_ge(returned, 16 * NE)
            for t in range(N // P):
                mm = pe.transpose(yt_ps[:, t * NE:(t + 1) * NE], rows[:, t * P:(t + 1) * P], ident[0:NE, 0:NE])
            mm.then_inc(turned, 1)
            pe.wait_ge(weights, 48)
            pe.wait_ge(ex.share_all_ready, 1)

        def collect(pe, n):
            for t in range(W // P):
                mm = pe.transpose(yt_ps[:, t * P:(t + 1) * P], ex.acc[:, t], ident[:])
            mm.then_inc(y_ready, 1)

        def route_scalar(act):
            for n in range(CHUNKS):
                act.wait_ge(score_ready, n + 1)
                act.copy(rows[:, n * W:(n + 1) * W], (yt_ps, misc_ps)[n % 2][0:NE, :]).then_inc(score_copied, 1)
            act.wait_ge(v_step, 2)
            act.wait_ge(gathered, 16 * NE)
            act.activation(exps[:], s[:], ACT.Exp, bias=negtop[:, 0:1]).then_inc(exp_ready, 1)

        def route_vector(dve):
            done = [0]

            def step(instruction):
                done[0] += 1
                instruction.then_inc(v_step, 1)
                dve.wait_ge(v_step, done[0])

            dve.wait_ge(score_copied, CHUNKS)
            step(dve.tensor_reduce(top[:], rows[:], AX_X, ALU.max))
            dve.wait_ge(p_step, 1)
            step(dve.tensor_scalar(negtop[:], misc_ps[:, 0:1], -1.0, None, ALU.mult))
            step(dve.memset(one[:], 1.0))
            step(dve.memset(found[:], 0))
            dve.wait_ge(gathered, 16 * NE)
            step(dve.scalar_tensor_tensor(hits[:], s[:], 0.0, one[:], ALU.is_ge, ALU.mult, accum_out=count[:]))
            dve.wait_ge(p_step, 2)
            step(dve.tensor_scalar(pos[:], misc_ps[:, 1:2], float(CAP), None, ALU.is_ge))
            step(dve.tensor_scalar(sign[:], pos[:], 2.0, -1.0, ALU.mult, ALU.add))
            step(dve.tensor_scalar(want[:], pos[:], float(2 * CAP - N - 1), float(N - CAP + 1), ALU.mult, ALU.add))
            step(dve.tensor_scalar(y[:], s[:], sign[:, 0:1], None, ALU.mult))
            step(dve.memset(bit[:], 1 << (BITS - 1)))
            with dve.Fori(0, BITS) as i:
                dve.tensor_tensor(cand[:], found[:], bit[:], ALU.bitwise_or).then_inc(cand_ready, 1)
                dve.wait_ge(cand_ready, i + 1)
                dve.scalar_tensor_tensor(hits[:], y[:], cand[:].bitcast(F32), one[:], ALU.is_ge, ALU.mult,
                                         accum_out=count[:]).then_inc(bit_counted, 1)
                dve.wait_ge(bit_summed, i + 1)
                dve.tensor_scalar(taken[:], yt_ps[:, 0:1], want[:, 0:1], -1.0, ALU.is_ge, ALU.mult).then_inc(taken_ready, 1)
                dve.wait_ge(taken_ready, i + 1)
                dve.tensor_tensor(taken[:], taken[:], bit[:], ALU.bitwise_and).then_inc(taken_bit, 1)
                dve.wait_ge(taken_bit, i + 1)
                dve.tensor_tensor(found[:], found[:], taken[:], ALU.bitwise_or).then_inc(found_ready, 1)
                dve.tensor_scalar(bit[:], bit[:], 1, None, ALU.logical_shift_right).then_inc(bit_moved, 1)
                dve.wait_ge(found_ready, i + 1)
                dve.wait_ge(bit_moved, i + 1)
            step(dve.tensor_scalar(thr[:], found[:].bitcast(F32), sign[:, 0:1], None, ALU.mult))
            step(dve.tensor_scalar(above[:], s[:], thr[:, 0:1], None, ALU.is_gt))
            step(dve.tensor_scalar(equal[:], s[:], thr[:, 0:1], None, ALU.is_equal))
            step(dve.tensor_reduce(count[:], above[:], AX_X, ALU.add))
            dve.wait_ge(p_step, 3)
            step(dve.tensor_scalar(room[:], misc_ps[:, 2:3], -1.0, float(CAP), ALU.mult, ALU.add))
            step(dve.memset(hits[:], 0.0))
            step(dve.tensor_tensor_scan(rank[:], equal[:], hits[:], 0.0, ALU.add, ALU.add))
            dve.wait_ge(p_step, 4)
            step(dve.tensor_tensor(room2[:], room[:], misc_ps[:, 3:4], ALU.subtract))
            step(dve.scalar_tensor_tensor(hits[:], rank[:], room2[:, 0:1], equal[:], ALU.is_le, ALU.mult))
            step(dve.tensor_tensor(above[:], above[:], hits[:], ALU.add))
            dve.wait_ge(exp_ready, 1)
            step(dve.tensor_tensor(exps[:], exps[:], above[:], ALU.mult))
            step(dve.tensor_reduce(part[:], exps[:], AX_X, ALU.add))
            dve.wait_ge(p_step, 5)
            step(dve.reciprocal(inv[:], misc_ps[:, 4:5]))
            step(dve.tensor_scalar(weight[:], exps[:], inv[:, 0:1], None, ALU.mult))
            dve.wait_ge(turned, 1)
            dve.tensor_copy(ex.share_all[:], yt_ps[:, 0:N // P * NE].rearrange("p (t e) -> p t e", e=NE)).then_inc(ex.share_all_ready, 1)

        ex.run(block, norm, collect, {"tensor": route_tensor, "scalar": route_scalar, "vector": route_vector})


def top2_experts_stage(nc, g, tag, w):
    X, ones, eps, ident = g["X"], g["ones"], g["eps"], g["ident"]
    NR, NS = 8, 2
    NE = NR + NS
    TT = N // P
    with ExitStack() as ctx:
        def sb(name, shape, dt=F32):
            return ctx.enter_context(nc.sbuf_tensor(tag + name, shape, dt))

        def ps(name, shape=(P, W)):
            return ctx.enter_context(nc.psum_tensor(tag + name, list(shape), F32))

        def sem(name):
            return stage_semaphore(nc, g, tag + name)

        ex = Experts(nc, sb, ps, sem, g, NE, True)
        yt_ps, misc_ps = ps("yt_ps"), ps("misc_ps")
        w_router = sb("w_router", [P, NR])
        b_router = sb("b_router", [NR, 1])
        b_down = sb("b_down", [NE, D])
        lower = sb("lower", [P, NR, NR])
        gate_rows = sb("gate_rows", [NR, N])
        gates = sb("gates", [P, TT, NR])
        top = sb("top", [P, TT])
        exps = sb("exps", [P, TT, NR])
        total = sb("total", [P, TT])
        inv = sb("inv", [P, TT])
        higher = sb("higher", [P, TT, NR, NR])
        ties = sb("ties", [P, TT, NR, NR])
        rank = sb("rank", [P, TT, NR])
        share_rows = sb("share_rows", [NE, N])

        early, weights = sem("early"), sem("weights")
        filled = sem("filled")
        logits_ready, logits_copied, logits_turned = sem("logits_ready"), sem("logits_copied"), sem("logits_turned")
        v_step = sem("v_step")
        exp_ready = sem("exp_ready")
        share_turned, share_copied = sem("share_turned"), sem("share_copied")
        y_ready, stored = sem("y_ready"), sem("stored")
        norm = Norm(nc, sb, sem, X, ones, eps, misc_ps[:], yt_ps[:], y_ready, yt_ps[:])
        block = ctx.enter_context(nc.Block())

        @block.sync
        def _(sp):
            for dst, name in ((w_router, "router"), (b_router, "b_router"), (lower, "lower")):
                sp.dma_start(dst[:], w[name]).then_inc(early, 16)
            for dst, name in ((ex.w_gate, "gate"), (ex.b_gate, "b_gate"), (ex.w_up, "up"), (ex.b_up, "b_up"),
                              (ex.w_down, "down"), (b_down, "b_down")):
                sp.dma_start(dst[:], w[name]).then_inc(weights, 16)
            with sp.Fori(0, CHUNKS) as n:
                sp.wait_ge(norm.x_ready, n + 1)
                sp.dma_start(w["outT"][:, bass.ds(n * W, W)], X[:, bass.ds(n * W, W)]).then_inc(stored, 16)
            sp.wait_ge(stored, 16 * CHUNKS)

        @block.gpsimd
        def _(pool):
            pool.memset(ex.share_all[:], 1.0 / NS).then_inc(filled, 1)

        def route_tensor(pe):
            pe.wait_ge(early, 48)
            banks = (yt_ps, misc_ps)
            for n in range(CHUNKS):
                if n >= 2:
                    pe.wait_ge(logits_copied, n - 1)
                pe.matmul(banks[n % 2][0:NR, :], w_router[:], X[:, n * W:(n + 1) * W], start=True, stop=True).then_inc(logits_ready, 1)
            pe.wait_ge(logits_copied, CHUNKS)
            for t in range(TT):
                mm = pe.transpose(yt_ps[:, t * NR:(t + 1) * NR], gate_rows[:, t * P:(t + 1) * P], ident[0:NR, 0:NR])
            mm.then_inc(logits_turned, 1)
            pe.wait_ge(ex.share_all_ready, 1)
            for n in range(CHUNKS):
                if n >= 2:
                    pe.wait_ge(share_copied, n - 1)
                for t in range(W // P):
                    mm = pe.transpose(banks[n % 2][0:NE, t * P:(t + 1) * P], ex.share_all[:, n * (W // P) + t], ident[:])
                mm.then_inc(share_turned, 1)
            pe.wait_ge(share_copied, CHUNKS)
            pe.wait_ge(weights, 16 * 6)

        def route_scalar(act):
            act.wait_ge(early, 48)
            for n in range(CHUNKS):
                act.wait_ge(logits_ready, n + 1)
                act.activation(gate_rows[:, n * W:(n + 1) * W], (yt_ps, misc_ps)[n % 2][0:NR, :], ACT.Identity,
                               bias=b_router[:, 0:1]).then_inc(logits_copied, 1)
            act.wait_ge(v_step, 3)
            act.activation(exps[:], exps[:], ACT.Exp).then_inc(exp_ready, 1)
            for n in range(CHUNKS):
                act.wait_ge(share_turned, n + 1)
                act.copy(share_rows[:, n * W:(n + 1) * W], (yt_ps, misc_ps)[n % 2][0:NE, :]).then_inc(share_copied, 1)
            act.wait_ge(weights, 16 * 6)

        def route_vector(dve):
            done = [0]

            def step(instruction):
                done[0] += 1
                instruction.then_inc(v_step, 1)
                dve.wait_ge(v_step, done[0])

            four = [P, TT, NR, NR]
            dve.wait_ge(early, 48)
            dve.wait_ge(filled, 1)
            dve.wait_ge(logits_turned, 1)
            step(dve.tensor_copy(gates[:], yt_ps[:, 0:TT * NR].rearrange("p (t e) -> p t e", e=NR)))
            step(dve.tensor_reduce(top[:], gates[:], AX_X, ALU.max))
            step(dve.tensor_tensor(exps[:], gates[:], top[:, :, None].to_broadcast([P, TT, NR]), ALU.subtract))
            mine, other = gates[:, :, :, None].to_broadcast(four), gates[:, :, None, :].to_broadcast(four)
            step(dve.tensor_tensor(ties[:], other, mine, ALU.is_equal))
            step(dve.tensor_tensor(ties[:], ties[:], lower[:, None, :, :].to_broadcast(four), ALU.mult))
            step(dve.tensor_tensor(higher[:], other, mine, ALU.is_gt))
            step(dve.tensor_tensor(higher[:], higher[:], ties[:], ALU.add))
            step(dve.tensor_reduce(rank[:], higher[:], AX_X, ALU.add))
            dve.wait_ge(exp_ready, 1)
            step(dve.tensor_reduce(total[:], exps[:], AX_X, ALU.add))
            step(dve.reciprocal(inv[:], total[:]))
            step(dve.tensor_tensor(exps[:], exps[:], inv[:, :, None].to_broadcast([P, TT, NR]), ALU.mult))
            dve.scalar_tensor_tensor(ex.share_all[:, :, 0:NR], rank[:], 1.5, exps[:], ALU.is_lt, ALU.mult).then_inc(ex.share_all_ready, 1)
            dve.wait_ge(weights, 16 * 6)

        def collect(pe, n):
            pe.matmul(yt_ps[:], b_down[:], share_rows[:, bass.ds(n * W, W)], start=True, stop=False)
            for t in range(W // P):
                mm = pe.matmul(yt_ps[:, t * P:(t + 1) * P], ex.acc[:, t], ident[:], start=False, stop=(t == W // P - 1))
            mm.then_inc(y_ready, 1)

        ex.run(block, norm, collect, {"tensor": route_tensor, "scalar": route_scalar, "vector": route_vector})


def path_attention_stage(nc, g, tag, w):
    X, ones, eps, ident = g["X"], g["ones"], g["eps"], g["ident"]
    LOW, KT = 32, 3
    HG = H // 2
    GD = HG * DH
    STEP = 8
    GROW = 4
    QKVB = 3 * D + H
    ROW = 2 * D
    SCALE = DH ** -0.5
    PI = 3.141592653589793
    TWO_PI_HI = 6.28125
    TWO_PI_LO = 2 * PI - TWO_PI_HI
    with ExitStack() as ctx:
        def sb(name, shape, dt=F32):
            return ctx.enter_context(nc.sbuf_tensor(tag + name, shape, dt))

        def ps(name, shape=(P, W)):
            return ctx.enter_context(nc.psum_tensor(tag + name, list(shape), F32))

        def sem(name):
            return stage_semaphore(nc, g, tag + name)

        w_o = sb("w_o", [P, 2, D])
        angle = sb("angle", [P, 2])
        beta_bias = sb("beta_bias", [P, H])
        below = sb("below", [P, 2 * S])
        shut = sb("shut", [P, 2 * S])
        K = sb("K", [P, H, DH, S])
        QV = sb("QV", [P, S * ROW])
        Wd = sb("Wd", [P, S * D])
        A = sb("A", [P, 2, HG * DH * S])
        C = sb("C", [P, S * GD])
        trig = sb("trig", [P, 2, S])
        normed = sb("normed", [P, 2, W])
        p = sb("p", [P, 2, HG * S])
        top = sb("top", [P, 2, HG])
        total = sb("total", [P, 2, HG])
        inv = sb("inv", [P, 2, HG])
        o_sum = sb("o_sum", [P, 2, GD])
        O = sb("O", [P, D])
        OT = sb("OT", [P, P])

        A_flat, used = A[:].rearrange("p a n -> p (a n)"), [0]

        def scratch(rows, *shape):
            n = 1
            for x in shape:
                n *= x
            view = A_flat[0:rows, used[0]:used[0] + n]
            used[0] += n
            return view if len(shape) == 1 else view.rearrange("p (a b) -> p a b", b=shape[1])

        w_tok = scratch(P, 2, QKVB)
        w_low = scratch(P, KT * LOW)
        w_up = scratch(KT * LOW, 2, 2 * D)
        taps = scratch(KT * LOW, 2, 2 * D)
        pos = scratch(P, S)
        turns = scratch(P, S).bitcast(I32)
        th, th2, excess = scratch(P, S), scratch(P, S), scratch(P, S)
        xs, ls = scratch(P, 2, B), scratch(KT * LOW, 2, B)
        raw = scratch(P, 2, 2 * D)
        beta = scratch(P, S, H)
        low = C[0:KT * LOW, :].rearrange("p (b s) -> p b s", s=S)
        sumsq, z = C[:, 0:S * H], C[:, S * H:2 * S * H]

        u_ps, l_ps, o_ps = ps("u_ps", (P, 2, W)), ps("l_ps", (P, 2, W)), ps("o_ps", (P, 2, W))
        ot_ps, y_ps = ps("ot_ps"), ps("y_ps")

        weights, consts = sem("weights"), sem("consts")
        v_step, s_step = sem("v_step"), sem("s_step")
        low_ready, low_copied = sem("low_ready"), sem("low_copied")
        staged, tok_ready, w_ready, silu_ready, half_ready = (
            sem("staged"), sem("tok_ready"), sem("w_ready"), sem("silu_ready"), sem("half_ready"))
        qv_stored, k_stored, w_stored = sem("qv_stored"), sem("k_stored"), sem("w_stored")
        wk_ready, u_ready, masked, move_ready, k_ready, qk_ready, l_ready = (
            sem("wk_ready"), sem("u_ready"), sem("masked"), sem("move_ready"), sem("k_ready"), sem("qk_ready"), sem("l_ready"))
        shut_ready, top_ready, shifted, exp_ready, total_ready, inv_ready = (
            sem("shut_ready"), sem("top_ready"), sem("shifted"), sem("exp_ready"), sem("total_ready"), sem("inv_ready"))
        pv_ready, o_ready, o_summed, o_scaled, ot_ready, ot_copied, y_ready = (
            sem("pv_ready"), sem("o_ready"), sem("o_summed"), sem("o_scaled"), sem("ot_ready"), sem("ot_copied"), sem("y_ready"))
        norm = Norm(nc, sb, sem, X, ones, eps, ot_ps[:], ot_ps[:], y_ready, None, per=STEP,
                    buffers=(normed[:, 0], normed[:, 1]))
        block = ctx.enter_context(nc.Block())

        def steps(engine, body):
            for t in range(0, S, GROW):
                J, peeled = t + GROW, 1
                body(t, J, t, (t - 1) % STEP, None)
                if t and t % STEP == 0:
                    body(t + 1, J, J, 0, t // STEP - 1)
                    peeled = 2
                with engine.Fori(0, GROW - peeled) as i:
                    body(i + t + peeled, J, J, i + (t + peeled - 1) % STEP, None)

        def pairs(engine, count, body):
            body(0)
            with engine.Fori(0, count // 2 - 2) as i:
                body(i * 2 + 2)
            body(count - 2)

        LOADS = 10
        Xbt = X[:].rearrange("p (b t) -> p b t", t=S)

        def heads(buf, gi, J):
            return buf[:, gi, 0:HG * DH * J].rearrange("p (h d j) -> p h d j", h=HG, d=DH)

        def keys(gi, J):
            return K[:, gi * HG:(gi + 1) * HG, :, 0:J]

        def row(buf, at, J):
            return buf[:, bass.ds(at, GD)].rearrange("p (h d) -> p h d", d=DH)[:, :, :, None].to_broadcast([P, HG, DH, J])

        @block.sync
        def _(sp):
            for dst, name in ((w_tok, "tok"), (w_low, "low"), (w_up, "up"), (taps, "taps"), (w_o, "o"), (angle, "angle"),
                              (beta_bias, "beta_bias"), (pos, "pos"), (below, "below"), (shut, "shut")):
                sp.dma_start(dst[:], w[name]).then_inc(weights, 16)

        @block.gpsimd
        def _(pool):
            pool.memset(low[0:2 * LOW, :, 0:2], 0.0).then_inc(consts, 1)

            def weigh(t, J):
                for gi in range(2):
                    k = t * 2 + gi
                    pool.wait_ge(exp_ready, k + 1)
                    pool.wait_ge(o_ready, k)
                    v = QV[:].rearrange("p (j c) -> p j c", c=ROW)[:, 0:J, D + gi * GD:D + (gi + 1) * GD]
                    pool.tensor_tensor(C[:, 0:J * GD].rearrange("p (j h d) -> p j h d", h=HG, d=DH),
                                       v.rearrange("p j (h d) -> p j h d", d=DH),
                                       p[:, gi, 0:HG * J].rearrange("p (h j) -> p j h", j=J)[:, :, :, None].to_broadcast([P, J, HG, DH]),
                                       ALU.mult).then_inc(pv_ready, 1)

            pool.wait_ge(v_step, 21)
            for c in range(S // GROW):
                with pool.Fori(0, GROW) as i:
                    weigh(i + c * GROW, (c + 1) * GROW)

        @block.tensor
        def _(pe):
            pe.wait_ge(weights, 16 * LOADS)

            def project_low(n):
                for u in range(2):
                    if not isinstance(n, int) or n:
                        pe.wait_ge(low_copied, (n + u - 1) * KT)
                    pe.matmul(o_ps[0:KT * LOW, u], w_low, X[:, bass.ds((n + u) * W, W)], start=True, stop=True).then_inc(low_ready, 1)

            def project_tokens(t):
                for u in range(2):
                    pe.wait_ge(staged, (t + u) * 2 + 2)
                    if not isinstance(t, int) or t:
                        pe.wait_ge(qv_stored, t + u - 1)
                        pe.wait_ge(k_stored, t + u - 1)
                    for r in range(2):
                        pe.matmul(o_ps[r * B:(r + 1) * B, u, 0:ROW], xs[:, u], w_tok[:, r, 0:ROW], start=True, stop=True)
                    for r in range(2):
                        mm = pe.matmul(u_ps[r * B:(r + 1) * B, u, 0:QKVB - ROW], xs[:, u], w_tok[:, r, ROW:QKVB],
                                       start=True, stop=True)
                    mm.then_inc(tok_ready, 1)
                    if not isinstance(t, int) or t:
                        pe.wait_ge(silu_ready, t + u - 1)
                    for r in range(2):
                        mm = pe.matmul(l_ps[r * B:(r + 1) * B, u, 0:2 * D], ls[:, u], w_up[:, r], start=True, stop=True)
                    mm.then_inc(w_ready, 1)

            pairs(pe, CHUNKS, project_low)
            pe.wait_ge(v_step, 1)
            pe.wait_ge(low_copied, CHUNKS * KT)
            pairs(pe, S, project_tokens)

            def dots(ready, bank, done, gi, k, J):
                pe.wait_ge(ready, k + 1)
                for d in range(DH):
                    mm = pe.matmul(bank[:, gi, 0:HG * J], ident[:], heads(A, gi, J)[:, :, d, :], start=(d == 0), stop=(d == DH - 1))
                mm.then_inc(done, 1)

            def outputs(t, gi, J):
                pe.wait_ge(pv_ready, t * 2 + gi + 1)
                if gi == 0:
                    pe.wait_ge(o_summed, t * 2)
                for j in range(J // 4):
                    mm = pe.matmul(o_ps[:, gi, 0:4 * GD], ident[:], C[:, j * 4 * GD:(j + 1) * 4 * GD], start=(j == 0), stop=(j == J // 4 - 1))
                mm.then_inc(o_ready, 1)

            def project(t, slot):
                pe.wait_ge(o_scaled, t + 1)
                pe.transpose(ot_ps[:, 0:P], O[:], ident[:]).then_inc(ot_ready, 1)
                pe.wait_ge(ot_copied, t + 1)
                for r in range(2):
                    mm = pe.matmul(y_ps[:, bass.ds(slot * B, B)], w_o[:, r], OT[:, r * B:(r + 1) * B], start=(r == 0), stop=(r == 1))
                mm.then_inc(y_ready, 1)

            def body(t, J, before, slot, closed):
                for gi in range(2):
                    dots(wk_ready, u_ps, u_ready, gi, t * 2 + gi, J)
                    if closed is not None and gi == 0:
                        norm.mean(pe, closed)
                for gi in range(2):
                    if before:
                        outputs(t - 1, gi, before)
                    dots(qk_ready, l_ps, l_ready, gi, t * 2 + gi, J)
                    if closed is not None and gi == 0:
                        norm.variance(pe, closed)
                if closed is not None:
                    pe.wait_ge(norm.logvar_ready, closed + 1)
                if before:
                    project(t - 1, slot)

            steps(pe, body)
            for gi in range(2):
                outputs(S - 1, gi, S)
            project(S - 1, STEP - 1)
            norm.tensor(pe, S // STEP - 1)

        @block.scalar
        def _(act):
            act.wait_ge(v_step, 15)
            for a in range(2):
                act.activation(trig[:, a], (th2, th)[a], ACT.Sin).then_inc(s_step, 1)

            def activate(t):
                for u in range(2):
                    act.wait_ge(w_ready, t + u + 1)
                    if not isinstance(t, int) or t:
                        act.wait_ge(w_stored, t + u - 1)
                    act.activation(raw[:, u], l_ps[:, u, 0:2 * D], ACT.Silu).then_inc(silu_ready, 1)
                    act.copy(QV[:, bass.ds(t * ROW + u * ROW, ROW)], o_ps[:, u, 0:ROW]).then_inc(qv_stored, 1)

            pairs(act, S, activate)
            act.wait_ge(w_stored, S)
            act.wait_ge(v_step, 16)
            act.activation(A[:].rearrange("p a n -> p (a n)"), Wd[:], ACT.Square).then_inc(s_step, 1)
            act.wait_ge(v_step, 17)
            act.activation(z, z, ACT.Exp, scale=-1.0).then_inc(s_step, 1)
            act.wait_ge(v_step, 20)
            act.activation(sumsq, sumsq, ACT.Sqrt, scale=2.0).then_inc(s_step, 1)
            load_ln_exp(nc, act)

            def exponentials(t, gi, J):
                act.wait_ge(shifted, t * 2 + gi + 1)
                act.activation(p[:, gi, 0:HG * J], p[:, gi, 0:HG * J], ACT.Exp, scale=SCALE).then_inc(exp_ready, 1)

            def copy_turned(t):
                act.wait_ge(ot_ready, t + 1)
                act.copy(OT[:], ot_ps[:, 0:P]).then_inc(ot_copied, 1)

            def body(t, J, before, slot, closed):
                if not before:
                    return
                exponentials(t - 1, 0, before)
                if closed is not None:
                    norm.square(act, closed)
                exponentials(t - 1, 1, before)
                if closed is not None:
                    norm.root(act, closed)
                copy_turned(t - 1)

            steps(act, body)
            for gi in range(2):
                exponentials(S - 1, gi, S)
            copy_turned(S - 1)
            norm.scalar(act, S // STEP - 1, load=False)

        @block.vector
        def _(dve):
            done = [0]

            def step(instruction):
                done[0] += 1
                instruction.then_inc(v_step, 1)
                dve.wait_ge(v_step, done[0])

            def wrap():
                step(dve.tensor_scalar(excess, th2, PI, -2 * PI, ALU.is_gt, ALU.mult))
                step(dve.tensor_tensor(th2, th2, excess, ALU.add))
                step(dve.tensor_scalar(excess, th2, -PI, 2 * PI, ALU.is_lt, ALU.mult))
                step(dve.tensor_tensor(th2, th2, excess, ALU.add))

            dve.wait_ge(weights, 16 * LOADS)
            step(dve.tensor_tensor(w_up, w_up, taps, ALU.mult))
            step(dve.tensor_scalar(th, pos, angle[:, 0:1], angle[:, 1:2], ALU.mult, ALU.add))
            step(dve.tensor_scalar(turns, th, 1 / (2 * PI), None, ALU.mult))
            step(dve.scalar_tensor_tensor(th, turns, -TWO_PI_HI, th, ALU.mult, ALU.add))
            step(dve.scalar_tensor_tensor(th2, turns, -TWO_PI_LO, th, ALU.mult, ALU.add))
            wrap()
            step(dve.tensor_scalar(th, th2, PI, -PI, ALU.min, ALU.max))
            step(dve.tensor_scalar(th2, th, PI / 2, None, ALU.add))
            wrap()
            dve.wait_ge(consts, 1)

            def copy_low(n):
                for u in range(2):
                    dve.wait_ge(low_ready, n + u + 1)
                    for k in range(KT):
                        lag = KT - 1 - k
                        rows = slice(k * LOW, (k + 1) * LOW)
                        dve.tensor_scalar(low[rows, bass.ds((n + u) * BC, BC), lag:S],
                                          o_ps[rows, u].rearrange("p (b s) -> p b s", s=S)[:, :, 0:S - lag],
                                          1.0, None, ALU.mult).then_inc(low_copied, 1)

            def stage(t, u):
                dve.tensor_scalar(xs[:, u, :], Xbt[:, :, bass.ds(t + u, 1)].rearrange("p b o -> p (b o)"), 1.0, None, ALU.mult).then_inc(staged, 1)
                dve.tensor_scalar(ls[:, u, :], low[:, :, bass.ds(t + u, 1)].rearrange("p b o -> p (b o)"), 1.0, None, ALU.mult).then_inc(staged, 1)

            def rotate(t, u):
                dve.wait_ge(silu_ready, t + 1)
                dve.tensor_scalar(Wd[:, bass.ds(t * D, D)], raw[:, u, 0:D], trig[:, 0, bass.ds(t, 1)], None, ALU.mult).then_inc(half_ready, 1)
                dve.wait_ge(half_ready, t + 1)
                dve.scalar_tensor_tensor(Wd[:, bass.ds(t * D, D)], raw[:, u, D:2 * D], trig[:, 1, bass.ds(t, 1)],
                                         Wd[:, bass.ds(t * D, D)], ALU.mult, ALU.add).then_inc(w_stored, 1)

            def store(t):
                for u in range(2):
                    dve.wait_ge(tok_ready, t + u + 1)
                    dve.wait_ge(w_ready, t + u + 1)
                    if not isinstance(t, int) or t < S - 2:
                        stage(t + 2, u)
                    dve.tensor_scalar(beta[:, bass.ds(t + u, 1), :], u_ps[:, u, None, 0:H], 1.0, None, ALU.mult)
                    dve.tensor_scalar(K[:].rearrange("p h d j -> p (h d) j")[:, :, bass.ds(t + u, 1)],
                                      u_ps[:, u, H:QKVB - ROW][:, :, None], 1.0, None, ALU.mult).then_inc(k_stored, 1)
                    if not isinstance(t, int) or t + u:
                        rotate(t + u - 1, 1 - u)

            pairs(dve, CHUNKS, copy_low)
            dve.wait_ge(low_copied, KT * CHUNKS)
            dve.wait_ge(s_step, 2)
            stage(0, 0)
            stage(0, 1)
            pairs(dve, S, store)
            rotate(S - 1, 1)
            dve.wait_ge(w_stored, S)
            dve.wait_ge(k_stored, S)
            step(dve.tensor_tensor(z.rearrange("p (t h) -> p t h", h=H), beta,
                                   beta_bias[:, None, :].to_broadcast([P, S, H]), ALU.add))
            dve.wait_ge(s_step, 3)
            step(dve.tensor_reduce(sumsq, A[:].rearrange("p a (n d) -> p (a n) d", d=DH), AX_X, ALU.add))
            dve.wait_ge(s_step, 4)
            step(dve.tensor_scalar(z, z, 1.0, None, ALU.add))
            step(dve.scalar_tensor_tensor(sumsq, sumsq, 1e-6, z, ALU.add, ALU.mult))
            step(dve.reciprocal(sumsq, sumsq))
            dve.wait_ge(s_step, 5)
            step(dve.tensor_tensor(Wd[:].rearrange("p (n d) -> p n d", d=DH), Wd[:].rearrange("p (n d) -> p n d", d=DH),
                                   sumsq[:, :, None].to_broadcast([P, S * H, DH]), ALU.mult))

            def soften(t, gi, J, to_end):
                k = t * 2 + gi
                s = p[:, gi, 0:HG * J].rearrange("p (h j) -> p h j", j=J)
                if isinstance(t, int):
                    dve.wait_ge(l_ready, k + 1)
                l = l_ps[:, gi, 0:HG * J].rearrange("p (h j) -> p h j", j=J)
                dve.tensor_tensor(l[:, :, J - GROW:J], l[:, :, J - GROW:J],
                                  shut[:, None, bass.ds(to_end + (J - GROW - 1), GROW)].to_broadcast([P, HG, GROW]), ALU.add).then_inc(shut_ready, 1)
                dve.wait_ge(shut_ready, k + 1)
                dve.tensor_reduce(top[:, gi], l, AX_X, ALU.max).then_inc(top_ready, 1)
                dve.wait_ge(top_ready, k + 1)
                dve.tensor_tensor(s, l, top[:, gi, :, None].to_broadcast([P, HG, J]), ALU.subtract).then_inc(shifted, 1)

            def product(t, gi, J):
                k = t * 2 + gi
                if not isinstance(t, int) or t:
                    dve.wait_ge(l_ready, k - 1)
                dve.tensor_tensor(heads(A, gi, J), keys(gi, J), row(Wd, t * D + gi * GD, J), ALU.mult).then_inc(wk_ready, 1)

            def update(t, gi, J, to_end):
                k = t * 2 + gi
                dve.wait_ge(u_ready, k + 1)
                dots = u_ps[:, gi, 0:HG * J].rearrange("p (h j) -> p h j", j=J)
                dve.tensor_tensor(dots[:, :, J - GROW:J], dots[:, :, J - GROW:J],
                                  below[:, None, bass.ds(to_end + (J - GROW), GROW)].to_broadcast([P, HG, GROW]), ALU.mult).then_inc(masked, 1)
                dve.wait_ge(masked, k + 1)
                dve.tensor_tensor(heads(A, gi, J), dots[:, :, None, :].to_broadcast([P, HG, DH, J]), row(Wd, t * D + gi * GD, J), ALU.mult).then_inc(move_ready, 1)
                dve.wait_ge(move_ready, k + 1)
                dve.tensor_tensor(keys(gi, J), keys(gi, J), heads(A, gi, J), ALU.subtract).then_inc(k_ready, 1)
                dve.wait_ge(k_ready, k + 1)
                dve.tensor_tensor(heads(A, gi, J), keys(gi, J), row(QV, t * ROW + gi * GD, J), ALU.mult).then_inc(qk_ready, 1)

            def finish(t, J):
                dve.wait_ge(exp_ready, t * 2 + 2)
                for gi in range(2):
                    dve.tensor_reduce(total[:, gi], p[:, gi, 0:HG * J].rearrange("p (h j) -> p h j", j=J), AX_X, ALU.add).then_inc(total_ready, 1)
                dve.wait_ge(total_ready, t * 2 + 2)
                dve.reciprocal(inv[:], total[:]).then_inc(inv_ready, 1)
                for gi in range(2):
                    dve.wait_ge(o_ready, t * 2 + gi + 1)
                    dve.tensor_reduce(o_sum[:, gi], o_ps[:, gi, 0:4 * GD].rearrange("p (j n) -> p n j", j=4), AX_X, ALU.add).then_inc(o_summed, 1)
                dve.wait_ge(inv_ready, t + 1)
                dve.wait_ge(o_summed, t * 2 + 2)
                dve.wait_ge(ot_ready, t)
                dve.tensor_tensor(O[:].rearrange("p (h d) -> p h d", d=DH), o_sum[:].rearrange("p a (h d) -> p (a h) d", d=DH),
                                  inv[:].rearrange("p a h -> p (a h)")[:, :, None].to_broadcast([P, H, DH]), ALU.mult).then_inc(o_scaled, 1)

            def body(t, J, before, slot, closed):
                to_end = S - t if isinstance(t, int) else dve.snap(S - t)
                product(t, 0, J)
                if closed is not None:
                    norm.add(dve, closed, x=positions(closed), y=projected)
                if before:
                    soften(t - 1, 0, before, to_end + 1)
                product(t, 1, J)
                if closed is not None:
                    norm.centre(dve, closed)
                if before:
                    soften(t - 1, 1, before, to_end + 1)
                for gi in range(2):
                    update(t, gi, J, to_end)
                if closed is not None:
                    norm.scale(dve, closed, positions(closed))
                if before:
                    finish(t - 1, before)

            def positions(c):
                return Xbt[:, :, c * STEP:(c + 1) * STEP]

            projected = y_ps[:].rearrange("p (t b) -> p b t", b=B)
            steps(dve, body)
            for gi in range(2):
                soften(S - 1, gi, S, 1)
            finish(S - 1, S)
            norm.vector(dve, S // STEP - 1, x=positions(S // STEP - 1), y=projected)


STAGES = (1, 2, 3, 4, 5, 6)


def build(nc, t):
    with ExitStack() as ctx:
        def sb(name, shape, dt=F32):
            return ctx.enter_context(nc.sbuf_tensor(name, shape, dt))

        g = {"sems": [], "X": sb("X", [P, N]), "ones": sb("ones", [P, P]), "eps": sb("eps", [P, 1]), "ident": sb("ident", [P, P])}
        loaded = ctx.enter_context(nc.semaphore("x_loaded"))
        stored = ctx.enter_context(nc.semaphore("out_stored"))
        filled = ctx.enter_context(nc.semaphore("consts_filled"))
        with nc.Block() as block:
            @block.sync
            def _(sp):
                sp.dma_start(g["X"][:], t["xT"]).then_inc(loaded, 16)
                sp.dma_start(g["ident"][:], t["ident"]).then_inc(loaded, 16)
                sp.wait_ge(loaded, 32)

            @block.gpsimd
            def _(pool):
                pool.memset(g["ones"][:], 1.0 / D).then_inc(filled, 1)
                pool.memset(g["eps"][:], EPS).then_inc(filled, 1)
                pool.wait_ge(filled, 2)
        if 1 in STAGES:
            conv_mlp_stage(nc, g, "s1_", {k[3:]: v for k, v in t.items() if k.startswith("s1_")})
            end_stage(nc, g)
        for n in (2, 3, 4, 5, 6):
            tag = f"s{n}_"
            if n in STAGES:
                w = {k[3:]: v for k, v in t.items() if k.startswith(tag)}
                w["ctxT"], w["mask"], w["outT"] = t["ctxT"], t["mask"], t["outT"]
                if n in (2, 5):
                    attention_stage(nc, g, tag, w, n == 5)
                elif n == 3:
                    expert_choice_stage(nc, g, tag, w)
                elif n == 4:
                    path_attention_stage(nc, g, tag, w)
                elif n == 6:
                    top2_experts_stage(nc, g, tag, w)
                if n != 6:
                    end_stage(nc, g)
        with nc.Block() as block:
            if 6 in STAGES:
                return
            @block.sync
            def _(sp):
                sp.dma_start(t["outT"], g["X"][:]).then_inc(stored, 16)
                sp.wait_ge(stored, 16)


def kernel(**inputs):
    import numpy as np
    import concourse.bacc as bacc
    from concourse.bass_utils import run_bass_kernel_spmd

    a = {k: np.asarray(v) for k, v in inputs.items()}
    f32 = np.float32

    def columns(v):
        return v.reshape(-1, P).T

    def halves(m):
        return m.reshape(2, P, -1).transpose(1, 0, 2)

    def down(m):
        return m.reshape(-1, 2, P, D).transpose(2, 0, 1, 3)

    def direction(m):
        return m.reshape(-1, H, 2, 2, DH).transpose(0, 2, 3, 1, 4).reshape(-1, 2, 2 * D)

    def per_r(m):
        return np.repeat(m, B, 0)

    conv = a["L0_attn_conv_w"]
    conv_bd = np.zeros((P, 2, TAPS, P), f32)
    for o in range(INNER):
        m, r = divmod(o, P)
        conv_bd[r // 32 * 32:r // 32 * 32 + 32, m, :, r] = conv[o]
    lay = {
        "xT": a["x"].reshape(N, D).T,
        "ident": np.eye(P, dtype=f32),
        "s1_in": a["L0_attn_in_proj_w"].T,
        "s1_conv": conv_bd,
        "s1_cols": np.concatenate([columns(a["L0_attn_" + k]) for k in ("conv_b", "ln_g", "ln_b", "cproj_b", "fc_b")], 1),
        "s1_fc": halves(a["L0_attn_fc_w"].T),
        "s1_cproj": a["L0_attn_cproj_w"].T,
        "s1_out": halves(a["L0_attn_out_w"].T),
        "ctxT": a["ctx_1024"].reshape(N, D).T,
        "mask": a["mask_1x1xSxS2_ik0"].reshape(S, S),
        "s3_router": a["L0_ffn_Wg"].T,
        "s3_same": np.kron(np.eye(8), np.ones((16, 16))).astype(f32),
        "s3_before": np.kron(np.eye(8), np.triu(np.ones((16, 16)), 1)).astype(f32),
        "s3_spread": np.kron(np.eye(8), np.ones((1, 16))).astype(f32),
        "s3_gate": a["L0_ffn_W1"].transpose(2, 0, 1),
        "s3_up": a["L0_ffn_W3"].transpose(2, 0, 1),
        "s3_down": down(a["L0_ffn_W2"].transpose(0, 2, 1)),
        "s4_tok": np.stack([np.concatenate([a["L1_attn_q_w"].T, a["L1_attn_v_w"].T, a["L1_attn_bt_w"][r::2].T,
                                            a["L1_attn_k_w"].T], 1) for r in range(2)], 1),
        "s4_low": np.tile(a["L1_attn_w1"].T, (1, 3)),
        "s4_up": np.tile(direction(a["L1_attn_w2"].T), (3, 1, 1)),
        "s4_taps": np.repeat(direction(a["L1_attn_conv_w"].T), 32, 0),
        "s4_o": a["L1_attn_o_w"].T.reshape(H, 2, DH, D).transpose(0, 2, 1, 3).reshape(P, 2, D),
        "s4_angle": per_r(np.stack([a["L1_attn_omega"].reshape(2), a["L1_attn_phi"].reshape(2)], 1)),
        "s4_beta_bias": per_r(a["L1_attn_bt_b"].reshape(H, 2).T),
        "s4_pos": np.broadcast_to(np.arange(S, dtype=f32), (P, S)),
        "s4_below": np.broadcast_to((np.arange(2 * S) < S).astype(f32), (P, 2 * S)),
        "s4_shut": np.broadcast_to(np.where(np.arange(2 * S) < S, 0, -1e30).astype(f32), (P, 2 * S)),
        "s6_router": a["L1_ffn_gate_w"],
        "s6_b_router": a["L1_ffn_gate_b"][:, None],
        "s6_lower": np.broadcast_to(np.tril(np.ones((8, 8), f32), -1), (P, 8, 8)),
        "s6_gate": np.concatenate([a["L1_ffn_rw1"], a["L1_ffn_sw1"]]).transpose(1, 0, 2),
        "s6_up": np.concatenate([a["L1_ffn_rw2"], a["L1_ffn_sw2"]]).transpose(1, 0, 2),
        "s6_down": down(np.concatenate([a["L1_ffn_rw3"], a["L1_ffn_sw3"]])),
        "s6_b_gate": np.concatenate([a["L1_ffn_rb1"], a["L1_ffn_sb1"]]).reshape(-1, 2, P).transpose(2, 0, 1),
        "s6_b_up": np.concatenate([a["L1_ffn_rb2"], a["L1_ffn_sb2"]]).reshape(-1, 2, P).transpose(2, 0, 1),
        "s6_b_down": np.concatenate([a["L1_ffn_rb3"], a["L1_ffn_sb3"]]),
        "s2_qkvo": np.stack([a["L0_xattn_w" + c] for c in "qkvo"], 1),
        "s2_bias": np.stack([a["L0_xattn_b" + c] for c in "qkvo"], 1),
        "s5_qkvo": np.stack([a["L1_xattn_W" + c].T for c in "qkvo"], 1),
        "s5_bias": np.stack([a["L1_xattn_b" + c] for c in "qkvo"], 1),
    }
    nc = bacc.Bacc("TRN2", target_bir_lowering=False, num_devices=1)
    arrays = {k: np.ascontiguousarray(v) for k, v in lay.items()}
    t = {k: nc.dram_tensor("in_" + k, v.shape, mybir.dt.from_np(v.dtype), kind="ExternalInput").ap() for k, v in arrays.items()}
    t["outT"] = nc.dram_tensor("outT", (D, N), F32, kind="ExternalOutput").ap()
    build(nc, t)
    r = run_bass_kernel_spmd(nc, [{"in_" + k: v for k, v in arrays.items()}], core_ids=[0])
    return np.ascontiguousarray(r.results[0]["outT"].T).reshape(B, S, D)
```

```python
from contextlib import ExitStack

import concourse.bass as bass
from concourse import mybir

ALU = mybir.AluOpType
ACT = mybir.ActivationFunctionType
F32 = mybir.dt.float32
I32 = mybir.dt.int32
BF16 = mybir.dt.bfloat16
F32R = mybir.dt.float32r
AX_X = mybir.AxisListType.X

P = 128
B = 64
S = 64
D = 128
N = B * S
W = 512
CHUNKS = N // W
BC = W // S
INNER = 256
TAPS = 4
H = 16
DH = D // H
EPS = 1e-5
LN_EXP_SET = 6


def stage_semaphore(nc, g, name):
    g["sems"].append(nc.alloc_semaphore(name))
    return g["sems"][-1]


def end_stage(nc, g):
    nc.clear_and_free_semaphores(g["sems"])
    g["sems"].clear()
    nc.all_engine_barrier()


def load_ln_exp(nc, act):
    act.add_instruction(mybir.InstLoadActFuncSet(
        name=nc.get_next_instruction_name(), engine=mybir.EngineType.Activation,
        act_func_set_id=LN_EXP_SET, ins=[], outs=[]))


class Norm:

    def __init__(self, nc, sb, sem, X, ones, eps, mean_ps, var_ps, y_ready, y_ps, per=1, buffers=None):
        self.nc, self.X, self.ones, self.eps = nc, X, ones, eps
        self.mean_ps, self.var_ps, self.y_ps, self.y_ready = mean_ps, var_ps, y_ps, y_ready
        self.per = per
        self.resid, self.rstd = buffers or (sb("resid", [P, W])[:], sb("rstd", [P, W])[:])
        self.centred = self.resid
        self.squares = self.rstd
        self.resid_ready = sem("resid_ready")
        self.mean_ready = sem("mean_ready")
        self.centred_ready = sem("centred_ready")
        self.squares_ready = sem("squares_ready")
        self.var_ready = sem("var_ready")
        self.logvar_ready = sem("logvar_ready")
        self.rstd_ready = sem("rstd_ready")
        self.x_ready = sem("x_ready")

    def chunk(self, i):
        return self.X[:, bass.ds(i * W, W)]

    def like(self, buf, x):
        return buf if len(x.shape) == 2 else buf.rearrange("p (a b) -> p a b", b=x.shape[2])

    def add(self, dve, i, bias=None, x=None, y=None):
        x = self.chunk(i) if x is None else x
        y = self.y_ps if y is None else y
        dve.wait_ge(self.y_ready, i * self.per + self.per)
        if bias is None:
            dve.tensor_tensor(self.like(self.resid, x), y, x, ALU.add).then_inc(self.resid_ready, 1)
        else:
            dve.scalar_tensor_tensor(self.like(self.resid, x), y, bias, x, ALU.add, ALU.add).then_inc(self.resid_ready, 1)

    def centre(self, dve, i):
        dve.wait_ge(self.mean_ready, i + 1)
        dve.tensor_tensor(self.centred, self.resid, self.mean_ps, ALU.subtract).then_inc(self.centred_ready, 1)

    def scale(self, dve, i, x=None):
        x = self.chunk(i) if x is None else x
        dve.wait_ge(self.rstd_ready, i + 1)
        dve.tensor_tensor(x, self.like(self.centred, x), self.like(self.rstd, x), ALU.mult).then_inc(self.x_ready, 1)

    def vector(self, dve, i, bias=None, x=None, y=None):
        self.add(dve, i, bias, x, y)
        self.centre(dve, i)
        self.scale(dve, i, x)

    def mean(self, pe, i):
        pe.wait_ge(self.resid_ready, i + 1)
        pe.matmul(self.mean_ps, self.ones[:], self.resid, start=True, stop=True).then_inc(self.mean_ready, 1)

    def variance(self, pe, i):
        pe.wait_ge(self.squares_ready, i + 1)
        pe.matmul(self.var_ps, self.ones[:], self.squares, start=True, stop=True).then_inc(self.var_ready, 1)

    def tensor(self, pe, i):
        self.mean(pe, i)
        self.variance(pe, i)

    def square(self, act, i):
        act.wait_ge(self.centred_ready, i + 1)
        act.activation(self.squares, self.centred, ACT.Square).then_inc(self.squares_ready, 1)

    def root(self, act, i):
        act.wait_ge(self.var_ready, i + 1)
        act.activation(self.rstd, self.var_ps, ACT.Ln, bias=self.eps[:, 0:1]).then_inc(self.logvar_ready, 1)
        act.wait_ge(self.logvar_ready, i + 1)
        act.activation(self.rstd, self.rstd, ACT.Exp, scale=-0.5).then_inc(self.rstd_ready, 1)

    def scalar(self, act, i, load=True):
        self.square(act, i)
        if load:
            load_ln_exp(self.nc, act)
        self.root(act, i)


def conv_mlp_stage(nc, g, tag, w):
    X, ones, eps = g["X"], g["ones"], g["eps"]
    with ExitStack() as ctx:
        def sb(name, shape):
            return ctx.enter_context(nc.sbuf_tensor(tag + name, shape, F32))

        def ps(name, shape=(P, W)):
            return ctx.enter_context(nc.psum_tensor(tag + name, list(shape), F32))

        def sem(name):
            return stage_semaphore(nc, g, tag + name)

        w_in = sb("w_in", [P, 2 * INNER])
        w_conv = sb("w_conv", [P, 2, TAPS, P])
        cols = sb("cols", [P, 9])
        w_fc = sb("w_fc", [P, 2, D])
        w_cproj = sb("w_cproj", [P, INNER])
        w_out = sb("w_out", [P, 2, D])
        ones_inner = sb("ones_inner", [P, P])
        hpad = sb("hpad", [P, 2, BC, S + TAPS - 1])
        gate = sb("gate", [P, 2, W])
        h = sb("h", [P, 2, W])
        c = sb("c", [P, 2, W])
        sq = sb("sq", [P, 2, W])
        rs = sb("rs", [P, W])
        hn = sb("hn", [P, 2, W])
        s_fc = sb("s_fc", [P, W])
        h2 = sb("h2", [P, 2, W])
        h_ps = ps("h_ps", (P, 2, W))
        g_ps = ps("g_ps", (P, 2, W))
        fc_ps = ps("fc_ps")
        var_ps = ps("var_ps")
        cproj_ps = ps("cproj_ps", (P, 2, W))
        mean_ps, norm_var_ps, out_ps = fc_ps, cproj_ps[:, 0], cproj_ps[:, 1]

        weights = sem("weights")
        x_loaded = sem("x_loaded")
        consts = sem("consts")
        proj_h = sem("proj_h")
        proj_g = sem("proj_g")
        h_copied = sem("h_copied")
        gated = sem("gated")
        conv = sem("conv")
        h_ready = sem("h_ready")
        hmean = sem("hmean")
        c_ready = sem("c_ready")
        sq_ready = sem("sq_ready")
        hvar = sem("hvar")
        log_ready = sem("log_ready")
        rs_ready = sem("rs_ready")
        cn_ready = sem("cn_ready")
        hn_ready = sem("hn_ready")
        fc_ready = sem("fc_ready")
        fc_silu = sem("fc_silu")
        cproj = sem("cproj")
        h2_ready = sem("h2_ready")
        y_ready = sem("y_ready")
        norm = Norm(nc, sb, sem, X, ones, eps, var_ps[:], norm_var_ps, y_ready, out_ps)
        LOADS = 6
        block = ctx.enter_context(nc.Block())

        LAST = CHUNKS - 1

        def chunks(engine, body):
            body(0, False, True)
            with engine.Fori(0, CHUNKS - 2) as i:
                body(i + 1, True, True)
            body(LAST, True, False)

        @block.sync
        def _(sp):
            for dst, name in ((w_in, "in"), (w_conv, "conv"), (cols, "cols"), (w_fc, "fc"),
                              (w_cproj, "cproj"), (w_out, "out")):
                sp.dma_start(dst[:], w[name]).then_inc(weights, 16)
            sp.dma_start(X[:, W:], w["xT"][:, W:]).then_inc(x_loaded, 16)

        @block.gpsimd
        def _(pool):
            pool.memset(ones_inner[:], 1.0 / INNER).then_inc(consts, 1)
            pool.memset(hpad[:], 0.0).then_inc(consts, 1)

        @block.tensor
        def _(pe):
            pe.wait_ge(weights, 16 * LOADS)
            pe.wait_ge(consts, 2)

            def project_h(n):
                for m in range(2):
                    pe.matmul(h_ps[:, m], w_in[:, m * P:(m + 1) * P], X[:, bass.ds(n * W, W)], start=True, stop=True).then_inc(proj_h, 1)

            def project_gate(n):
                for m in range(2):
                    pe.matmul(g_ps[:, m], w_in[:, INNER + m * P:INNER + (m + 1) * P], X[:, bass.ds(n * W, W)],
                              start=True, stop=True).then_inc(proj_g, 1)

            def convolve(n, m):
                pe.wait_ge(h_copied, n * 2 + 2)
                for k in range(TAPS):
                    mm = pe.matmul(h_ps[:, m], w_conv[:, m, k], hpad[:, m, :, k:k + S],
                                   start=(k == 0), stop=(k == TAPS - 1))
                mm.then_inc(conv, 1)

            def both(bank, lhs, rhs, done):
                pe.matmul(bank, lhs[0], rhs[:, 0], start=True, stop=False)
                pe.matmul(bank, lhs[1], rhs[:, 1], start=False, stop=True).then_inc(done, 1)

            def body(n, earlier, later):
                pe.wait_ge(h_ready, n * 2 + 2)
                both(mean_ps[:], (ones_inner[:], ones_inner[:]), h, hmean)
                if earlier:
                    norm.mean(pe, n - 1)
                if later:
                    project_h(n + 1)
                if earlier:
                    norm.variance(pe, n - 1)
                pe.wait_ge(sq_ready, n + 1)
                both(var_ps[:], (ones_inner[:], ones_inner[:]), sq, hvar)
                if later:
                    project_gate(n + 1)
                    convolve(n + 1, 0)
                pe.wait_ge(hn_ready, n * 2 + 2)
                both(fc_ps[:], (w_fc[:, 0], w_fc[:, 1]), hn, fc_ready)
                if later:
                    convolve(n + 1, 1)
                pe.wait_ge(fc_silu, n + 1)
                if earlier:
                    pe.wait_ge(norm.logvar_ready, n)
                for m in range(2):
                    pe.matmul(cproj_ps[:, m], w_cproj[:, m * P:(m + 1) * P], s_fc[:], start=True, stop=True).then_inc(cproj, 1)
                pe.wait_ge(h2_ready, n * 2 + 2)
                both(out_ps, (w_out[:, 0], w_out[:, 1]), h2, y_ready)

            project_h(0)
            project_gate(0)
            convolve(0, 0)
            convolve(0, 1)
            pe.wait_ge(x_loaded, 16)
            chunks(pe, body)
            norm.tensor(pe, LAST)

        @block.scalar
        def _(act):
            act.wait_ge(weights, 16 * LOADS)
            act.wait_ge(consts, 2)

            def pad(n):
                for m in range(2):
                    act.wait_ge(proj_h, n * 2 + 1 + m)
                    act.copy(hpad[:, m, :, TAPS - 1:], h_ps[:, m].rearrange("p (b s) -> p b s", s=S)).then_inc(h_copied, 1)

            def gates(n):
                for m in range(2):
                    act.wait_ge(proj_g, n * 2 + 1 + m)
                    act.activation(gate[:, m], g_ps[:, m], ACT.Silu).then_inc(gated, 1)

            def body(n, earlier, later):
                act.wait_ge(c_ready, n + 1)
                act.activation(sq[:], c[:], ACT.Square).then_inc(sq_ready, 1)
                if earlier:
                    norm.square(act, n - 1)
                if later:
                    pad(n + 1)
                load_ln_exp(nc, act)
                if earlier:
                    norm.root(act, n - 1)
                act.wait_ge(hvar, n + 1)
                act.activation(rs[:], var_ps[:], ACT.Ln, bias=eps[:, 0:1]).then_inc(log_ready, 1)
                act.wait_ge(log_ready, n + 1)
                act.activation(rs[:], rs[:], ACT.Exp, scale=-0.5).then_inc(rs_ready, 1)
                act.wait_ge(cn_ready, n + 1)
                for m in range(2):
                    act.activation(hn[:, m], sq[:, m], ACT.Identity, scale=cols[:, 2 + m:3 + m],
                                   bias=cols[:, 4 + m:5 + m]).then_inc(hn_ready, 1)
                if later:
                    gates(n + 1)
                act.wait_ge(fc_ready, n + 1)
                act.activation(s_fc[:], fc_ps[:], ACT.Silu, bias=cols[:, 8:9]).then_inc(fc_silu, 1)

            pad(0)
            gates(0)
            chunks(act, body)
            norm.scalar(act, LAST)

        @block.vector
        def _(dve):
            dve.wait_ge(weights, 16 * LOADS)

            def gated_channels(n):
                for m in range(2):
                    dve.wait_ge(gated, n * 2 + 1 + m)
                    dve.wait_ge(conv, n * 2 + 1 + m)
                    dve.scalar_tensor_tensor(h[:, m], h_ps[:, m], cols[:, m:m + 1], gate[:, m],
                                             ALU.add, ALU.mult).then_inc(h_ready, 1)

            def body(n, earlier, later):
                dve.wait_ge(hmean, n + 1)
                dve.wait_ge(h_ready, n * 2 + 2)
                dve.tensor_tensor(c[:], h[:], mean_ps[:, None, :].to_broadcast([P, 2, W]), ALU.subtract).then_inc(c_ready, 1)
                if earlier:
                    norm.centre(dve, n - 1)
                    norm.scale(dve, n - 1)
                dve.wait_ge(rs_ready, n + 1)
                dve.wait_ge(hvar, n + 1)
                dve.tensor_tensor(sq[:], c[:], rs[:, None, :].to_broadcast([P, 2, W]), ALU.mult).then_inc(cn_ready, 1)
                for m in range(2):
                    dve.wait_ge(cproj, n * 2 + 1 + m)
                    dve.scalar_tensor_tensor(h2[:, m], cproj_ps[:, m], cols[:, 6 + m:7 + m], h[:, m],
                                             ALU.add, ALU.add).then_inc(h2_ready, 1)
                if later:
                    dve.wait_ge(h2_ready, n * 2 + 2)
                    gated_channels(n + 1)
                norm.add(dve, n)

            gated_channels(0)
            chunks(dve, body)
            norm.centre(dve, LAST)
            norm.scale(dve, LAST)


def attention_stage(nc, g, tag, w, masked):
    X, ones, eps, ident = g["X"], g["ones"], g["eps"], g["ident"]
    with ExitStack() as ctx:
        def sb(name, shape, dt=F32):
            return ctx.enter_context(nc.sbuf_tensor(tag + name, shape, dt))

        def ps(name, shape=(P, W)):
            return ctx.enter_context(nc.psum_tensor(tag + name, list(shape), F32))

        def sem(name):
            return stage_semaphore(nc, g, tag + name)

        w_qkvo = sb("w_qkvo", [P, 4, D])
        own = sb("own", [P, H])
        bias = sb("bias", [P, 4])
        C = sb("C", [P, 2, W])
        K = sb("K", [P, 2, BC, S])
        Kbd = sb("Kbd", [P, 2, BC, H, S])
        Q = sb("Q", [P, 2, W])
        Vbd = sb("Vbd", [P, 2, BC, H // 2, 2, DH])
        E = sb("E", [P, 2, H, S])
        PT = sb("PT", [P, H // 2, P])
        top = sb("top", [P, 2, H])
        total = sb("total", [P, 2, H])
        share = sb("share", [P, 2, H])
        O = sb("O", [P, 2, D])
        OT = sb("OT", [P, W])
        if masked:
            mask_i = sb("mask_i", [S, S], I32)
            drop = sb("drop", [S, 8, S], BF16)
            pick = sb("pick", [S, S], BF16)

        s_ps = ps("s_ps", (P, 2, W))
        t_ps = ps("t_ps", (P, 2, W))
        o_ps = ps("o_ps")
        ot_ps = ps("ot_ps")
        z0 = ps("z0")
        z1 = ps("z1")

        weights, zeroed = sem("weights"), sem("zeroed")
        c_loaded = [sem("c_loaded0"), sem("c_loaded1")]
        k_ready, q_ready = sem("k_ready"), sem("q_ready")
        k_copied, q_copied = sem("k_copied"), sem("q_copied")
        v_ready = [sem("v0_ready"), sem("v1_ready")]
        v_copied = [sem("v0_copied"), sem("v1_copied")]
        k_spread = [sem("k_spread0"), sem("k_spread1")]
        s_ready, top_ready, e_ready, exp_ready = sem("s_ready"), sem("top_ready"), sem("e_ready"), sem("exp_ready")
        mask_ready = sem("mask_ready")
        own_ready, first_spread = sem("own_ready"), sem("first_spread")
        total_ready, share_ready = sem("total_ready"), sem("share_ready")
        pt_ready, pt_copied = sem("pt_ready"), sem("pt_copied")
        o_ready, o_scaled, ot_ready, ot_copied = sem("o_ready"), sem("o_scaled"), sem("ot_ready"), sem("ot_copied")
        y_ready = sem("y_ready")
        norm = Norm(nc, sb, sem, X, ones, eps, z1[:], z0[:], y_ready, z0[:])
        block = ctx.enter_context(nc.Block())
        LOADS = 3 if masked else 2
        PAIRS = BC // 2
        LAST = CHUNKS - 1

        def chunks(engine, body):
            body(0, 0)
            body(1, 1)
            with engine.Fori(0, (CHUNKS - 4) // 2) as j:
                body(j * 2 + 2, 0)
                body(j * 2 + 3, 1)
            body(LAST - 1, 0)
            body(LAST, 1)

        def inside(n, ahead):
            return not isinstance(n, int) or 0 <= n + ahead < CHUNKS

        def loads(n, u):
            return n * 8 + (8 if u else 16)

        @block.sync
        def _(sp):
            sp.dma_start(w_qkvo[:], w["qkvo"]).then_inc(weights, 16)
            sp.dma_start(bias[:], w["bias"]).then_inc(weights, 16)
            if masked:
                sp.dma_start(mask_i[:], w["mask"]).then_inc(weights, 16)
            for u in range(2):
                sp.dma_start(C[:, u], w["ctxT"][:, u * W:(u + 1) * W]).then_inc(c_loaded[u], 16)

            def spread(n, u):
                sp.wait_ge(k_copied, n + 1)
                for h in range(H):
                    sp.dma_start(Kbd[h * DH:(h + 1) * DH, u, :, h, :], K[h * DH:(h + 1) * DH, u]).then_inc(k_spread[u], 16)

            sp.wait_ge(zeroed, 2)
            spread(1, 1)

            def reload(n, u):
                sp.wait_ge(v_ready[1], n + 1)
                sp.dma_start(C[:, u], w["ctxT"][:, bass.ds(n * W + 2 * W, W)]).then_inc(c_loaded[u], 16)
                spread(n + 2, u)

            with sp.Fori(0, (CHUNKS - 2) // 2) as j:
                for u in range(2):
                    reload(j * 2 + u, u)

        @block.gpsimd
        def _(pool):
            pool.memset(Kbd[:, 1], 0.0).then_inc(zeroed, 1)
            pool.memset(Vbd[:], 0.0).then_inc(zeroed, 1)

        @block.tensor
        def _(pe):
            def project_k(n, u):
                pe.wait_ge(c_loaded[u], loads(n, u))
                pe.matmul(z1[:], w_qkvo[:, 1], C[:, u], start=True, stop=True).then_inc(k_ready, 1)

            def project_q(n):
                pe.matmul(z1[:], w_qkvo[:, 0], X[:, bass.ds(n * W, W)], start=True, stop=True).then_inc(q_ready, 1)

            def project_v(half, bank, u):
                for b in range(4):
                    at = (half * 4 + b) * S
                    for h2 in range(2):
                        mm = pe.matmul(bank[h2 * S:(h2 + 1) * S, b * P:(b + 1) * P], C[:, u, at:at + S],
                                       w_qkvo[:, 2], start=True, stop=True)
                mm.then_inc(v_ready[half], 1)

            def scores(u, pr, n):
                if pr == 0:
                    pe.wait_ge(q_copied, n + 1)
                    if inside(n, -1):
                        pe.wait_ge(k_spread[u], (loads(n, u) - (0 if u else 16)) * H)
                if not inside(n, -1):
                    pe.wait_ge(first_spread, pr + 1)
                if inside(n, -1) or pr:
                    pe.wait_ge(e_ready, n * PAIRS + pr)
                for half in range(2):
                    for b in range(2):
                        out = s_ps[b * S:(b + 1) * S, half]
                        mm = pe.matmul(out, Q[:, u, (2 * pr + b) * S:(2 * pr + b + 1) * S],
                                       Kbd[:, u, 2 * pr + b, half * 8:half * 8 + 8, :], start=True, stop=not masked)
                if masked:
                    for half in range(2):
                        for b in range(2):
                            mm = pe.matmul(s_ps[b * S:(b + 1) * S, half], pick[:], drop[:], start=False, stop=True)
                mm.then_inc(s_ready, 1)

            def transposes(pr, n):
                pe.wait_ge(exp_ready, n * PAIRS + pr + 1)
                if inside(n, -1) or pr:
                    pe.wait_ge(pt_copied, (n * PAIRS + pr) * 2)
                for half in range(2):
                    for c in range(4):
                        mm = pe.transpose(t_ps[:, half, c * P:(c + 1) * P],
                                          E[:, pr % 2, half * 8 + 2 * c:half * 8 + 2 * c + 2, :], ident[:])
                    mm.then_inc(pt_ready, 1)

            def weigh(pr, n, u):
                pe.wait_ge(pt_copied, (n * PAIRS + pr) * 2 + 2)
                if inside(n, -1) or pr:
                    pe.wait_ge(o_scaled, n * PAIRS + pr)
                for hp in range(H // 2):
                    for b in range(2):
                        mm = pe.matmul(o_ps[b * S:(b + 1) * S, hp * 16:hp * 16 + 16], PT[:, hp, b * S:(b + 1) * S],
                                       Vbd[:, u, 2 * pr + b, hp], start=True, stop=True)
                mm.then_inc(o_ready, 1)

            def turn(pr, n):
                pe.wait_ge(o_scaled, n * PAIRS + pr + 1)
                pe.transpose(ot_ps[:, pr * P:(pr + 1) * P], O[:, pr % 2], ident[:]).then_inc(ot_ready, 1)

            def project_o(n):
                pe.wait_ge(ot_copied, n + 1)
                pe.matmul(z0[:], w_qkvo[:, 3], OT[:], start=True, stop=True).then_inc(y_ready, 1)

            def beside(pr, n, u):
                if pr == 0:
                    if inside(n, -2):
                        pe.wait_ge(norm.logvar_ready, n - 1)
                    project_v(1, z0, u)
                    if inside(n, 1):
                        pe.wait_ge(k_copied, n + 2)
                        project_q(n + 1)
                if pr == 1:
                    if inside(n, -1):
                        pe.wait_ge(v_copied[1], n * 2 + 2)
                        project_o(n - 1)
                    if inside(n, 1):
                        pe.wait_ge(q_copied, n + 2)
                        project_v(0, z1, 1 - u)
                if pr == 2 and inside(n, -1):
                    if inside(n, 1):
                        pe.wait_ge(v_copied[0], n * 2 + 4)
                    norm.mean(pe, n - 1)
                if pr == 3:
                    if inside(n, -1):
                        norm.variance(pe, n - 1)
                    elif inside(n, 2):
                        pe.wait_ge(v_copied[0], n * 2 + 4)
                    if inside(n, 2):
                        project_k(n + 2, u)

            def body(n, u):
                for pr in range(PAIRS):
                    transposes(pr, n)
                    if pr < PAIRS - 2:
                        scores(u, pr + 2, n)
                    elif inside(n, 1):
                        scores(1 - u, pr + 2 - PAIRS, n + 1)
                    beside(pr, n, u)
                    if pr:
                        turn(pr - 1, n)
                    elif inside(n, -1):
                        turn(PAIRS - 1, n - 1)
                    weigh(pr, n, u)

            pe.wait_ge(weights, 16 * LOADS)
            if masked:
                pe.wait_ge(mask_ready, 2)
            project_k(0, 0)
            pe.wait_ge(k_copied, 1)
            project_q(0)
            pe.wait_ge(q_copied, 1)
            project_k(1, 1)
            pe.wait_ge(k_copied, 2)
            project_v(0, z1, 0)
            pe.wait_ge(v_copied[0], 2)
            scores(0, 0, 0)
            scores(0, 1, 0)
            chunks(pe, body)
            turn(PAIRS - 1, LAST)
            project_o(LAST)
            norm.mean(pe, LAST)
            norm.variance(pe, LAST)

        @block.scalar
        def _(act):
            def copy_k(n, u):
                act.wait_ge(k_ready, n + 1)
                act.activation(K[:, u], z1[:].rearrange("p (b s) -> p b s", s=S), ACT.Identity, bias=bias[:, 1:2]).then_inc(k_copied, 1)

            def copy_q(n, u):
                act.wait_ge(q_ready, n + 1)
                act.activation(Q[:, u], z1[:], ACT.Identity, bias=bias[:, 0:1]).then_inc(q_copied, 1)

            def copy_v(half, bank, n, u):
                act.wait_ge(v_ready[half], n + 1)
                for h2 in range(2):
                    rows = slice(h2 * S, (h2 + 1) * S)
                    v = bank[rows, :].rearrange("p (b c k d) -> p b c k d", b=4, k=2, d=DH)[:, :, :, h2, :]
                    act.copy(Vbd[rows, u, half * 4:half * 4 + 4, :, h2, :], v).then_inc(v_copied[half], 1)

            def copy_o(n):
                act.wait_ge(ot_ready, n * PAIRS + PAIRS)
                if inside(n, -1):
                    act.wait_ge(y_ready, n)
                act.activation(OT[:], ot_ps[:], ACT.Identity, bias=bias[:, 2:3]).then_inc(ot_copied, 1)

            def exponentials(pr, n):
                act.wait_ge(e_ready, n * PAIRS + pr + 1)
                act.activation(E[:, pr % 2], E[:, pr % 2], ACT.Exp, scale=DH ** -0.5).then_inc(exp_ready, 1)

            def beside(pr, n, u):
                if pr == 0:
                    copy_v(1, z0, n, u)
                    if inside(n, 1):
                        copy_q(n + 1, 1 - u)
                    if inside(n, -1):
                        copy_o(n - 1)
                if pr == 1 and inside(n, 1):
                    copy_v(0, z1, n + 1, 1 - u)
                if pr == 2 and inside(n, -1):
                    norm.square(act, n - 1)
                if pr == 3:
                    if inside(n, -1):
                        norm.root(act, n - 1)
                    if inside(n, 2):
                        copy_k(n + 2, u)

            def body(n, u):
                for pr in range(PAIRS):
                    pair = n * PAIRS + pr
                    for half in range(2):
                        act.wait_ge(pt_ready, pair * 2 + half + 1)
                        if half == 0 and (inside(n, -1) or pr):
                            act.wait_ge(o_ready, pair)
                        act.copy(PT[:, half * 4:half * 4 + 4], t_ps[:, half].rearrange("p (c q) -> p c q", q=P)).then_inc(pt_copied, 1)
                    if pr < PAIRS - 2:
                        exponentials(pr + 2, n)
                    elif inside(n, 1):
                        exponentials(pr + 2 - PAIRS, n + 1)
                    beside(pr, n, u)

            load_ln_exp(nc, act)
            act.wait_ge(weights, 16 * LOADS)
            copy_k(0, 0)
            copy_q(0, 0)
            copy_k(1, 1)
            act.wait_ge(zeroed, 2)
            copy_v(0, z1, 0, 0)
            exponentials(0, 0)
            exponentials(1, 0)
            chunks(act, body)
            copy_o(LAST)
            norm.square(act, LAST)
            norm.root(act, LAST)

        @block.vector
        def _(dve):
            dve.tensor_reduce(own[:], ident[:].rearrange("p (h d) -> p h d", d=DH), AX_X, ALU.add).then_inc(own_ready, 1)
            dve.wait_ge(weights, 16 * LOADS)
            if masked:
                dve.tensor_scalar(drop[:], mask_i[:, None, :].to_broadcast([S, 8, S]), 0, -2.0 ** 60, ALU.is_equal,
                                  ALU.mult).then_inc(mask_ready, 1)
                dve.tensor_copy(pick[:], ident[0:S, 0:S]).then_inc(mask_ready, 1)

            def shift(pr, n):
                pair, e = n * PAIRS + pr, pr % 2
                s = s_ps[:].rearrange("p a (h s) -> p (a h) s", s=S)
                dve.wait_ge(s_ready, pair + 1)
                dve.tensor_reduce(top[:, e], s, AX_X, ALU.max).then_inc(top_ready, 1)
                dve.wait_ge(top_ready, pair + 1)
                dve.tensor_tensor(E[:, e], s, top[:, e, :, None].to_broadcast([P, H, S]), ALU.subtract).then_inc(e_ready, 1)

            def sums(pr, n):
                pair, e = n * PAIRS + pr, pr % 2
                dve.wait_ge(exp_ready, pair + 1)
                dve.tensor_reduce(total[:, e], E[:, e], AX_X, ALU.add).then_inc(total_ready, 1)
                dve.wait_ge(total_ready, pair + 1)
                dve.reciprocal(share[:, e], total[:, e]).then_inc(share_ready, 1)

            def scale(pr, n):
                pair, e = n * PAIRS + pr, pr % 2
                dve.wait_ge(o_ready, pair + 1)
                dve.wait_ge(share_ready, pair + 1)
                dve.tensor_tensor(O[:, e].rearrange("p (h d) -> p h d", d=DH),
                                  o_ps[:, 0:D].rearrange("p (h d) -> p h d", d=DH),
                                  share[:, e, :, None].to_broadcast([P, H, DH]), ALU.mult).then_inc(o_scaled, 1)

            def body(n, u):
                for pr in range(PAIRS):
                    sums(pr, n)
                    if pr < PAIRS - 2:
                        shift(pr + 2, n)
                    elif inside(n, 1):
                        shift(pr + 2 - PAIRS, n + 1)
                    scale(pr, n)
                    if pr == 0 and inside(n, -2):
                        norm.scale(dve, n - 2)
                    if pr == 1 and inside(n, -1):
                        norm.add(dve, n - 1, bias[:, 3:4])
                    if pr == 2 and inside(n, -1):
                        norm.centre(dve, n - 1)

            def spread_first(pr):
                kb = Kbd[:, 0, 2 * pr:2 * pr + 2]
                dve.tensor_tensor(kb, K[:, 0, 2 * pr:2 * pr + 2, None, :].to_broadcast([P, 2, H, S]),
                                  own[:, None, :, None].to_broadcast([P, 2, H, S]), ALU.mult).then_inc(first_spread, 1)

            dve.wait_ge(own_ready, 1)
            dve.wait_ge(k_copied, 1)
            spread_first(0)
            spread_first(1)
            shift(0, 0)
            spread_first(2)
            shift(1, 0)
            spread_first(3)
            chunks(dve, body)
            norm.scale(dve, LAST - 1)
            dve.wait_ge(norm.x_ready, LAST)
            norm.add(dve, LAST, bias[:, 3:4])
            norm.centre(dve, LAST)
            norm.scale(dve, LAST)


class Experts:

    def __init__(self, nc, sb, ps, sem, g, count, biased, other_ps):
        self.nc, self.g, self.count, self.biased = nc, g, count, biased
        self.raw = sb("raw", [P, 2, count * INNER])
        self.w = {name: (sb("wl_" + name, [P, count, INNER], F32R), sb("wh_" + name, [P, count, INNER], F32R))
                  for name in ("gate", "up", "down")}
        self.x = (sb("x_low", [P, N], F32R), sb("x_high", [P, N], F32R))
        self.share = sb("share", [64, N], F32R)
        self.pick = sb("pick", [64, count, P], F32R)
        self.a = sb("a", [P, 2, W])
        self.products = sb("products", [P, 2, 2, W])
        self.h = self.products[:, 0]
        self.hs = self.products[:, 1]
        self.hs_high = sb("hs_high", [P, 2, 2, W], F32R)
        self.hs_low = sb("hs_low", [P, 2, 2, W], F32R)
        self.gate_ps = ps("gate_ps", (P, 2, W))
        self.up_ps = ps("up_ps", (P, 2, W))
        self.share_ps = ps("share_ps")[:], other_ps
        self.y_ps = ps("y_ps")
        self.raw_loaded = sem("raw0_loaded"), sem("raw1_loaded")
        self.high_ready, self.low_ready = sem("high_ready"), sem("low_ready")
        self.share_filled, self.share_high, self.share_low = sem("share_filled"), sem("share_high"), sem("share_low")
        self.gate_ready, self.up_ready, self.spread_ready = sem("gate_ready"), sem("up_ready"), sem("spread_ready")
        self.silu_ready, self.h_ready, self.hs_ready = sem("silu_ready"), sem("h_ready"), sem("hs_ready")
        self.hs_high_ready, self.hs_low_ready = sem("hs_high_ready"), (sem("hs_low0_ready"), sem("hs_low1_ready"))
        self.down_ready, self.y_ready = sem("down_ready"), sem("y_ready")
        if biased:
            self.b_gate = sb("b_gate", [P, count, 2])
            self.b_up = sb("b_up", [P, count, 2])
            self.biases_loaded = sem("biases_loaded")
            self.b_down = (sb("bl_down", [64, D], F32R), sb("bh_down", [64, D], F32R))

    def loads(self):
        weights = [(name, P, self.count * INNER) + tuple(x[:].rearrange("p e i -> p (e i)") for x in self.w[name])
                   for name in ("gate", "up", "down")]
        biases = [("b_down", 64, D, self.b_down[0][:], self.b_down[1][:])] if self.biased else []
        return [("pick", 64, self.count * P, None, self.pick[:].rearrange("p e i -> p (e i)"))] + weights + biases

    def load(self, sp, w):
        if self.biased:
            for dst, name in ((self.b_gate, "b_gate"), (self.b_up, "b_up")):
                sp.dma_start(dst[:], w[name]).then_inc(self.biases_loaded, 16)
        for n, (name, rows, columns, low, high) in enumerate(self.loads()):
            if n == 2:
                sp.wait_ge(self.high_ready, 2)
            if n > 2:
                sp.wait_ge(self.low_ready, n - 1)
            sp.dma_start(self.raw[0:rows, n % 2, 0:columns], w[name]).then_inc(self.raw_loaded[n % 2], 16)

    def split_high(self, act):
        act.copy(self.x[1][:], self.g["X"][:]).then_inc(self.high_ready, 1)
        for n, (name, rows, columns, low, high) in enumerate(self.loads()):
            act.wait_ge(self.raw_loaded[n % 2], 16 * (n // 2 + 1))
            act.copy(high, self.raw[0:rows, n % 2, 0:columns]).then_inc(self.high_ready, 1)
        if self.biased:
            act.wait_ge(self.biases_loaded, 32)

    def split_low(self, pool):
        pool.tensor_scalar(self.share[:].rearrange("p (a b) -> p a b", b=P), self.g["ident"][0:64, None, :].to_broadcast([64, N // P, P]),
                           0.0, None, ALU.mult).then_inc(self.share_filled, 1)
        pool.wait_ge(self.high_ready, 1)
        pool.tensor_tensor(self.x[0][:], self.g["X"][:], self.x[1][:].bitcast(F32), ALU.subtract).then_inc(self.low_ready, 1)
        for n, (name, rows, columns, low, high) in enumerate(self.loads()):
            if n:
                pool.wait_ge(self.high_ready, n + 2)
                pool.tensor_tensor(low, self.raw[0:rows, n % 2, 0:columns], high.bitcast(F32), ALU.subtract).then_inc(self.low_ready, 1)

    def wait(self, engine, semaphore, value):
        if not isinstance(value, int) or value > 0:
            engine.wait_ge(semaphore, value)

    def product(self, pe, out, weight, value):
        pe.matmul(out, weight[0], value[1], start=True, stop=False)
        pe.matmul(out, weight[1], value[0], start=False, stop=False)
        return pe.matmul(out, weight[1], value[1], start=False, stop=True)

    def weight(self, name, e, m):
        low, high = self.w[name]
        return low[:, e, m * P:(m + 1) * P], high[:, e, m * P:(m + 1) * P]

    def down(self, pe, n, k, e):
        if e == 0 and self.biased:
            chunk = self.share[:, bass.ds(n * W, W)]
            pe.matmul(self.y_ps[:], self.b_down[0][:], chunk, start=True, stop=False)
            pe.matmul(self.y_ps[:], self.b_down[1][:], chunk, start=False, stop=False)
        for m in range(2):
            pe.wait_ge(self.hs_high_ready, k * 2 + m + 1)
            for part, weight in enumerate(self.weight("down", e, m)):
                pe.matmul(self.y_ps[:], weight, self.hs_high[:, e % 2, m],
                          start=(e == 0 and m == 0 and part == 0 and not self.biased), stop=False)
        for m in range(2):
            pe.wait_ge(self.hs_low_ready[m], k + 1)
            mm = pe.matmul(self.y_ps[:], self.weight("down", e, m)[1], self.hs_low[:, e % 2, m], start=False,
                           stop=(e == self.count - 1 and m == 1))
        mm.then_inc(self.down_ready, 1)

    def tensor(self, pe, n, norm):
        earlier = not isinstance(n, int) or n > 0
        tok = bass.ds(n * W, W)
        x = self.x[0][:, tok], self.x[1][:, tok]
        for e in range(self.count):
            k = n * self.count + e
            pe.matmul(self.share_ps[e % 2], self.pick[:, e], self.share[:, tok], start=True, stop=True).then_inc(self.spread_ready, 1)
            self.wait(pe, self.silu_ready, k * 2)
            for m in range(2):
                self.product(pe, self.gate_ps[:, m], self.weight("gate", e, m), x).then_inc(self.gate_ready, 1)
            if earlier and e == 3:
                norm.variance(pe, n - 1)
            self.wait(pe, self.h_ready, k * 2)
            for m in range(2):
                self.product(pe, self.up_ps[:, m], self.weight("up", e, m), x).then_inc(self.up_ready, 1)
            if earlier and e == 1:
                norm.mean(pe, n - 1)
            if e:
                self.down(pe, n, k - 1, e - 1)
            elif earlier:
                self.down(pe, n - 1, k - 1, self.count - 1)

    def scalar(self, act, n, norm):
        earlier = not isinstance(n, int) or n > 0
        for e in range(self.count):
            k = n * self.count + e
            for m in range(2):
                act.wait_ge(self.gate_ready, k * 2 + m + 1)
                self.wait(act, self.h_ready, k * 2 + m - 1)
                bias = {"bias": self.b_gate[:, e, m:m + 1]} if self.biased else {}
                act.activation(self.a[:, m], self.gate_ps[:, m], ACT.Silu, **bias).then_inc(self.silu_ready, 1)
                if m == 0 and (e or earlier):
                    self.high(act, k - 1, (e - 1) % self.count, 1)
            if earlier and e == 2:
                norm.square(act, n - 1)
            if earlier and e == 3:
                load_ln_exp(self.nc, act)
                norm.root(act, n - 1)
            self.high(act, k, e, 0)

    def high(self, act, k, e, m):
        act.wait_ge(self.hs_ready, k * 2 + m + 1)
        self.wait(act, self.down_ready, k - 1)
        act.copy(self.hs_high[:, e % 2, m], self.hs[:, m]).then_inc(self.hs_high_ready, 1)

    def low(self, engine, k, e, m):
        engine.wait_ge(self.hs_high_ready, k * 2 + m + 1)
        engine.tensor_tensor(self.hs_low[:, e % 2, m], self.hs[:, m], self.hs_high[:, e % 2, m].bitcast(F32),
                             ALU.subtract).then_inc(self.hs_low_ready[m], 1)

    def gpsimd(self, pool, n):
        for e in range(self.count):
            k = n * self.count + e
            for m in range(2):
                self.low(pool, k, e, m)

    def vector(self, dve, n, norm):
        earlier = not isinstance(n, int) or n > 0
        for e in range(self.count):
            k = n * self.count + e
            for m in range(2):
                dve.wait_ge(self.silu_ready, k * 2 + m + 1)
                dve.wait_ge(self.up_ready, k * 2 + m + 1)
                self.wait(dve, self.hs_ready, k * 2 + m - 1)
                if self.biased:
                    dve.scalar_tensor_tensor(self.h[:, m], self.up_ps[:, m], self.b_up[:, e, m:m + 1],
                                             self.a[:, m], ALU.add, ALU.mult).then_inc(self.h_ready, 1)
                else:
                    dve.tensor_tensor(self.h[:, m], self.up_ps[:, m], self.a[:, m], ALU.mult).then_inc(self.h_ready, 1)
                dve.wait_ge(self.h_ready, k * 2 + m + 1)
                dve.wait_ge(self.spread_ready, k + 1)
                self.wait(dve, self.hs_low_ready[m], k)
                dve.tensor_tensor(self.hs[:, m], self.h[:, m], self.share_ps[e % 2], ALU.mult).then_inc(self.hs_ready, 1)
            if earlier and e == 0:
                norm.add(dve, n - 1)
            if earlier and e == 1:
                norm.centre(dve, n - 1)
            if earlier and e == 4:
                norm.scale(dve, n - 1)

    def run(self, block, norm, before):

        def chunks(engine, body):
            body(0)
            with engine.Fori(0, CHUNKS - 1) as i:
                body(i + 1)

        @block.tensor
        def _(pe):
            before["tensor"](pe)
            pe.wait_ge(self.low_ready, len(self.loads()))
            pe.wait_ge(self.share_low, before["share_parts"])
            chunks(pe, lambda n: self.tensor(pe, n, norm))
            self.down(pe, CHUNKS - 1, CHUNKS * self.count - 1, self.count - 1)
            norm.tensor(pe, CHUNKS - 1)

        @block.scalar
        def _(act):
            before["scalar"](act)
            chunks(act, lambda n: self.scalar(act, n, norm))
            self.high(act, CHUNKS * self.count - 1, self.count - 1, 1)
            norm.scalar(act, CHUNKS - 1)

        @block.gpsimd
        def _(pool):
            before["gpsimd"](pool)
            self.split_low(pool)
            chunks(pool, lambda n: self.gpsimd(pool, n))

        @block.vector
        def _(dve):
            before["vector"](dve)
            chunks(dve, lambda n: self.vector(dve, n, norm))
            norm.vector(dve, CHUNKS - 1)


def expert_choice_stage(nc, g, tag, w):
    X, ones, eps = g["X"], g["ones"], g["eps"]
    NE, CAP = 8, N // 8
    SL = P // NE
    T = N // SL
    TOP_BIT = 30
    ROUNDS = TOP_BIT // 2
    with ExitStack() as ctx:
        def sb(name, shape, dt=F32):
            return ctx.enter_context(nc.sbuf_tensor(tag + name, shape, dt))

        def ps(name, shape=(P, W)):
            return ctx.enter_context(nc.psum_tensor(tag + name, list(shape), F32))

        def sem(name):
            return stage_semaphore(nc, g, tag + name)

        yt_ps, misc_ps = ps("yt_ps"), ps("misc_ps")
        ex = Experts(nc, sb, ps, sem, g, NE, False, yt_ps[:])
        w_router = sb("w_router", [P, NE])
        same = sb("same", [P, P])
        before = sb("before", [P, P])
        spread = sb("spread", [NE, P])
        rows = sb("rows", [NE, N])
        top = sb("top", [NE, 1])
        negtop = sb("negtop", [P, 1])
        s = sb("s", [P, T])
        y = sb("y", [P, T])
        one = sb("one", [P, T])
        hits = sb("hits", [P, T])
        count = sb("count", [P, 3])
        pos = sb("pos", [P, 1])
        sign = sb("sign", [P, 1])
        want = sb("want", [P, 1])
        found = sb("found", [P, 1], I32)
        more = sb("more", [P, 3], I32)
        lower_bit = sb("lower_bit", [P, 3])
        cand = sb("cand", [P, 3], I32)
        reached = sb("reached", [P, 3])
        added = sb("added", [P, 1])
        added_bits = sb("added_bits", [P, 1], I32)
        thr = sb("thr", [P, 1])
        above = sb("above", [P, T])
        equal = sb("equal", [P, T])
        rank = sb("rank", [P, T])
        room = sb("room", [P, 1])
        room2 = sb("room2", [P, 1])
        part = sb("part", [P, 1])
        inv = sb("inv", [P, 1])
        exps = sb("exps", [P, T])
        weight = sb("weight", [P, T])

        early, gathered, returned = sem("early"), sem("gathered"), sem("returned")
        score_ready, score_copied = sem("score_ready"), sem("score_copied")
        v_step = sem("v_step")
        p_step = sem("p_step")
        exp_ready = sem("exp_ready")
        bit_counted, bit_summed = sem("bit_counted"), sem("bit_summed")
        cand_ready, added_ready, bits_ready, found_ready, moved = (
            sem("cand_ready"), sem("added_ready"), sem("bits_ready"), sem("found_ready"), sem("moved"))
        norm = Norm(nc, sb, sem, X, ones, eps, misc_ps[:], misc_ps[:], ex.down_ready, ex.y_ps[:], per=NE)
        block = ctx.enter_context(nc.Block())

        @block.sync
        def _(sp):
            for dst, name in ((w_router, "router"), (same, "same"), (before, "before"), (spread, "spread")):
                sp.dma_start(dst[:], w[name]).then_inc(early, 16)
            sp.wait_ge(score_copied, CHUNKS)
            for e in range(NE):
                sp.dma_start(s[e * SL:(e + 1) * SL, :], rows[e:e + 1, :].rearrange("o (c t) -> o c t", t=T)).then_inc(gathered, 16)
            ex.load(sp, w)
            sp.wait_ge(v_step, 28)
            for e in range(NE):
                sp.dma_start(rows[e:e + 1, :].rearrange("o (c t) -> o c t", t=T), weight[e * SL:(e + 1) * SL, :]).then_inc(returned, 16)

        def route_tensor(pe):
            pe.wait_ge(early, 64)
            for n in range(CHUNKS):
                if n >= 2:
                    pe.wait_ge(score_copied, n - 1)
                bank = (yt_ps, misc_ps)[n % 2]
                pe.matmul(bank[0:NE, :], w_router[:], X[:, n * W:(n + 1) * W], start=True, stop=True).then_inc(score_ready, 1)
            pe.wait_ge(score_copied, CHUNKS)
            pe.wait_ge(v_step, 1)
            pe.matmul(misc_ps[:, 0:1], spread[:], top[:], start=True, stop=True).then_inc(p_step, 1)
            pe.wait_ge(v_step, 5)
            pe.matmul(misc_ps[:, 1:2], same[:], count[:, 0:1], start=True, stop=True).then_inc(p_step, 1)
            pe.wait_ge(bit_counted, 1)
            pe.matmul(yt_ps[:, 0:1], same[:], count[:, 0:1], start=True, stop=True).then_inc(bit_summed, 1)
            with pe.Fori(0, ROUNDS) as i:
                pe.wait_ge(bit_counted, i * 3 + 4)
                pe.matmul(yt_ps[:, 0:3], same[:], count[:], start=True, stop=True).then_inc(bit_summed, 1)
            pe.wait_ge(v_step, 18)
            pe.matmul(misc_ps[:, 2:3], same[:], count[:, 0:1], start=True, stop=True).then_inc(p_step, 1)
            pe.wait_ge(v_step, 21)
            pe.matmul(misc_ps[:, 3:4], before[:], rank[:, T - 1:T], start=True, stop=True).then_inc(p_step, 1)
            pe.wait_ge(v_step, 26)
            pe.matmul(misc_ps[:, 4:5], same[:], part[:], start=True, stop=True).then_inc(p_step, 1)

        def route_scalar(act):
            for n in range(CHUNKS):
                act.wait_ge(score_ready, n + 1)
                act.copy(rows[:, n * W:(n + 1) * W], (yt_ps, misc_ps)[n % 2][0:NE, :]).then_inc(score_copied, 1)
            ex.split_high(act)
            act.wait_ge(v_step, 2)
            act.wait_ge(gathered, 16 * NE)
            act.activation(exps[:], s[:], ACT.Exp, bias=negtop[:, 0:1]).then_inc(exp_ready, 1)

            act.wait_ge(returned, 16 * NE)
            act.wait_ge(ex.share_filled, 1)
            act.copy(ex.share[0:NE], rows[:]).then_inc(ex.share_high, 1)

        def route_vector(dve):
            done = [0]

            def step(instruction):
                done[0] += 1
                instruction.then_inc(v_step, 1)
                dve.wait_ge(v_step, done[0])

            dve.wait_ge(score_copied, CHUNKS)
            step(dve.tensor_reduce(top[:], rows[:], AX_X, ALU.max))
            dve.wait_ge(p_step, 1)
            step(dve.tensor_scalar(negtop[:], misc_ps[:, 0:1], -1.0, None, ALU.mult))
            step(dve.memset(one[:], 1.0))
            step(dve.memset(found[:], 0))
            dve.wait_ge(gathered, 16 * NE)
            step(dve.scalar_tensor_tensor(hits[:], s[:], 0.0, one[:], ALU.is_ge, ALU.mult, accum_out=count[:, 0:1]))
            dve.wait_ge(p_step, 2)
            step(dve.tensor_scalar(pos[:], misc_ps[:, 1:2], float(CAP), None, ALU.is_ge))
            step(dve.tensor_scalar(sign[:], pos[:], 2.0, -1.0, ALU.mult, ALU.add))
            step(dve.tensor_scalar(want[:], pos[:], float(2 * CAP - N - 1), float(N - CAP + 1), ALU.mult, ALU.add))
            step(dve.tensor_scalar(y[:], s[:], sign[:, 0:1], None, ALU.mult))
            for times in range(1, 4):
                step(dve.memset(more[:, times - 1:times], times << (TOP_BIT - 2)))
            step(dve.memset(cand[:, 0:1], 1 << TOP_BIT))
            step(dve.memset(lower_bit[:], float(1 << TOP_BIT)))

            def counts(n):
                for c in range(n):
                    dve.scalar_tensor_tensor((hits, above, equal)[c][:], y[:], cand[:, c:c + 1].bitcast(F32), one[:], ALU.is_ge, ALU.mult,
                                             accum_out=count[:, c:c + 1]).then_inc(bit_counted, 1)

            def take(n, done):
                dve.wait_ge(bit_summed, done + 1)
                dve.scalar_tensor_tensor(reached[:, 0:n], yt_ps[:, 0:n], want[:, 0:1], lower_bit[:, 0:n], ALU.is_ge,
                                         ALU.mult, accum_out=added[:]).then_inc(added_ready, 1)
                dve.wait_ge(added_ready, done + 1)
                dve.tensor_scalar(added_bits[:], added[:], 1.0, None, ALU.mult).then_inc(bits_ready, 1)
                dve.tensor_scalar(lower_bit[:], lower_bit[:], 0.25, None, ALU.mult).then_inc(moved, 1)
                dve.wait_ge(bits_ready, done + 1)
                dve.tensor_tensor(found[:], found[:], added_bits[:], ALU.bitwise_or).then_inc(found_ready, 1)

            counts(1)
            take(1, 0)
            with dve.Fori(0, ROUNDS) as i:
                dve.wait_ge(found_ready, i + 1)
                dve.wait_ge(moved, i * 2 + 1)
                dve.tensor_tensor(cand[:], found[:].to_broadcast([P, 3]), more[:], ALU.bitwise_or).then_inc(cand_ready, 1)
                dve.wait_ge(cand_ready, i + 1)
                dve.tensor_scalar(more[:], more[:], 2, None, ALU.logical_shift_right).then_inc(moved, 1)
                counts(3)
                take(3, i + 1)
            dve.wait_ge(found_ready, ROUNDS + 1)
            step(dve.tensor_scalar(thr[:], found[:].bitcast(F32), sign[:, 0:1], None, ALU.mult))
            step(dve.tensor_scalar(above[:], s[:], thr[:, 0:1], None, ALU.is_gt))
            step(dve.tensor_scalar(equal[:], s[:], thr[:, 0:1], None, ALU.is_equal))
            step(dve.tensor_reduce(count[:, 0:1], above[:], AX_X, ALU.add))
            dve.wait_ge(p_step, 3)
            step(dve.tensor_scalar(room[:], misc_ps[:, 2:3], -1.0, float(CAP), ALU.mult, ALU.add))
            step(dve.memset(hits[:], 0.0))
            step(dve.tensor_tensor_scan(rank[:], equal[:], hits[:], 0.0, ALU.add, ALU.add))
            dve.wait_ge(p_step, 4)
            step(dve.tensor_tensor(room2[:], room[:], misc_ps[:, 3:4], ALU.subtract))
            step(dve.scalar_tensor_tensor(hits[:], rank[:], room2[:, 0:1], equal[:], ALU.is_le, ALU.mult))
            step(dve.tensor_tensor(above[:], above[:], hits[:], ALU.add))
            dve.wait_ge(exp_ready, 1)
            step(dve.tensor_tensor(exps[:], exps[:], above[:], ALU.mult))
            step(dve.tensor_reduce(part[:], exps[:], AX_X, ALU.add))
            dve.wait_ge(p_step, 5)
            step(dve.reciprocal(inv[:], misc_ps[:, 4:5]))
            step(dve.tensor_scalar(weight[:], exps[:], inv[:, 0:1], None, ALU.mult))
            dve.wait_ge(ex.share_high, 1)
            dve.tensor_tensor(ex.share[32:32 + NE], rows[:], ex.share[0:NE].bitcast(F32), ALU.subtract).then_inc(ex.share_low, 1)

        ex.run(block, norm, {"tensor": route_tensor, "scalar": route_scalar, "vector": route_vector,
                             "gpsimd": lambda pool: None, "share_parts": 1})


def top2_experts_stage(nc, g, tag, w):
    X, ones, eps, ident = g["X"], g["ones"], g["eps"], g["ident"]
    NR, NS = 8, 2
    NE = NR + NS
    TT = N // P
    with ExitStack() as ctx:
        def sb(name, shape, dt=F32):
            return ctx.enter_context(nc.sbuf_tensor(tag + name, shape, dt))

        def ps(name, shape=(P, W)):
            return ctx.enter_context(nc.psum_tensor(tag + name, list(shape), F32))

        def sem(name):
            return stage_semaphore(nc, g, tag + name)

        yt_ps, misc_ps = ps("yt_ps"), ps("misc_ps")
        ex = Experts(nc, sb, ps, sem, g, NE, True, yt_ps[:])
        w_router = sb("w_router", [P, NR])
        b_router = sb("b_router", [NR, 1])
        lower = sb("lower", [P, NR, NR])
        rows = sb("rows", [P, N])
        gate_rows = rows[0:NR]
        gates = sb("gates", [P, TT, NR])
        top = sb("top", [P, TT])
        exps = sb("exps", [P, TT, NR])
        total = sb("total", [P, TT])
        inv = sb("inv", [P, TT])
        higher = sb("higher", [P, TT, NR, NR])
        ties = ex.products[:].rearrange("p a m (t e f) -> p (a m t) e f", e=NR, f=NR)
        rank = sb("rank", [P, TT, NR])
        share = ex.a[:].rearrange("p m w -> p (m w)")[:, 0:TT * NE].rearrange("p (t e) -> p t e", e=NE)

        early = sem("early")
        filled = sem("filled")
        logits_ready, logits_copied, logits_turned = sem("logits_ready"), sem("logits_copied"), sem("logits_turned")
        v_step = sem("v_step")
        exp_ready = sem("exp_ready")
        share_ready, share_turned = sem("share_ready"), sem("share_turned")
        stored = sem("stored")
        norm = Norm(nc, sb, sem, X, ones, eps, misc_ps[:], misc_ps[:], ex.down_ready, ex.y_ps[:], per=NE,
                    buffers=(rows[:, 0:W], rows[:, W:2 * W]))
        block = ctx.enter_context(nc.Block())

        @block.sync
        def _(sp):
            for dst, name in ((w_router, "router"), (b_router, "b_router"), (lower, "lower")):
                sp.dma_start(dst[:], w[name]).then_inc(early, 16)
            ex.load(sp, w)
            with sp.Fori(0, CHUNKS) as n:
                sp.wait_ge(norm.x_ready, n + 1)
                sp.dma_start(w["outT"][:, bass.ds(n * W, W)], X[:, bass.ds(n * W, W)]).then_inc(stored, 16)
            sp.wait_ge(stored, 16 * CHUNKS)

        def fill(pool):
            pool.memset(share, 1.0 / NS).then_inc(filled, 1)

        def route_tensor(pe):
            pe.wait_ge(early, 48)
            banks = (yt_ps, misc_ps)
            for n in range(CHUNKS):
                if n >= 2:
                    pe.wait_ge(logits_copied, n - 1)
                pe.matmul(banks[n % 2][0:NR, :], w_router[:], X[:, n * W:(n + 1) * W], start=True, stop=True).then_inc(logits_ready, 1)
            pe.wait_ge(logits_copied, CHUNKS)
            for t in range(TT):
                mm = pe.transpose(yt_ps[:, t * NR:(t + 1) * NR], gate_rows[:, t * P:(t + 1) * P], ident[0:NR, 0:NR])
            mm.then_inc(logits_turned, 1)
            pe.wait_ge(share_ready, 1)
            for n in range(CHUNKS):
                if n >= 2:
                    pe.wait_ge(ex.share_low, n - 1)
                for t in range(W // P):
                    mm = pe.transpose(banks[n % 2][0:NE, t * P:(t + 1) * P], share[:, n * (W // P) + t], ident[:])
                mm.then_inc(share_turned, 1)

        def route_scalar(act):
            act.wait_ge(early, 48)
            for n in range(CHUNKS):
                act.wait_ge(logits_ready, n + 1)
                act.activation(gate_rows[:, n * W:(n + 1) * W], (yt_ps, misc_ps)[n % 2][0:NR, :], ACT.Identity,
                               bias=b_router[:, 0:1]).then_inc(logits_copied, 1)
            act.wait_ge(v_step, 3)
            act.activation(exps[:], exps[:], ACT.Exp).then_inc(exp_ready, 1)
            ex.split_high(act)
            act.wait_ge(ex.share_filled, 1)
            for n in range(CHUNKS):
                act.wait_ge(share_turned, n + 1)
                act.copy(ex.share[0:NE, n * W:(n + 1) * W], (yt_ps, misc_ps)[n % 2][0:NE, :]).then_inc(ex.share_high, 1)

        def route_vector(dve):
            done = [0]

            def step(instruction):
                done[0] += 1
                instruction.then_inc(v_step, 1)
                dve.wait_ge(v_step, done[0])

            four = [P, TT, NR, NR]
            dve.wait_ge(early, 48)
            dve.wait_ge(filled, 1)
            dve.wait_ge(logits_turned, 1)
            step(dve.tensor_copy(gates[:], yt_ps[:, 0:TT * NR].rearrange("p (t e) -> p t e", e=NR)))
            step(dve.tensor_reduce(top[:], gates[:], AX_X, ALU.max))
            step(dve.tensor_tensor(exps[:], gates[:], top[:, :, None].to_broadcast([P, TT, NR]), ALU.subtract))
            mine, other = gates[:, :, :, None].to_broadcast(four), gates[:, :, None, :].to_broadcast(four)
            step(dve.tensor_tensor(ties, other, mine, ALU.is_equal))
            step(dve.tensor_tensor(ties, ties, lower[:, None, :, :].to_broadcast(four), ALU.mult))
            step(dve.tensor_tensor(higher[:], other, mine, ALU.is_gt))
            step(dve.tensor_tensor(higher[:], higher[:], ties, ALU.add))
            step(dve.tensor_reduce(rank[:], higher[:], AX_X, ALU.add))
            dve.wait_ge(exp_ready, 1)
            step(dve.tensor_reduce(total[:], exps[:], AX_X, ALU.add))
            step(dve.reciprocal(inv[:], total[:]))
            step(dve.tensor_tensor(exps[:], exps[:], inv[:, :, None].to_broadcast([P, TT, NR]), ALU.mult))
            dve.scalar_tensor_tensor(share[:, :, 0:NR], rank[:], 1.5, exps[:], ALU.is_lt, ALU.mult).then_inc(share_ready, 1)
            for n in range(CHUNKS):
                dve.wait_ge(ex.share_high, n + 1)
                dve.tensor_tensor(ex.share[32:32 + NE, n * W:(n + 1) * W], (yt_ps, misc_ps)[n % 2][0:NE, :],
                                  ex.share[0:NE, n * W:(n + 1) * W].bitcast(F32), ALU.subtract).then_inc(ex.share_low, 1)

        ex.run(block, norm, {"tensor": route_tensor, "scalar": route_scalar, "vector": route_vector,
                             "gpsimd": fill, "share_parts": CHUNKS})


def path_attention_stage(nc, g, tag, w):
    X, ones, eps, ident = g["X"], g["ones"], g["eps"], g["ident"]
    LOW, KT = 32, 3
    HG = H // 2
    GD = HG * DH
    STEP = 8
    GROW = 4
    QKVB = 3 * D + H
    ROW = 2 * D
    SOON = 16
    HALF = S * D // 2
    SCALE = DH ** -0.5
    PI = 3.141592653589793
    TWO_PI_HI = 6.28125
    TWO_PI_LO = 2 * PI - TWO_PI_HI
    with ExitStack() as ctx:
        def sb(name, shape, dt=F32):
            return ctx.enter_context(nc.sbuf_tensor(tag + name, shape, dt))

        def ps(name, shape=(P, W)):
            return ctx.enter_context(nc.psum_tensor(tag + name, list(shape), F32))

        def sem(name):
            return stage_semaphore(nc, g, tag + name)

        w_o = sb("w_o", [P, 2, D])
        angle = sb("angle", [P, 2])
        beta_bias = sb("beta_bias", [P, H])
        below = sb("below", [P, 2 * S])
        shut = sb("shut", [P, 2 * S])
        K = sb("K", [P, H, DH, S])
        QV = sb("QV", [P, S * ROW])
        Wd = sb("Wd", [P, S * D])
        A = sb("A", [P, 2, HG * DH * S])
        C = sb("C", [P, S * GD])
        trig = sb("trig", [P, 2, S])
        normed = sb("normed", [P, 2, W])
        p = sb("p", [P, 2, HG * S])
        top = sb("top", [P, 2, HG])
        total = sb("total", [P, 2, HG])
        inv = sb("inv", [P, 2, HG])
        o_sum = sb("o_sum", [P, 2, GD])
        O = sb("O", [P, D])
        OT = sb("OT", [P, P])

        A_flat, used = A[:].rearrange("p a n -> p (a n)"), [0]

        def scratch(rows, *shape):
            n = 1
            for x in shape:
                n *= x
            view = A_flat[0:rows, used[0]:used[0] + n]
            used[0] += n
            return view if len(shape) == 1 else view.rearrange("p (a b) -> p a b", b=shape[1])

        w_tok = scratch(P, 2, QKVB)
        w_low = scratch(P, KT * LOW)
        w_up = scratch(KT * LOW, 2, 2 * D)
        taps = scratch(KT * LOW, 2, 2 * D)
        pos = scratch(P, S)
        turns = scratch(P, S).bitcast(I32)
        th, th2, excess = scratch(P, S), scratch(P, S), scratch(P, S)
        xs, ls = scratch(P, 2, B), scratch(KT * LOW, 2, B)
        raw = scratch(P, 2, 2 * D)
        beta = scratch(P, S, H)
        low = C[0:KT * LOW, :].rearrange("p (b s) -> p b s", s=S)
        sumsq, z = C[:, 0:S * H], C[:, S * H:2 * S * H]

        u_ps, l_ps, o_ps = ps("u_ps", (P, 2, W)), ps("l_ps", (P, 2, W)), ps("o_ps", (P, 2, W))
        ot_ps, y_ps = ps("ot_ps"), ps("y_ps")

        weights, consts = sem("weights"), sem("consts")
        v_step, s_step = sem("v_step"), sem("s_step")
        low_ready, low_copied = sem("low_ready"), sem("low_copied")
        staged, tok_ready, w_ready, silu_ready, half_ready = (
            sem("staged"), sem("tok_ready"), sem("w_ready"), sem("silu_ready"), sem("half_ready"))
        scaled_later = sem("scaled_later")
        qv_stored, k_stored, w_stored = sem("qv_stored"), sem("k_stored"), sem("w_stored")
        wk_ready, u_ready, masked, move_ready, k_ready, qk_ready, l_ready = (
            sem("wk_ready"), sem("u_ready"), sem("masked"), sem("move_ready"), sem("k_ready"), sem("qk_ready"), sem("l_ready"))
        shut_ready, top_ready, shifted, exp_ready, total_ready, inv_ready = (
            sem("shut_ready"), sem("top_ready"), sem("shifted"), sem("exp_ready"), sem("total_ready"), sem("inv_ready"))
        pv_ready, o_ready, o_summed, o_scaled, ot_ready, ot_copied, y_ready = (
            sem("pv_ready"), sem("o_ready"), sem("o_summed"), sem("o_scaled"), sem("ot_ready"), sem("ot_copied"), sem("y_ready"))
        norm = Norm(nc, sb, sem, X, ones, eps, ot_ps[:], ot_ps[:], y_ready, None, per=STEP,
                    buffers=(normed[:, 0], normed[:, 1]))
        block = ctx.enter_context(nc.Block())

        def steps(engine, body):
            for t in range(0, S, GROW):
                J, peeled = t + GROW, 1
                body(t, J, t, (t - 2) % STEP, None)
                if t % STEP == 0:
                    body(t + 1, J, J, (t - 1) % STEP, t // STEP - 1 if t else None)
                    peeled = 2
                with engine.Fori(0, GROW - peeled) as i:
                    body(i + t + peeled, J, J, i + (t + peeled - 2) % STEP, None)

        def pairs(engine, count, body):
            body(0)
            with engine.Fori(0, count // 2 - 2) as i:
                body(i * 2 + 2)
            body(count - 2)

        LOADS = 10
        Xbt = X[:].rearrange("p (b t) -> p b t", t=S)

        def heads(buf, gi, J):
            return buf[:, gi, 0:HG * DH * J].rearrange("p (h d j) -> p h d j", h=HG, d=DH)

        def keys(gi, J):
            return K[:, gi * HG:(gi + 1) * HG, :, 0:J]

        def row(buf, at, J):
            return buf[:, bass.ds(at, GD)].rearrange("p (h d) -> p h d", d=DH)[:, :, :, None].to_broadcast([P, HG, DH, J])

        def scaled(engine, start, end):
            w_part = Wd[:, start * D:end * D].rearrange("p (n d) -> p n d", d=DH)
            return engine.tensor_tensor(w_part, w_part, sumsq[:, start * H:end * H, None].to_broadcast([P, (end - start) * H, DH]), ALU.mult)

        @block.sync
        def _(sp):
            for dst, name in ((w_tok, "tok"), (w_low, "low"), (w_up, "up"), (taps, "taps"), (w_o, "o"), (angle, "angle"),
                              (beta_bias, "beta_bias"), (pos, "pos"), (below, "below"), (shut, "shut")):
                sp.dma_start(dst[:], w[name]).then_inc(weights, 16)

        @block.gpsimd
        def _(pool):
            pool.memset(low[0:2 * LOW, :, 0:2], 0.0).then_inc(consts, 1)

            def weigh(t, J):
                for gi in range(2):
                    k = t * 2 + gi
                    pool.wait_ge(exp_ready, k + 1)
                    if not isinstance(t, int) or k:
                        pool.wait_ge(o_ready, k)
                    v = QV[:].rearrange("p (j c) -> p j c", c=ROW)[:, 0:J, D + gi * GD:D + (gi + 1) * GD]
                    pool.tensor_tensor(C[:, 0:J * GD].rearrange("p (j h d) -> p j h d", h=HG, d=DH),
                                       v.rearrange("p j (h d) -> p j h d", d=DH),
                                       p[:, gi, 0:HG * J].rearrange("p (h j) -> p j h", j=J)[:, :, :, None].to_broadcast([P, J, HG, DH]),
                                       ALU.mult).then_inc(pv_ready, 1)

            pool.wait_ge(s_step, 6)
            scaled(pool, SOON, S).then_inc(scaled_later, 1)
            pool.wait_ge(scaled_later, 1)
            pool.wait_ge(v_step, 22)
            weigh(0, GROW)
            for t in range(0, S, GROW):
                peeled = 0 if t else 1
                with pool.Fori(0, GROW - peeled) as i:
                    weigh(i + t + peeled, t + GROW)

        @block.tensor
        def _(pe):
            pe.wait_ge(weights, 16 * LOADS)

            def project_low(n):
                for u in range(2):
                    if not isinstance(n, int) or n:
                        pe.wait_ge(low_copied, (n + u - 1) * KT)
                    pe.matmul(o_ps[0:KT * LOW, u], w_low, X[:, bass.ds((n + u) * W, W)], start=True, stop=True).then_inc(low_ready, 1)

            def project_tokens(t):
                for u in range(2):
                    pe.wait_ge(staged, (t + u) * 2 + 2)
                    if not isinstance(t, int) or t:
                        pe.wait_ge(qv_stored, t + u - 1)
                        pe.wait_ge(k_stored, t + u - 1)
                    for r in range(2):
                        pe.matmul(o_ps[r * B:(r + 1) * B, u, 0:ROW], xs[:, u], w_tok[:, r, 0:ROW], start=True, stop=True)
                    for r in range(2):
                        mm = pe.matmul(u_ps[r * B:(r + 1) * B, u, 0:QKVB - ROW], xs[:, u], w_tok[:, r, ROW:QKVB],
                                       start=True, stop=True)
                    mm.then_inc(tok_ready, 1)
                    if not isinstance(t, int) or t:
                        pe.wait_ge(silu_ready, t + u - 1)
                    for r in range(2):
                        mm = pe.matmul(l_ps[r * B:(r + 1) * B, u, 0:2 * D], ls[:, u], w_up[:, r], start=True, stop=True)
                    mm.then_inc(w_ready, 1)

            pairs(pe, CHUNKS, project_low)
            pe.wait_ge(v_step, 1)
            pe.wait_ge(low_copied, CHUNKS * KT)
            pairs(pe, S, project_tokens)

            def dots(ready, bank, done, gi, k, J):
                pe.wait_ge(ready, k + 1)
                for d in range(DH):
                    mm = pe.matmul(bank[:, gi, 0:HG * J], ident[:], heads(A, gi, J)[:, :, d, :], start=(d == 0), stop=(d == DH - 1))
                mm.then_inc(done, 1)

            def outputs(t, gi, J):
                pe.wait_ge(pv_ready, t * 2 + gi + 1)
                if gi == 0 and (not isinstance(t, int) or t):
                    pe.wait_ge(o_summed, t * 2)
                for j in range(J // 4):
                    mm = pe.matmul(o_ps[:, gi, 0:4 * GD], ident[:], C[:, j * 4 * GD:(j + 1) * 4 * GD], start=(j == 0), stop=(j == J // 4 - 1))
                mm.then_inc(o_ready, 1)

            def turn(t):
                pe.wait_ge(o_scaled, t + 1)
                pe.transpose(ot_ps[:, 0:P], O[:], ident[:]).then_inc(ot_ready, 1)

            def project(t, slot):
                pe.wait_ge(ot_copied, t + 1)
                for r in range(2):
                    mm = pe.matmul(y_ps[:, bass.ds(slot * B, B)], w_o[:, r], OT[:, r * B:(r + 1) * B], start=(r == 0), stop=(r == 1))
                mm.then_inc(y_ready, 1)

            def body(t, J, before, slot, closed):
                for gi in range(2):
                    dots(wk_ready, u_ps, u_ready, gi, t * 2 + gi, J)
                    if gi == 0 and (not isinstance(t, int) or t >= 2):
                        project(t - 2, slot)
                for gi in range(2):
                    if before:
                        outputs(t - 1, gi, before)
                    if closed is not None and gi == 0:
                        norm.mean(pe, closed)
                    dots(qk_ready, l_ps, l_ready, gi, t * 2 + gi, J)
                    if closed is not None and gi == 0:
                        norm.variance(pe, closed)
                if closed is not None:
                    pe.wait_ge(norm.logvar_ready, closed + 1)
                if before:
                    turn(t - 1)

            steps(pe, body)
            project(S - 2, STEP - 2)
            for gi in range(2):
                outputs(S - 1, gi, S)
            turn(S - 1)
            project(S - 1, STEP - 1)
            norm.tensor(pe, S // STEP - 1)

        @block.scalar
        def _(act):
            act.wait_ge(v_step, 15)
            for a in range(2):
                act.activation(trig[:, a], (th2, th)[a], ACT.Sin).then_inc(s_step, 1)

            def activate(t):
                for u in range(2):
                    act.wait_ge(w_ready, t + u + 1)
                    if not isinstance(t, int) or t:
                        act.wait_ge(w_stored, t + u - 1)
                    act.activation(raw[:, u], l_ps[:, u, 0:2 * D], ACT.Silu).then_inc(silu_ready, 1)
                    act.copy(QV[:, bass.ds(t * ROW + u * ROW, ROW)], o_ps[:, u, 0:ROW]).then_inc(qv_stored, 1)

            pairs(act, S, activate)
            act.wait_ge(w_stored, S)
            act.wait_ge(v_step, 16)
            for a in range(2):
                act.activation(A[:, a], Wd[:, a * HALF:(a + 1) * HALF], ACT.Square).then_inc(s_step, 1)
            act.activation(z, z, ACT.Exp, scale=-1.0).then_inc(s_step, 1)
            act.wait_ge(v_step, 21)
            act.activation(sumsq, sumsq, ACT.Sqrt, scale=2.0).then_inc(s_step, 1)
            load_ln_exp(nc, act)

            def exponentials(t, gi, J):
                act.wait_ge(shifted, t * 2 + gi + 1)
                act.activation(p[:, gi, 0:HG * J], p[:, gi, 0:HG * J], ACT.Exp, scale=SCALE).then_inc(exp_ready, 1)

            def copy_turned(t):
                act.wait_ge(ot_ready, t + 1)
                act.copy(OT[:], ot_ps[:, 0:P]).then_inc(ot_copied, 1)

            def body(t, J, before, slot, closed):
                if not before:
                    return
                exponentials(t - 1, 0, before)
                exponentials(t - 1, 1, before)
                if closed is not None:
                    norm.square(act, closed)
                    norm.root(act, closed)
                copy_turned(t - 1)

            steps(act, body)
            for gi in range(2):
                exponentials(S - 1, gi, S)
            copy_turned(S - 1)
            norm.scalar(act, S // STEP - 1, load=False)

        @block.vector
        def _(dve):
            done = [0]

            def step(instruction):
                done[0] += 1
                instruction.then_inc(v_step, 1)
                dve.wait_ge(v_step, done[0])

            def wrap():
                step(dve.tensor_scalar(excess, th2, PI, -2 * PI, ALU.is_gt, ALU.mult))
                step(dve.tensor_tensor(th2, th2, excess, ALU.add))
                step(dve.tensor_scalar(excess, th2, -PI, 2 * PI, ALU.is_lt, ALU.mult))
                step(dve.tensor_tensor(th2, th2, excess, ALU.add))

            dve.wait_ge(weights, 16 * LOADS)
            step(dve.tensor_tensor(w_up, w_up, taps, ALU.mult))
            step(dve.tensor_scalar(th, pos, angle[:, 0:1], angle[:, 1:2], ALU.mult, ALU.add))
            step(dve.tensor_scalar(turns, th, 1 / (2 * PI), None, ALU.mult))
            step(dve.scalar_tensor_tensor(th, turns, -TWO_PI_HI, th, ALU.mult, ALU.add))
            step(dve.scalar_tensor_tensor(th2, turns, -TWO_PI_LO, th, ALU.mult, ALU.add))
            wrap()
            step(dve.tensor_scalar(th, th2, PI, -PI, ALU.min, ALU.max))
            step(dve.tensor_scalar(th2, th, PI / 2, None, ALU.add))
            wrap()
            dve.wait_ge(consts, 1)

            def copy_low(n):
                for u in range(2):
                    dve.wait_ge(low_ready, n + u + 1)
                    for k in range(KT):
                        lag = KT - 1 - k
                        rows = slice(k * LOW, (k + 1) * LOW)
                        dve.tensor_scalar(low[rows, bass.ds((n + u) * BC, BC), lag:S],
                                          o_ps[rows, u].rearrange("p (b s) -> p b s", s=S)[:, :, 0:S - lag],
                                          1.0, None, ALU.mult).then_inc(low_copied, 1)

            def stage(t, u):
                dve.tensor_scalar(xs[:, u, :], Xbt[:, :, bass.ds(t + u, 1)].rearrange("p b o -> p (b o)"), 1.0, None, ALU.mult).then_inc(staged, 1)
                dve.tensor_scalar(ls[:, u, :], low[:, :, bass.ds(t + u, 1)].rearrange("p b o -> p (b o)"), 1.0, None, ALU.mult).then_inc(staged, 1)

            def rotate(t, u):
                dve.wait_ge(silu_ready, t + 1)
                dve.tensor_scalar(Wd[:, bass.ds(t * D, D)], raw[:, u, 0:D], trig[:, 0, bass.ds(t, 1)], None, ALU.mult).then_inc(half_ready, 1)
                dve.wait_ge(half_ready, t + 1)
                dve.scalar_tensor_tensor(Wd[:, bass.ds(t * D, D)], raw[:, u, D:2 * D], trig[:, 1, bass.ds(t, 1)],
                                         Wd[:, bass.ds(t * D, D)], ALU.mult, ALU.add).then_inc(w_stored, 1)

            def store(t):
                for u in range(2):
                    dve.wait_ge(tok_ready, t + u + 1)
                    dve.wait_ge(w_ready, t + u + 1)
                    if not isinstance(t, int) or t < S - 2:
                        stage(t + 2, u)
                    dve.tensor_scalar(beta[:, bass.ds(t + u, 1), :], u_ps[:, u, None, 0:H], 1.0, None, ALU.mult)
                    dve.tensor_scalar(K[:].rearrange("p h d j -> p (h d) j")[:, :, bass.ds(t + u, 1)],
                                      u_ps[:, u, H:QKVB - ROW][:, :, None], 1.0, None, ALU.mult).then_inc(k_stored, 1)
                    if not isinstance(t, int) or t + u:
                        rotate(t + u - 1, 1 - u)

            pairs(dve, CHUNKS, copy_low)
            dve.wait_ge(low_copied, KT * CHUNKS)
            dve.wait_ge(s_step, 2)
            stage(0, 0)
            stage(0, 1)
            pairs(dve, S, store)
            rotate(S - 1, 1)
            dve.wait_ge(w_stored, S)
            dve.wait_ge(k_stored, S)
            step(dve.tensor_tensor(z.rearrange("p (t h) -> p t h", h=H), beta,
                                   beta_bias[:, None, :].to_broadcast([P, S, H]), ALU.add))
            for a in range(2):
                dve.wait_ge(s_step, 3 + a)
                step(dve.tensor_reduce(sumsq[:, a * (S * H // 2):(a + 1) * (S * H // 2)],
                                       A[:, a].rearrange("p (n d) -> p n d", d=DH), AX_X, ALU.add))
            dve.wait_ge(s_step, 5)
            step(dve.tensor_scalar(z, z, 1.0, None, ALU.add))
            step(dve.scalar_tensor_tensor(sumsq, sumsq, 1e-6, z, ALU.add, ALU.mult))
            step(dve.reciprocal(sumsq, sumsq))
            dve.wait_ge(s_step, 6)
            step(scaled(dve, 0, SOON))

            def soften(t, gi, J, to_end):
                k = t * 2 + gi
                s = p[:, gi, 0:HG * J].rearrange("p (h j) -> p h j", j=J)
                if isinstance(t, int):
                    dve.wait_ge(l_ready, k + 1)
                l = l_ps[:, gi, 0:HG * J].rearrange("p (h j) -> p h j", j=J)
                dve.tensor_tensor(l[:, :, J - GROW:J], l[:, :, J - GROW:J],
                                  shut[:, None, bass.ds(to_end + (J - GROW - 1), GROW)].to_broadcast([P, HG, GROW]), ALU.add).then_inc(shut_ready, 1)
                dve.wait_ge(shut_ready, k + 1)
                dve.tensor_reduce(top[:, gi], l, AX_X, ALU.max).then_inc(top_ready, 1)
                dve.wait_ge(top_ready, k + 1)
                dve.tensor_tensor(s, l, top[:, gi, :, None].to_broadcast([P, HG, J]), ALU.subtract).then_inc(shifted, 1)

            def product(t, gi, J):
                k = t * 2 + gi
                if not isinstance(t, int) or t:
                    dve.wait_ge(l_ready, k - 1)
                dve.tensor_tensor(heads(A, gi, J), keys(gi, J), row(Wd, t * D + gi * GD, J), ALU.mult).then_inc(wk_ready, 1)

            def update(t, gi, J, to_end):
                k = t * 2 + gi
                dve.wait_ge(u_ready, k + 1)
                dots = u_ps[:, gi, 0:HG * J].rearrange("p (h j) -> p h j", j=J)
                dve.tensor_tensor(dots[:, :, J - GROW:J], dots[:, :, J - GROW:J],
                                  below[:, None, bass.ds(to_end + (J - GROW), GROW)].to_broadcast([P, HG, GROW]), ALU.mult).then_inc(masked, 1)
                dve.wait_ge(masked, k + 1)
                dve.tensor_tensor(heads(A, gi, J), dots[:, :, None, :].to_broadcast([P, HG, DH, J]), row(Wd, t * D + gi * GD, J), ALU.mult).then_inc(move_ready, 1)
                dve.wait_ge(move_ready, k + 1)
                dve.tensor_tensor(keys(gi, J), keys(gi, J), heads(A, gi, J), ALU.subtract).then_inc(k_ready, 1)
                dve.wait_ge(k_ready, k + 1)
                dve.tensor_tensor(heads(A, gi, J), keys(gi, J), row(QV, t * ROW + gi * GD, J), ALU.mult).then_inc(qk_ready, 1)

            def finish(t, J):
                dve.wait_ge(exp_ready, t * 2 + 2)
                for gi in range(2):
                    dve.tensor_reduce(total[:, gi], p[:, gi, 0:HG * J].rearrange("p (h j) -> p h j", j=J), AX_X, ALU.add).then_inc(total_ready, 1)
                dve.wait_ge(total_ready, t * 2 + 2)
                dve.reciprocal(inv[:], total[:]).then_inc(inv_ready, 1)
                for gi in range(2):
                    dve.wait_ge(o_ready, t * 2 + gi + 1)
                    dve.tensor_reduce(o_sum[:, gi], o_ps[:, gi, 0:4 * GD].rearrange("p (j n) -> p n j", j=4), AX_X, ALU.add).then_inc(o_summed, 1)
                dve.wait_ge(inv_ready, t + 1)
                dve.wait_ge(o_summed, t * 2 + 2)
                if not isinstance(t, int) or t:
                    dve.wait_ge(ot_ready, t)
                dve.tensor_tensor(O[:].rearrange("p (h d) -> p h d", d=DH), o_sum[:].rearrange("p a (h d) -> p (a h) d", d=DH),
                                  inv[:].rearrange("p a h -> p (a h)")[:, :, None].to_broadcast([P, H, DH]), ALU.mult).then_inc(o_scaled, 1)

            def body(t, J, before, slot, closed):
                if isinstance(t, int) and t == SOON:
                    dve.wait_ge(scaled_later, 1)
                to_end = S - t if isinstance(t, int) else dve.snap(S - t)
                product(t, 0, J)
                if before:
                    soften(t - 1, 0, before, to_end + 1)
                product(t, 1, J)
                if before:
                    soften(t - 1, 1, before, to_end + 1)
                if closed is not None:
                    norm.add(dve, closed, x=positions(closed), y=projected)
                update(t, 0, J, to_end)
                if closed is not None:
                    norm.centre(dve, closed)
                update(t, 1, J, to_end)
                if closed is not None:
                    norm.scale(dve, closed, positions(closed))
                if before:
                    finish(t - 1, before)

            def positions(c):
                return Xbt[:, :, c * STEP:(c + 1) * STEP]

            projected = y_ps[:].rearrange("p (t b) -> p b t", b=B)
            steps(dve, body)
            for gi in range(2):
                soften(S - 1, gi, S, 1)
            finish(S - 1, S)
            norm.vector(dve, S // STEP - 1, x=positions(S // STEP - 1), y=projected)


def build(nc, t):
    with ExitStack() as ctx:
        def sb(name, shape, dt=F32):
            return ctx.enter_context(nc.sbuf_tensor(name, shape, dt))

        g = {"sems": [], "X": sb("X", [P, N]), "ones": sb("ones", [P, P]), "eps": sb("eps", [P, 1]), "ident": sb("ident", [P, P])}
        loaded = ctx.enter_context(nc.semaphore("first_loaded"))
        filled = ctx.enter_context(nc.semaphore("consts_filled"))
        with nc.Block() as block:
            @block.sync
            def _(sp):
                sp.dma_start(g["X"][:, 0:W], t["xT"][:, 0:W]).then_inc(loaded, 16)
                sp.dma_start(g["ident"][:], t["ident"]).then_inc(loaded, 16)
                sp.wait_ge(loaded, 32)

            @block.gpsimd
            def _(pool):
                pool.memset(g["ones"][:], 1.0 / D).then_inc(filled, 1)
                pool.memset(g["eps"][:], EPS).then_inc(filled, 1)
                pool.wait_ge(filled, 2)

        def of(stage):
            tag = f"s{stage}_"
            return {k[3:]: v for k, v in t.items() if k.startswith(tag)} | {k: t[k] for k in ("xT", "ctxT", "mask", "outT")}

        conv_mlp_stage(nc, g, "s1_", of(1))
        end_stage(nc, g)
        attention_stage(nc, g, "s2_", of(2), masked=False)
        end_stage(nc, g)
        expert_choice_stage(nc, g, "s3_", of(3))
        end_stage(nc, g)
        path_attention_stage(nc, g, "s4_", of(4))
        end_stage(nc, g)
        attention_stage(nc, g, "s5_", of(5), masked=True)
        end_stage(nc, g)
        top2_experts_stage(nc, g, "s6_", of(6))


def kernel(**inputs):
    import numpy as np
    import concourse.bacc as bacc
    from concourse.bass_utils import run_bass_kernel_spmd

    a = {k: np.asarray(v) for k, v in inputs.items()}
    f32 = np.float32

    def columns(v):
        return v.reshape(-1, P).T

    def halves(m):
        return m.reshape(2, P, -1).transpose(1, 0, 2)

    def down(m):
        return m.reshape(-1, 2, P, D).transpose(2, 0, 1, 3).reshape(P, -1)

    def direction(m):
        return m.reshape(-1, H, 2, 2, DH).transpose(0, 2, 3, 1, 4).reshape(-1, 2, 2 * D)

    def per_r(m):
        return np.repeat(m, B, 0)

    def rows_twice(m):
        out = np.zeros((64,) + m.shape[1:], f32)
        out[:len(m)] = out[32:32 + len(m)] = m
        return out

    def pick(count):
        return rows_twice(np.repeat(np.eye(count, dtype=f32), P, 1))

    conv = a["L0_attn_conv_w"]
    conv_bd = np.zeros((P, 2, TAPS, P), f32)
    for o in range(INNER):
        m, r = divmod(o, P)
        conv_bd[r // 32 * 32:r // 32 * 32 + 32, m, :, r] = conv[o]
    lay = {
        "xT": a["x"].reshape(N, D).T,
        "ident": np.eye(P, dtype=f32),
        "s1_in": a["L0_attn_in_proj_w"].T,
        "s1_conv": conv_bd,
        "s1_cols": np.concatenate([columns(a["L0_attn_" + k]) for k in ("conv_b", "ln_g", "ln_b", "cproj_b", "fc_b")], 1),
        "s1_fc": halves(a["L0_attn_fc_w"].T),
        "s1_cproj": a["L0_attn_cproj_w"].T,
        "s1_out": halves(a["L0_attn_out_w"].T),
        "ctxT": a["ctx_1024"].reshape(N, D).T,
        "mask": a["mask_1x1xSxS2_ik0"].reshape(S, S),
        "s3_router": a["L0_ffn_Wg"].T,
        "s3_same": np.kron(np.eye(8), np.ones((16, 16))).astype(f32),
        "s3_before": np.kron(np.eye(8), np.triu(np.ones((16, 16)), 1)).astype(f32),
        "s3_spread": np.kron(np.eye(8), np.ones((1, 16))).astype(f32),
        "s3_pick": pick(8),
        "s3_gate": a["L0_ffn_W1"].transpose(2, 0, 1).reshape(P, -1),
        "s3_up": a["L0_ffn_W3"].transpose(2, 0, 1).reshape(P, -1),
        "s3_down": down(a["L0_ffn_W2"].transpose(0, 2, 1)),
        "s4_tok": np.stack([np.concatenate([a["L1_attn_q_w"].T, a["L1_attn_v_w"].T, a["L1_attn_bt_w"][r::2].T,
                                            a["L1_attn_k_w"].T], 1) for r in range(2)], 1),
        "s4_low": np.tile(a["L1_attn_w1"].T, (1, 3)),
        "s4_up": np.tile(direction(a["L1_attn_w2"].T), (3, 1, 1)),
        "s4_taps": np.repeat(direction(a["L1_attn_conv_w"].T), 32, 0),
        "s4_o": a["L1_attn_o_w"].T.reshape(H, 2, DH, D).transpose(0, 2, 1, 3).reshape(P, 2, D),
        "s4_angle": per_r(np.stack([a["L1_attn_omega"].reshape(2), a["L1_attn_phi"].reshape(2)], 1)),
        "s4_beta_bias": per_r(a["L1_attn_bt_b"].reshape(H, 2).T),
        "s4_pos": np.broadcast_to(np.arange(S, dtype=f32), (P, S)),
        "s4_below": np.broadcast_to((np.arange(2 * S) < S).astype(f32), (P, 2 * S)),
        "s4_shut": np.broadcast_to(np.where(np.arange(2 * S) < S, 0, -1e30).astype(f32), (P, 2 * S)),
        "s6_router": a["L1_ffn_gate_w"],
        "s6_b_router": a["L1_ffn_gate_b"][:, None],
        "s6_lower": np.broadcast_to(np.tril(np.ones((8, 8), f32), -1), (P, 8, 8)),
        "s6_pick": pick(10),
        "s6_gate": np.concatenate([a["L1_ffn_rw1"], a["L1_ffn_sw1"]]).transpose(1, 0, 2).reshape(P, -1),
        "s6_up": np.concatenate([a["L1_ffn_rw2"], a["L1_ffn_sw2"]]).transpose(1, 0, 2).reshape(P, -1),
        "s6_down": down(np.concatenate([a["L1_ffn_rw3"], a["L1_ffn_sw3"]])),
        "s6_b_gate": np.concatenate([a["L1_ffn_rb1"], a["L1_ffn_sb1"]]).reshape(-1, 2, P).transpose(2, 0, 1),
        "s6_b_up": np.concatenate([a["L1_ffn_rb2"], a["L1_ffn_sb2"]]).reshape(-1, 2, P).transpose(2, 0, 1),
        "s6_b_down": rows_twice(np.concatenate([a["L1_ffn_rb3"], a["L1_ffn_sb3"]])),
        "s2_qkvo": np.stack([a["L0_xattn_w" + c] for c in "qkvo"], 1),
        "s2_bias": np.stack([a["L0_xattn_b" + c] for c in "qkvo"], 1),
        "s5_qkvo": np.stack([a["L1_xattn_W" + c].T for c in "qkvo"], 1),
        "s5_bias": np.stack([a["L1_xattn_b" + c] for c in "qkvo"], 1),
    }
    nc = bacc.Bacc("TRN2", target_bir_lowering=False, num_devices=1)
    arrays = {k: np.ascontiguousarray(v) for k, v in lay.items()}
    t = {k: nc.dram_tensor("in_" + k, v.shape, mybir.dt.from_np(v.dtype), kind="ExternalInput").ap() for k, v in arrays.items()}
    t["outT"] = nc.dram_tensor("outT", (D, N), F32, kind="ExternalOutput").ap()
    build(nc, t)
    r = run_bass_kernel_spmd(nc, [{"in_" + k: v for k, v in arrays.items()}], core_ids=[0])
    return np.ascontiguousarray(r.results[0]["outT"].T).reshape(B, S, D)
```
